# Optimizing a Trainium2 kernel written in Bass

```python
import numpy as np
import jax
import jax.numpy as jnp

def _softmax(x, axis=-1):
    return jax.nn.softmax(x, axis=axis)

def _gelu(x):
    return jax.nn.gelu(x, approximate=True)

def _silu(x):
    return jax.nn.silu(x)

def _sigmoid(x):
    return jax.nn.sigmoid(x)

def _layernorm(x, axis=-1, eps=1e-05):
    m = jnp.mean(x, axis=axis, keepdims=True)
    v = jnp.var(x, axis=axis, keepdims=True)
    return (x - m) / jnp.sqrt(v + eps)

def _scatter_add(tgt, idx, src, axis=0):
    return tgt.at[idx].add(src)

def _segment_sum(src, seg, n):
    return jax.ops.segment_sum(src, seg, n)
kernel_name = 'mk_adaln_attn_ffn_d1_seqx_r4_15200c'

def setup_inputs(seed: int=0):
    np.random.seed(seed)
    _w = jnp.asarray

    def _rec_inputs():
        import jax
        import jax.numpy as jnp
        _rk = jax.random.key(seed)
        x = -1.394e-06 + 0.9999 * jax.random.normal(jax.random.fold_in(_rk, 1), (4, 512, 512), jnp.float32)
        _lenS = 512 - jax.random.randint(jax.random.fold_in(_rk, 7), (4,), 0, max(1, 512 // 4) + 1, jnp.int32)
        _lenS2 = 512 - jax.random.randint(jax.random.fold_in(_rk, 8), (4,), 0, max(1, 512 // 4) + 1, jnp.int32)
        cond_2048 = -0.00499425 + 1.0058 * jax.random.normal(jax.random.fold_in(_rk, 11), (4, 512), jnp.float32)
        return (x, cond_2048)
    x, cond_2048 = _rec_inputs()

    def _L0_cond_setup():
        import jax, jax.numpy as jnp
        import numpy as np
        B, T, D = (16, 128, 512)
        key = jax.random.key(seed)
        k0, k1, k2, k3 = jax.random.split(key, 4)
        scale = 1.0 / np.sqrt(D)
        return {'initial_state': jax.random.normal(k0, (B, D), jnp.float32), 'inputs': jax.random.normal(k1, (B, T, D), jnp.float32), 'W_ih': jax.random.normal(k2, (D, 3 * D), jnp.float32) * scale, 'W_hh': jax.random.normal(k3, (D, 3 * D), jnp.float32) * scale, 'b_ih': jnp.zeros((3 * D,), jnp.float32), 'b_hh': jnp.zeros((3 * D,), jnp.float32)}
    _L0_cond_all = _L0_cond_setup()
    _L0_cond_in = {k: v for k, v in _L0_cond_all.items() if k in ('W_ih', 'W_hh', 'b_ih', 'b_hh')}
    del _L0_cond_all

    def _L0_attn_setup():
        import math
        import jax, jax.numpy as jnp
        import numpy as np
        B, T, E, H = (1, 512, 512, 16)
        D = E // H // 2
        DEPTH = 12
        LAMBDA_INIT = 0.8 - 0.6 * math.exp(-0.3 * DEPTH)
        EPS = 1e-05
        NEG = -1e+30

        def rotary_cos_sin(seqlen, dim):
            inv_freq = 1.0 / 10000.0 ** (jnp.arange(0, dim, 2, dtype=jnp.float32) / dim)
            t = jnp.arange(seqlen, dtype=jnp.float32)
            freqs = jnp.outer(t, inv_freq)
            return (jnp.cos(freqs), jnp.sin(freqs))

        def apply_rotary_interleaved(x, cos, sin):
            x1 = x[..., 0::2]
            x2 = x[..., 1::2]
            c = cos[None, :, None, :]
            s = sin[None, :, None, :]
            o1 = x1 * c - x2 * s
            o2 = x1 * s + x2 * c
            return jnp.stack([o1, o2], axis=-1).reshape(x.shape)

        def causal_attn_pair(q, k, v1, v2, mask, scale):
            s = jnp.einsum('bthd,bshd->bhts', q, k) * scale
            s = jnp.where(mask, s, NEG)
            a = jax.nn.softmax(s, axis=-1)
            o1 = jnp.einsum('bhts,bshd->bthd', a, v1)
            o2 = jnp.einsum('bhts,bshd->bthd', a, v2)
            return jnp.concatenate([o1, o2], axis=-1)
        key = jax.random.key(seed)
        ks = jax.random.split(key, 10)
        return {'query': jax.random.normal(ks[0], (B, T, E), dtype=jnp.float32), 'Wq': jax.random.normal(ks[1], (E, E), dtype=jnp.float32) * 0.02, 'Wk': jax.random.normal(ks[2], (E, E), dtype=jnp.float32) * 0.02, 'Wv': jax.random.normal(ks[3], (E, E), dtype=jnp.float32) * 0.02, 'Wout': jax.random.normal(ks[4], (E, E), dtype=jnp.float32) * 0.02, 'lambda_q1': jax.random.normal(ks[5], (D,), dtype=jnp.float32) * 0.1, 'lambda_k1': jax.random.normal(ks[6], (D,), dtype=jnp.float32) * 0.1, 'lambda_q2': jax.random.normal(ks[7], (D,), dtype=jnp.float32) * 0.1, 'lambda_k2': jax.random.normal(ks[8], (D,), dtype=jnp.float32) * 0.1, 'rms_weight': jnp.ones((2 * D,), dtype=jnp.float32)}
    _L0_attn_all = _L0_attn_setup()
    _L0_attn_in = {k: v for k, v in _L0_attn_all.items() if k in ('Wq', 'Wk', 'Wv', 'Wout', 'lambda_q1', 'lambda_k1', 'lambda_q2', 'lambda_k2', 'rms_weight')}
    del _L0_attn_all

    def _L0_cond2_setup():
        import jax, jax.numpy as jnp
        import numpy as np
        HEADS = 16
        EPS = 1e-06

        def _rms_norm(x, g):
            xf = x.astype(jnp.float32)
            y = xf * jax.lax.rsqrt(jnp.mean(xf * xf, axis=-1, keepdims=True) + EPS)
            return y.astype(x.dtype) * g
        key = jax.random.key(seed)
        ks = jax.random.split(key, 6)
        b, n, dim, emb_dim = (4, 512, 512, 512)
        d_head = dim // HEADS
        return {'x': jax.random.normal(ks[0], (b, n, dim), jnp.float32), 'emb': jax.random.normal(ks[1], (b, 1, emb_dim), jnp.float32), 'W_emb': jax.random.normal(ks[2], (emb_dim, 2 * dim), jnp.float32) * emb_dim ** (-0.5), 'b_emb': jnp.zeros((2 * dim,), jnp.float32), 'g_norm': jnp.ones((dim,), jnp.float32), 'W_qkv': jax.random.normal(ks[3], (dim, 3 * dim), jnp.float32) * dim ** (-0.5), 'g_q': jnp.ones((d_head,), jnp.float32), 'g_k': jnp.ones((d_head,), jnp.float32), 'W_out': jax.random.normal(ks[4], (dim, dim), jnp.float32) * dim ** (-0.5)}
    _L0_cond2_all = _L0_cond2_setup()
    _L0_cond2_in = {k: v for k, v in _L0_cond2_all.items() if k in ('W_emb', 'b_emb', 'g_norm', 'W_qkv', 'g_q', 'g_k', 'W_out')}
    del _L0_cond2_all

    def _L0_ffn_setup():
        import jax, jax.numpy as jnp
        import numpy as np
        E = 64
        K = 6
        CAP = 128
        SCALE = 1.0
        H = 512
        I = 192
        SI = I * 2
        B, S = (2, 256)

        def _moe(x, gate_w, gate_up_proj, down_proj, shared_gate_w, shared_up_w, shared_down_w):
            b, s, h = x.shape
            T = b * s
            xf = x.reshape(T, h)
            scores = jax.nn.softmax(xf @ gate_w.T, axis=-1)
            topk_w, topk_idx = jax.lax.top_k(scores, K)
            topk_w = topk_w * SCALE
            flat_e = topk_idx.reshape(-1)
            order = jnp.argsort(flat_e)
            sorted_e = flat_e[order]
            sorted_tok = (order // K).astype(jnp.int32)
            sorted_w = topk_w.reshape(-1)[order]
            counts = jnp.zeros((E,), jnp.int32).at[flat_e].add(1)
            offsets = jnp.cumsum(counts) - counts
            pos = jnp.arange(T * K, dtype=jnp.int32) - offsets[sorted_e]
            buf_tok = jnp.full((E, CAP), T, jnp.int32).at[sorted_e, pos].set(sorted_tok, mode='drop')
            buf_w = jnp.zeros((E, CAP), x.dtype).at[sorted_e, pos].set(sorted_w, mode='drop')
            xp = jnp.concatenate([xf, jnp.zeros((1, h), x.dtype)], axis=0)
            gx = xp[buf_tok]
            gu = jnp.einsum('ech,ehi->eci', gx, gate_up_proj)
            g, u = jnp.split(gu, 2, axis=-1)
            hid = jax.nn.silu(g) * u
            eo = jnp.einsum('eci,eih->ech', hid, down_proj) * buf_w[..., None]
            routed = jnp.zeros((T + 1, h), x.dtype).at[buf_tok.reshape(-1)].add(eo.reshape(-1, h))[:T]
            shared = jax.nn.silu(xf @ shared_gate_w.T) * (xf @ shared_up_w.T) @ shared_down_w.T
            return (routed + shared).reshape(b, s, h)
        key = jax.random.key(seed)
        ks = jax.random.split(key, 7)
        x = jax.random.normal(ks[0], (B, S, H), jnp.float32)
        gate_w = jax.random.normal(ks[1], (E, H), jnp.float32) * 0.02
        gate_up_proj = jax.random.normal(ks[2], (E, H, 2 * I), jnp.float32) * 0.02
        down_proj = jax.random.normal(ks[3], (E, I, H), jnp.float32) * 0.02
        shared_gate_w = jax.random.normal(ks[4], (SI, H), jnp.float32) * 0.02
        shared_up_w = jax.random.normal(ks[5], (SI, H), jnp.float32) * 0.02
        shared_down_w = jax.random.normal(ks[6], (H, SI), jnp.float32) * 0.02
        return dict(x=x, gate_w=gate_w, gate_up_proj=gate_up_proj, down_proj=down_proj, shared_gate_w=shared_gate_w, shared_up_w=shared_up_w, shared_down_w=shared_down_w)
    _L0_ffn_all = _L0_ffn_setup()
    _L0_ffn_in = {k: v for k, v in _L0_ffn_all.items() if k in ('gate_w', 'gate_up_proj', 'down_proj', 'shared_gate_w', 'shared_up_w', 'shared_down_w')}
    del _L0_ffn_all
    return {'x': x, 'cond_2048': cond_2048, 'L0_cond_W_ih': _L0_cond_in['W_ih'], 'L0_cond_W_hh': _L0_cond_in['W_hh'], 'L0_cond_b_ih': _L0_cond_in['b_ih'], 'L0_cond_b_hh': _L0_cond_in['b_hh'], 'L0_attn_Wq': _L0_attn_in['Wq'], 'L0_attn_Wk': _L0_attn_in['Wk'], 'L0_attn_Wv': _L0_attn_in['Wv'], 'L0_attn_Wout': _L0_attn_in['Wout'], 'L0_attn_lambda_q1': _L0_attn_in['lambda_q1'], 'L0_attn_lambda_k1': _L0_attn_in['lambda_k1'], 'L0_attn_lambda_q2': _L0_attn_in['lambda_q2'], 'L0_attn_lambda_k2': _L0_attn_in['lambda_k2'], 'L0_attn_rms_weight': _L0_attn_in['rms_weight'], 'L0_cond2_W_emb': _L0_cond2_in['W_emb'], 'L0_cond2_b_emb': _L0_cond2_in['b_emb'], 'L0_cond2_g_norm': _L0_cond2_in['g_norm'], 'L0_cond2_W_qkv': _L0_cond2_in['W_qkv'], 'L0_cond2_g_q': _L0_cond2_in['g_q'], 'L0_cond2_g_k': _L0_cond2_in['g_k'], 'L0_cond2_W_out': _L0_cond2_in['W_out'], 'L0_ffn_gate_w': _L0_ffn_in['gate_w'], 'L0_ffn_gate_up_proj': _L0_ffn_in['gate_up_proj'], 'L0_ffn_down_proj': _L0_ffn_in['down_proj'], 'L0_ffn_shared_gate_w': _L0_ffn_in['shared_gate_w'], 'L0_ffn_shared_up_w': _L0_ffn_in['shared_up_w'], 'L0_ffn_shared_down_w': _L0_ffn_in['shared_down_w']}

def reference(x, cond_2048, L0_cond_W_ih, L0_cond_W_hh, L0_cond_b_ih, L0_cond_b_hh, L0_attn_Wq, L0_attn_Wk, L0_attn_Wv, L0_attn_Wout, L0_attn_lambda_q1, L0_attn_lambda_k1, L0_attn_lambda_q2, L0_attn_lambda_k2, L0_attn_rms_weight, L0_cond2_W_emb, L0_cond2_b_emb, L0_cond2_g_norm, L0_cond2_W_qkv, L0_cond2_g_q, L0_cond2_g_k, L0_cond2_W_out, L0_ffn_gate_w, L0_ffn_gate_up_proj, L0_ffn_down_proj, L0_ffn_shared_gate_w, L0_ffn_shared_up_w, L0_ffn_shared_down_w):
    import jax
    import jax.numpy as jnp

    def _L0_cond_ref(initial_state, inputs, W_ih, W_hh, b_ih, b_hh):
        import jax, jax.numpy as jnp
        import numpy as np
        B, T, D = (16, 128, 512)
        "ScanOverTime(GRU cell): sequential per-timestep module call with\n            dict-state passing; merge_dict_trees stacks the per-step\n            'state_predicted' tensors along axis=1 -> [B, T, D]."

        def cell(h, x):
            gi = x @ W_ih + b_ih
            gh = h @ W_hh + b_hh
            i_r, i_z, i_n = jnp.split(gi, 3, axis=-1)
            h_r, h_z, h_n = jnp.split(gh, 3, axis=-1)
            r = jax.nn.sigmoid(i_r + h_r)
            z = jax.nn.sigmoid(i_z + h_z)
            n = jnp.tanh(i_n + r * h_n)
            h_new = (1.0 - z) * n + z * h
            return (h_new, h_new)
        xs = jnp.swapaxes(inputs, 0, 1)
        _, hs = jax.lax.scan(cell, initial_state, xs)
        return jnp.swapaxes(hs, 0, 1)

    def _L0_attn_ref(query, Wq, Wk, Wv, Wout, lambda_q1, lambda_k1, lambda_q2, lambda_k2, rms_weight):
        import math
        import jax, jax.numpy as jnp
        import numpy as np
        B, T, E, H = (1, 512, 512, 16)
        D = E // H // 2
        DEPTH = 12
        LAMBDA_INIT = 0.8 - 0.6 * math.exp(-0.3 * DEPTH)
        EPS = 1e-05
        NEG = -1e+30

        def rotary_cos_sin(seqlen, dim):
            inv_freq = 1.0 / 10000.0 ** (jnp.arange(0, dim, 2, dtype=jnp.float32) / dim)
            t = jnp.arange(seqlen, dtype=jnp.float32)
            freqs = jnp.outer(t, inv_freq)
            return (jnp.cos(freqs), jnp.sin(freqs))

        def apply_rotary_interleaved(x, cos, sin):
            x1 = x[..., 0::2]
            x2 = x[..., 1::2]
            c = cos[None, :, None, :]
            s = sin[None, :, None, :]
            o1 = x1 * c - x2 * s
            o2 = x1 * s + x2 * c
            return jnp.stack([o1, o2], axis=-1).reshape(x.shape)

        def causal_attn_pair(q, k, v1, v2, mask, scale):
            s = jnp.einsum('bthd,bshd->bhts', q, k) * scale
            s = jnp.where(mask, s, NEG)
            a = jax.nn.softmax(s, axis=-1)
            o1 = jnp.einsum('bhts,bshd->bthd', a, v1)
            o2 = jnp.einsum('bhts,bshd->bthd', a, v2)
            return jnp.concatenate([o1, o2], axis=-1)
        bsz, tgt_len, embed_dim = query.shape
        cos, sin = rotary_cos_sin(tgt_len, D)
        scale = D ** (-0.5)
        mask = jnp.tril(jnp.ones((tgt_len, tgt_len), dtype=bool))[None, None]
        q = (query @ Wq).reshape(bsz, tgt_len, 2 * H, D)
        k = (query @ Wk).reshape(bsz, tgt_len, 2 * H, D)
        v = (query @ Wv).reshape(bsz, tgt_len, H, 2, D)
        q = apply_rotary_emb = apply_rotary_interleaved(q, cos, sin)
        k = apply_rotary_interleaved(k, cos, sin)
        q = q.reshape(bsz, tgt_len, H, 2, D)
        k = k.reshape(bsz, tgt_len, H, 2, D)
        q1, q2 = (q[:, :, :, 0], q[:, :, :, 1])
        k1, k2 = (k[:, :, :, 0], k[:, :, :, 1])
        v1, v2 = (v[:, :, :, 0], v[:, :, :, 1])
        attn1 = causal_attn_pair(q1, k1, v1, v2, mask, scale)
        attn2 = causal_attn_pair(q2, k2, v1, v2, mask, scale)
        lambda_1 = jnp.exp(jnp.sum(lambda_q1 * lambda_k1))
        lambda_2 = jnp.exp(jnp.sum(lambda_q2 * lambda_k2))
        lambda_full = lambda_1 - lambda_2 + LAMBDA_INIT
        f1 = jnp.fft.rfft(attn1, axis=1)
        f2 = jnp.fft.rfft(attn2, axis=1)
        attn_freq = f1 - lambda_full * f2
        n_freq = attn_freq.shape[1]
        sigma = 0.3 / 2.0
        x = jnp.linspace(0.0, 1.0, n_freq)
        filt = jnp.exp(-0.5 * (x / sigma) ** 2)
        attn_freq = attn_freq * filt[None, :, None, None]
        attn = jnp.fft.irfft(attn_freq, n=tgt_len, axis=1)
        attn = attn * jax.lax.rsqrt(jnp.mean(attn * attn, axis=-1, keepdims=True) + EPS) * rms_weight
        attn = attn * (1.0 - LAMBDA_INIT)
        attn = attn.reshape(bsz, tgt_len, H * 2 * D)
        return attn @ Wout

    def _L0_cond2_ref(x, emb, W_emb, b_emb, g_norm, W_qkv, g_q, g_k, W_out):
        import jax, jax.numpy as jnp
        import numpy as np
        HEADS = 16
        EPS = 1e-06

        def _rms_norm(x, g):
            xf = x.astype(jnp.float32)
            y = xf * jax.lax.rsqrt(jnp.mean(xf * xf, axis=-1, keepdims=True) + EPS)
            return y.astype(x.dtype) * g
        b, n, dim = x.shape
        h = HEADS
        d = dim // h
        scale_shift = emb @ W_emb + b_emb
        scale, shift = jnp.split(scale_shift, 2, axis=-1)
        xn = _rms_norm(x, g_norm) * (1.0 + scale) + shift
        qkv = xn @ W_qkv
        qkv = qkv.reshape(b, n, 3, h, d)
        q, k, v = jnp.moveaxis(qkv, 2, 0)
        q = jnp.swapaxes(q, 1, 2)
        k = jnp.swapaxes(k, 1, 2)
        v = jnp.swapaxes(v, 1, 2)
        q = _rms_norm(q, g_q)
        k = _rms_norm(k, g_k)
        logits = jnp.einsum('bhqd,bhkd->bhqk', q, k) * d ** (-0.5)
        attn = jax.nn.softmax(logits, axis=-1)
        o = jnp.einsum('bhqk,bhkd->bhqd', attn, v)
        o = jnp.swapaxes(o, 1, 2).reshape(b, n, dim)
        return o + o @ W_out

    def _L0_ffn_ref(x, gate_w, gate_up_proj, down_proj, shared_gate_w, shared_up_w, shared_down_w):
        import jax, jax.numpy as jnp
        import numpy as np
        E = 64
        K = 6
        CAP = 128
        SCALE = 1.0
        H = 512
        I = 192
        SI = I * 2
        B, S = (2, 256)

        def _moe(x, gate_w, gate_up_proj, down_proj, shared_gate_w, shared_up_w, shared_down_w):
            b, s, h = x.shape
            T = b * s
            xf = x.reshape(T, h)
            scores = jax.nn.softmax(xf @ gate_w.T, axis=-1)
            topk_w, topk_idx = jax.lax.top_k(scores, K)
            topk_w = topk_w * SCALE
            flat_e = topk_idx.reshape(-1)
            order = jnp.argsort(flat_e)
            sorted_e = flat_e[order]
            sorted_tok = (order // K).astype(jnp.int32)
            sorted_w = topk_w.reshape(-1)[order]
            counts = jnp.zeros((E,), jnp.int32).at[flat_e].add(1)
            offsets = jnp.cumsum(counts) - counts
            pos = jnp.arange(T * K, dtype=jnp.int32) - offsets[sorted_e]
            buf_tok = jnp.full((E, CAP), T, jnp.int32).at[sorted_e, pos].set(sorted_tok, mode='drop')
            buf_w = jnp.zeros((E, CAP), x.dtype).at[sorted_e, pos].set(sorted_w, mode='drop')
            xp = jnp.concatenate([xf, jnp.zeros((1, h), x.dtype)], axis=0)
            gx = xp[buf_tok]
            gu = jnp.einsum('ech,ehi->eci', gx, gate_up_proj)
            g, u = jnp.split(gu, 2, axis=-1)
            hid = jax.nn.silu(g) * u
            eo = jnp.einsum('eci,eih->ech', hid, down_proj) * buf_w[..., None]
            routed = jnp.zeros((T + 1, h), x.dtype).at[buf_tok.reshape(-1)].add(eo.reshape(-1, h))[:T]
            shared = jax.nn.silu(xf @ shared_gate_w.T) * (xf @ shared_up_w.T) @ shared_down_w.T
            return (routed + shared).reshape(b, s, h)
        return _moe(x, gate_w, gate_up_proj, down_proj, shared_gate_w, shared_up_w, shared_down_w)
    x = x + _L0_attn_ref(_L0_cond_ref(cond_2048, x, L0_cond_W_ih, L0_cond_W_hh, L0_cond_b_ih, L0_cond_b_hh), L0_attn_Wq, L0_attn_Wk, L0_attn_Wv, L0_attn_Wout, L0_attn_lambda_q1, L0_attn_lambda_k1, L0_attn_lambda_q2, L0_attn_lambda_k2, L0_attn_rms_weight)
    x = x + _L0_ffn_ref(_L0_cond2_ref(x, cond_2048[:, None, :], L0_cond2_W_emb, L0_cond2_b_emb, L0_cond2_g_norm, L0_cond2_W_qkv, L0_cond2_g_q, L0_cond2_g_k, L0_cond2_W_out), L0_ffn_gate_w, L0_ffn_gate_up_proj, L0_ffn_down_proj, L0_ffn_shared_gate_w, L0_ffn_shared_up_w, L0_ffn_shared_down_w)
    return x

_drawn_inputs = setup_inputs


def setup_inputs(seed=0):
    import zlib

    import numpy as np

    out = dict(_drawn_inputs(seed))
    spreads = {'L0_cond_b_ih': (0.0, 0.1),
     'L0_cond_b_hh': (0.0, 0.1),
     'L0_attn_rms_weight': (1.0, 0.6),
     'L0_cond2_b_emb': (0.0, 0.487),
     'L0_cond2_g_norm': (1.0, 0.6),
     'L0_cond2_g_q': (1.0, 0.6),
     'L0_cond2_g_k': (1.0, 0.6)}
    factors = {'L0_attn_Wq': 8.0,
     'L0_attn_Wk': 8.0,
     'L0_attn_lambda_q1': 8.0,
     'L0_attn_lambda_k1': 3.194,
     'L0_attn_lambda_q2': 8.0,
     'L0_attn_lambda_k2': 8.0,
     'L0_ffn_gate_w': 8.0,
     'L0_ffn_gate_up_proj': 8.0,
     'L0_ffn_down_proj': 8.0,
     'L0_ffn_shared_gate_w': 8.0,
     'L0_ffn_shared_up_w': 8.0,
     'L0_ffn_shared_down_w': 8.0}
    for name, (base, spread) in spreads.items():
        noise = np.random.default_rng([zlib.crc32(name.encode()), seed]).standard_normal(out[name].shape)
        drawn = base * np.exp(spread * noise) if base else spread * noise
        out[name] = jnp.asarray(drawn.astype(out[name].dtype))
    for name, factor in factors.items():
        out[name] = (out[name] * factor).astype(out[name].dtype)
    return out
```

```python
import math
from contextlib import ExitStack

import numpy as np
import concourse.bass as bass
from concourse import mybir

F32 = mybir.dt.float32
BF16 = mybir.dt.bfloat16
U32 = mybir.dt.uint32
I32 = mybir.dt.int32
ALU = mybir.AluOpType
ACT = mybir.ActivationFunctionType
AX = mybir.AxisListType.X

P = 128
B, T, D = 4, 512, 512
KD = D // P
TT = T // P
NTILE = B * TT
H = 16
DH = D // H
G3 = 3 * D
GC = G3 // P
ST = KD * B
HG = P // DH
DQ = DH // 2
LAMBDA_INIT = 0.8 - 0.6 * math.exp(-0.3 * 12)
E, K, CAP = 64, 6, 128
SLOTS = E * CAP
I = 192
SI = 2 * I


class Sems:

    def __init__(self, nc, prefix):
        self.nc, self.prefix, self.held = nc, prefix, []

    def __call__(self, name):
        self.held.append(self.nc.alloc_semaphore(name=self.prefix + name))
        return self.held[-1]

    def __enter__(self):
        return self

    def __exit__(self, *failed):
        if not failed[0]:
            self.nc.clear_and_free_semaphores(self.held)
            self.nc.all_engine_barrier()


def gate_inputs_stage(nc, t, x, W_ih, b_ih, b_hh):
    with ExitStack() as ctx:
        sem = ctx.enter_context(Sems(nc, "gi_"))
        wih = ctx.enter_context(nc.sbuf_tensor("wih", [P, KD, G3], F32))
        wraw = ctx.enter_context(nc.sbuf_tensor("wraw", [P, 2, G3], F32))
        xin = ctx.enter_context(nc.sbuf_tensor("gi_xin", [P, TT, D], F32))
        xT = ctx.enter_context(nc.sbuf_tensor("gi_xT", [P, KD, T], F32))
        bias = ctx.enter_context(nc.sbuf_tensor("gi_bias", [P, 2, GC], F32))
        pt = ctx.enter_context(nc.psum_tensor("gi_pt", [P, 2, T], F32))
        pg = ctx.enter_context(nc.psum_tensor("gi_pg", [P, 4, T], F32))
        x_in, w_in, b_in = sem("x_in"), [sem("w_in0"), sem("w_in1")], sem("b_in")
        xT_psum, xT_ready = sem("xT_psum"), sem("xT_ready")
        w_spread, bias_sum, bias_ready = sem("w_spread"), sem("bias_sum"), sem("bias_ready")
        gi_psum, gi_even, gi_odd = sem("gi_psum"), sem("gi_even"), sem("gi_odd")
        block = ctx.enter_context(nc.Block())

        @block.sync
        def _(sp):
            sp.dma_start(t.ident[:], t.const["ident"]).then_inc(b_in, 16)
            for n, bvec in enumerate((b_ih, b_hh)):
                for j in range(KD):
                    for g in range(3):
                        sp.dma_start(bias[32 * j:32 * j + 32, n, g * KD:(g + 1) * KD],
                                     bvec.rearrange("(g j c i) -> g j i c", g=3, j=KD, c=KD)[g, j],
                                     allow_slow_non_contiguous=True).then_inc(b_in, 16)
            sp.dma_start(xin[:], x[0, :, :].rearrange("(tt p) d -> p tt d", p=P)).then_inc(x_in, 16)
            with sp.Fori(1, B) as b:
                sp.wait_ge(xT_psum, b * KD)
                sp.dma_start(xin[:], x[bass.ds(b, 1), :, :].rearrange("o (tt p) d -> p (o tt) d", p=P)).then_inc(x_in, 16)

        @block.gpsimd
        def _(pool):
            for k in range(KD):
                if k >= 2:
                    pool.wait_ge(w_spread, 3 * (k - 1))
                pool.dma_start(wraw[:, k % 2, :], W_ih[k * P:(k + 1) * P, :]).then_inc(w_in[k % 2], 16)

        @block.tensor
        def _(pe):
            pe.wait_ge(b_in, 16 * (1 + 6 * KD))
            with pe.Fori(0, B) as b:
                pe.wait_ge(x_in, b * 16 + 16)
                for k in range(KD):
                    if k >= 2:
                        pe.wait_ge(xT_ready, b * KD + (k - 1))
                    for tt in range(TT):
                        last = nc.tensor.transpose(pt[:, k % 2, tt * P:(tt + 1) * P], xin[:, tt, k * P:(k + 1) * P], t.ident[:])
                    last.then_inc(xT_psum, 1)
                pe.wait_ge(w_spread, 3 * KD)
                pe.wait_ge(xT_ready, b * KD + KD)
                for c in range(GC):
                    if c >= 4:
                        pe.wait_ge(gi_even if c % 2 == 0 else gi_odd, b * (GC // 2) + (c - 4) // 2 + 1)
                    for k in range(KD):
                        last = nc.tensor.matmul(pg[:, c % 4, :], wih[:, k, c * P:(c + 1) * P], xT[:, k, :],
                                                start=(k == 0), stop=(k == KD - 1))
                    last.then_inc(gi_psum, 1)
                pe.wait_ge(gi_even, b * (GC // 2) + GC // 2)
                pe.wait_ge(gi_odd, b * (GC // 2) + GC // 2)

        def evict(eng, b, c, out_sem):
            eng.wait_ge(gi_psum, b * GC + c + 1)
            dst = t.giT[:, :, bass.ds(b + c * B, 1)].rearrange("p t o -> p (t o)")
            if c % 2 == 0:
                nc.scalar.activation(dst, pg[:, c % 4, :], ACT.Identity, bias=bias[:, 0, c:c + 1]).then_inc(out_sem, 1)
            else:
                nc.vector.tensor_scalar(dst, pg[:, c % 4, :], bias[:, 0, c:c + 1], None, ALU.add).then_inc(out_sem, 1)

        @block.scalar
        def _(act):
            act.wait_ge(bias_ready, 1)
            with act.Fori(0, B) as b:
                for c in range(0, GC, 2):
                    evict(act, b, c, gi_even)

        @block.vector
        def _(dve):
            dve.wait_ge(b_in, 16 * (1 + 6 * KD))
            nc.vector.tensor_copy(t.bhn[:].rearrange("p (c b) -> p c b", b=B),
                                  bias[:, 1, 2 * KD:3 * KD].unsqueeze(2).broadcast_to([P, KD, B])).then_inc(bias_sum, 1)
            nc.vector.tensor_tensor(bias[:, 0, 0:2 * KD], bias[:, 0, 0:2 * KD], bias[:, 1, 0:2 * KD], ALU.add).then_inc(bias_ready, 1)
            for k in range(KD):
                dve.wait_ge(w_in[k % 2], 16 * (k // 2 + 1))
                for g in range(3):
                    nc.vector.tensor_copy(wih[:, k, g * D:(g + 1) * D].rearrange("p (c j i) -> p c j i", c=KD, j=KD),
                                          wraw[:, k % 2, g * D:(g + 1) * D].rearrange("p (j c i) -> p c j i", c=KD, j=KD)
                                          ).then_inc(w_spread, 1)
            dve.wait_ge(bias_ready, 1)
            with dve.Fori(0, B) as b:
                for k in range(KD):
                    dve.wait_ge(xT_psum, b * KD + k + 1)
                    nc.vector.tensor_copy(xT[:, k, :], pt[:, k % 2, :]).then_inc(xT_ready, 1)
                for c in range(1, GC, 2):
                    evict(dve, b, c, gi_odd)


def gru_stage(nc, t, h0, W_hh):
    with ExitStack() as ctx:
        sem = ctx.enter_context(Sems(nc, "gru_"))

        def sb(name, shape):
            return ctx.enter_context(nc.sbuf_tensor("gru_" + name, shape, F32))

        whh = sb("whh", [P, KD, KD, 3, P])
        trz, tn = sb("trz", [P, 2 * KD, 32]), sb("tn", [P, KD, 32])
        pre, rz = sb("pre", [P, 2 * ST]), sb("rz", [P, 2 * ST])
        rb, u, rn, npre = sb("rb", [P, ST]), sb("u", [P, ST]), sb("rn", [P, ST]), sb("npre", [P, ST])
        d0, d1 = sb("d0", [P, ST, 2]), sb("d1", [P, ST, 2])
        hin, zeros = sb("hin", [P, KD, B]), sb("zeros", [P, 1, D])
        zero_set, cleared = sem("zero_set"), sem("cleared")
        prz = ctx.enter_context(nc.psum_tensor("gru_prz", [P, 4 * P], F32))
        pn = ctx.enter_context(nc.psum_tensor("gru_pn", [P, 4 * P], F32))
        loaded, h_ready, hs_kept = sem("loaded"), sem("h_ready"), sem("hs_kept")
        rz_rows, n_rows = sem("rz_rows"), sem("n_rows")
        trz_done, pre_done, rz_act = sem("trz_done"), sem("pre_done"), sem("rz_act")
        tn_done, rb_done, u_done, side = sem("tn_done"), sem("rb_done"), sem("u_done"), sem("side")
        rn_done, npre_done, tanh_done = sem("rn_done"), sem("npre_done"), sem("tanh_done")
        block = ctx.enter_context(nc.Block())
        state = t.h[:, :, 1]

        def cb(ap):
            return ap.rearrange("p (c b) -> p c b", b=B)

        @block.sync
        def _(sp):
            for jj in range(KD):
                rows = W_hh.rearrange("(jj c i) n -> jj i c n", jj=KD, c=KD)[jj]
                for g in range(3):
                    for c in range(KD):
                        sp.dma_start(whh[32 * jj:32 * jj + 32, c, :, g, :],
                                     rows[:, c, g * D:(g + 1) * D].rearrange("i (j f) -> i j f", j=KD)).then_inc(loaded, 16)
                for c in range(KD):
                    sp.dma_start(hin[32 * jj:32 * jj + 32, c, :],
                                 h0[:, jj * P + 32 * c:jj * P + 32 * c + 32].rearrange("b i -> i b"),
                                 allow_slow_non_contiguous=True).then_inc(loaded, 16)

        LOADS = 16 * KD * (3 * KD + KD)

        @block.gpsimd
        def _(pool):
            nc.gpsimd.memset(zeros[:], 0.0).then_inc(zero_set, 1)
            pool.wait_ge(zero_set, 1)
            R = 16
            xg = t.xg_dram.rearrange("(n r p) d -> n p r d", r=R, p=P)
            for n in range(SLOTS // (R * P)):
                pool.dma_start(xg[n], zeros[:].broadcast_to([P, R, D])).then_inc(cleared, 16)
            pool.dma_start(t.eo_dram[SLOTS:SLOTS + 1, :], zeros[0:1, 0, :]).then_inc(cleared, 16)
            pool.wait_ge(cleared, 16 * (SLOTS // (R * P) + 1))

        @block.tensor
        def _(pe):
            pe.wait_ge(loaded, LOADS)
            with pe.Fori(0, T) as s:
                pe.wait_ge(h_ready, s * 1 + 1)
                for rows, g0, g1, done in ((prz, 0, 2, rz_rows), (pn, 2, 3, n_rows)):
                    for c in range(KD):
                        for j in range(KD):
                            last = nc.tensor.matmul(rows[32 * j:32 * j + 2 * B, 0:(g1 - g0) * P],
                                                    t.h[:, c * B:(c + 1) * B, :].rearrange("p b o -> p (b o)"),
                                                    whh[:, c, j, g0:g1, :].rearrange("p g f -> p (g f)"),
                                                    start=(c == 0), stop=(c == KD - 1))
                    last.then_inc(done, 1)

        @block.scalar
        def _(act):
            nc.scalar.preload_act_table_set("sigmoid_and_others")
            with act.Fori(0, T) as s:
                act.wait_ge(pre_done, s * 1 + 1)
                nc.scalar.activation(rz[:], pre[:], ACT.Sigmoid).then_inc(rz_act, 1)
                act.wait_ge(npre_done, s * 1 + 1)
                nc.scalar.activation(d1[:, :, 0], npre[:], ACT.Tanh).then_inc(tanh_done, 1)

        @block.vector
        def _(dve):
            nc.vector.memset(prz[:], 0.0)
            nc.vector.memset(pn[:], 0.0)
            nc.vector.memset(t.h[:], 0.0).then_inc(side, 1)
            nc.vector.memset(d0[:], 0.0).then_inc(side, 1)
            dve.wait_ge(side, 2)
            dve.wait_ge(loaded, LOADS)
            nc.vector.tensor_copy(state, hin[:].rearrange("p c b -> p (c b)")).then_inc(h_ready, 1)
            with dve.Fori(0, T) as s:
                gi = t.giT[:, bass.ds(s, 1), :].rearrange("p o c -> p (o c)")
                dve.wait_ge(rz_rows, s * 1 + 1)
                nc.vector.transpose(trz[:].rearrange("p c x -> p (c x)"), prz[:, 0:2 * P]).then_inc(trz_done, 1)
                dve.wait_ge(trz_done, s * 1 + 1)
                nc.vector.tensor_tensor(cb(pre[:]), trz[:, :, 1:2 * B:2], cb(gi[:, 0:2 * ST]), ALU.add).then_inc(pre_done, 1)
                dve.wait_ge(rz_act, s * 1 + 1)
                nc.vector.tensor_tensor(rb[:], rz[:, 0:ST], t.bhn[:], ALU.mult).then_inc(rb_done, 1)
                nc.vector.tensor_scalar(d0[:, :, 1], rz[:, ST:2 * ST], -1.0, 1.0, ALU.mult, ALU.add).then_inc(side, 1)
                nc.vector.tensor_tensor(d1[:, :, 1], rz[:, ST:2 * ST], state, ALU.mult).then_inc(side, 1)
                dve.wait_ge(rb_done, s * 1 + 1)
                nc.vector.tensor_tensor(u[:], rb[:], gi[:, 2 * ST:3 * ST], ALU.add).then_inc(u_done, 1)
                dve.wait_ge(n_rows, s * 1 + 1)
                nc.vector.transpose(tn[:].rearrange("p c x -> p (c x)"), pn[:, 0:P]).then_inc(tn_done, 1)
                dve.wait_ge(tn_done, s * 1 + 1)
                nc.vector.tensor_tensor(cb(rn[:]), tn[:, :, 1:2 * B:2], cb(rz[:, 0:ST]), ALU.mult).then_inc(rn_done, 1)
                dve.wait_ge(rn_done, s * 1 + 1)
                dve.wait_ge(u_done, s * 1 + 1)
                nc.vector.tensor_tensor(npre[:], rn[:], u[:], ALU.add).then_inc(npre_done, 1)
                dve.wait_ge(side, s * 2 + 4)
                dve.wait_ge(tanh_done, s * 1 + 1)
                nc.vector.tensor_tensor_scan(t.h[:].rearrange("p c o -> p (c o)"), d0[:].rearrange("p c o -> p (c o)"),
                                             d1[:].rearrange("p c o -> p (c o)"), 0.0, ALU.mult, ALU.add).then_inc(h_ready, 1)
                dve.wait_ge(h_ready, s * 1 + 2)
                nc.vector.tensor_copy(t.hsT[:, :, :, bass.ds(s, 1)].rearrange("p k b o -> p (k b o)"), state).then_inc(hs_kept, 1)
            dve.wait_ge(hs_kept, T)


class AttentionCore:

    def __init__(self, nc, ctx, sem, prefix, NU, head, lane, scale, diagonal):
        self.nc, self.NU, self.head, self.lane, self.scale, self.diagonal = nc, NU, head, lane, scale, diagonal

        def sb(name, shape, dt=F32):
            return ctx.enter_context(nc.sbuf_tensor(prefix + name, shape, dt))

        self.prob, self.probT = sb("prob", [P, 2, 2, T]), sb("probT", [P, 2, 2, T])
        self.mx, self.nb, self.sums, self.rec = (sb(n, [P, 4, 2]) for n in ("mx", "nb", "sums", "rec"))
        self.ps = ctx.enter_context(nc.psum_tensor(prefix + "ps", [P, 4, T], F32))
        self.pt = ctx.enter_context(nc.psum_tensor(prefix + "pt", [P, 2, T], F32))
        self.po = ctx.enter_context(nc.psum_tensor(prefix + "po", [P, 2, 512], F32))
        self.o = self.po[:, :, 0:2 * DH].rearrange("p u (n d) -> p u n d", n=2)
        self.scored, self.max_done, self.bias_ready = sem("scored"), sem("max_done"), sem("bias_ready")
        self.prob_ready, self.transposed = sem("prob_ready"), sem("transposed")
        self.lane0_copied, self.lane1_copied = sem("lane0_copied"), sem("lane1_copied")
        self.product, self.rec_done, self.written = sem("product"), sem("rec_done"), sem("written")

    def wait(self, eng, sem, it, n):
        if n > 0:
            eng.wait_ge(sem, it * self.NU + n)

    def tensor(self, pe, it, q, v, ident, identb, maskb):
        nc = self.nc
        for step in range(self.NU + 2):
            u = step
            if u < self.NU:
                h = self.head(u)
                self.wait(pe, self.prob_ready, it, u - 1)
                for n in range(2):
                    qt, keys, L = self.lane(u, n)
                    bank = self.ps[:, 2 * (u % 2) + n, :]
                    last = nc.tensor.matmul(bank[:, 0:L], q[32 * h:32 * h + 32, qt * P:(qt + 1) * P],
                                            keys[32 * h:32 * h + 32, 0:L], start=True, stop=not self.diagonal)
                if self.diagonal:
                    for n in range(2):
                        qt, keys, L = self.lane(u, n)
                        last = nc.tensor.matmul(self.ps[:, 2 * (u % 2) + n, L - P:L], identb, maskb, start=False, stop=True)
                last.then_inc(self.scored, 1)
            u = step - 1
            if 0 <= u < self.NU:
                self.wait(pe, self.prob_ready, it, u + 1)
                self.wait(pe, self.lane0_copied, it, u)
                self.wait(pe, self.lane1_copied, it, u)
                for n in range(2):
                    L = self.lane(u, n)[2]
                    for kt in range(L // P):
                        last = nc.tensor.transpose(self.pt[:, n, kt * P:(kt + 1) * P],
                                                   self.prob[:, u % 2, n, kt * P:(kt + 1) * P], ident)
                last.then_inc(self.transposed, 1)
            u = step - 2
            if 0 <= u < self.NU:
                h = self.head(u)
                self.wait(pe, self.lane0_copied, it, u + 1)
                self.wait(pe, self.lane1_copied, it, u + 1)
                self.wait(pe, self.written, it, u - 1)
                for n in range(2):
                    L = self.lane(u, n)[2]
                    for kt in range(L // P):
                        last = nc.tensor.matmul(self.o[:, u % 2, n, :], self.probT[:, u % 2, n, kt * P:(kt + 1) * P],
                                                v[:, kt, h * DH:(h + 1) * DH], start=(kt == 0), stop=(kt == L // P - 1))
                last.then_inc(self.product, 1)

    def scalar(self, act, it):
        nc = self.nc
        for step in range(self.NU + 1):
            u = step
            if u < self.NU:
                self.wait(act, self.bias_ready, it, u + 1)
                self.wait(act, self.transposed, it, u - 1)
                for n in range(2):
                    L = self.lane(u, n)[2]
                    last = nc.scalar.activation(self.prob[:, u % 2, n, 0:L], self.ps[:, 2 * (u % 2) + n, 0:L], ACT.Exp,
                                                bias=self.nb[:, u % 4, n:n + 1], scale=self.scale,
                                                accum_out=self.sums[:, u % 4, n:n + 1])
                last.then_inc(self.prob_ready, 1)
            u = step - 1
            if 0 <= u < self.NU:
                L = self.lane(u, 0)[2]
                self.wait(act, self.transposed, it, u + 1)
                self.wait(act, self.product, it, u - 1)
                nc.scalar.activation(self.probT[:, u % 2, 0, 0:L], self.pt[:, 0, 0:L], ACT.Copy).then_inc(self.lane0_copied, 1)

    def vector(self, dve, it, write):
        nc = self.nc
        for step in range(self.NU + 3):
            u = step
            if u < self.NU:
                L = self.lane(u, 0)[2]
                self.wait(dve, self.scored, it, u + 1)
                nc.vector.tensor_reduce(self.mx[:, u % 4, :], self.ps[:, 2 * (u % 2):2 * (u % 2) + 2, 0:L], AX,
                                        ALU.max).then_inc(self.max_done, 1)
                self.wait(dve, self.max_done, it, u + 1)
                nc.vector.tensor_scalar(self.nb[:, u % 4, :], self.mx[:, u % 4, :], -self.scale, None,
                                        ALU.mult).then_inc(self.bias_ready, 1)
            u = step - 1
            if 0 <= u < self.NU:
                L = self.lane(u, 1)[2]
                self.wait(dve, self.transposed, it, u + 1)
                self.wait(dve, self.product, it, u - 1)
                nc.vector.tensor_copy(self.probT[:, u % 2, 1, 0:L], self.pt[:, 1, 0:L]).then_inc(self.lane1_copied, 1)
            u = step - 3
            if 0 <= u < self.NU:
                self.wait(dve, self.prob_ready, it, u + 1)
                nc.vector.reciprocal(self.rec[:, u % 4, :], self.sums[:, u % 4, :]).then_inc(self.rec_done, 1)
                self.wait(dve, self.rec_done, it, u + 1)
                self.wait(dve, self.product, it, u + 1)
                write(u).then_inc(self.written, 1)


def diff_attention_stage(nc, t, Wq, Wk, Wv, lambdas):
    with ExitStack() as ctx:
        sem = ctx.enter_context(Sems(nc, "da_"))

        def sb(name, shape, dt=F32):
            return ctx.enter_context(nc.sbuf_tensor("da_" + name, shape, dt))

        w = sb("w", [P, 3, KD, D])
        wqk = sb("wqk", [P, 2, KD, P])
        hb = sb("hb", [P, KD, T])
        cs = sb("cs", [P, 2, T])
        swap, half = sb("swap", [P, P]), sb("half", [P, 2])
        qk, rot, sw, cc = sb("qk", [P, 2, T]), sb("rot", [P, 2, T]), sb("sw", [P, 2, T]), sb("cc", [P, 2, T])
        keys = sb("keys", [P, 2, T])
        v = sb("v", [P, TT, P])
        identb, maskb = sb("identb", [P, P], BF16), sb("maskb", [P, P], BF16)
        maskf = sb("maskf", [P, P])
        lam = sb("lam", [P, 4, DQ])
        lp, ls, le, nlam = sb("lp", [P, 2, DQ]), sb("ls", [P, 2]), sb("le", [P, 2]), sb("nlam", [P, 2])
        lr, o2 = sb("lr", [P, 4]), sb("o2", [P, 4, DH])
        core = AttentionCore(nc, ctx, sem, "da_", H * TT // KD, lambda u: u // TT,
                             lambda u, n: (u % TT, keys[:, n, :], (u % TT + 1) * P), float(DQ) ** -0.5, True)
        w_in, const_in, hb_in, w_free = sem("w_in"), sem("const_in"), sem("hb_in"), sem("w_free")
        const_ready, lstep = sem("const_ready"), sem("lstep")
        projected, v_done, raw, v_ready = sem("projected"), sem("v_done"), sem("raw"), sem("v_ready")
        swapped, cosed, sined, rotated, keys_ready = (sem(n) for n in ("swapped", "cosed", "sined", "rotated", "keys_ready"))
        scaled = sem("scaled")
        block = ctx.enter_context(nc.Block())
        N_W, N_C = 16 * 3 * KD, 16 * (1 + 1 + 1 + 1 + 4)

        @block.sync
        def _(sp):
            for n, W in enumerate((Wq, Wk, Wv)):
                for jj in range(KD):
                    sp.dma_start(w[32 * jj:32 * jj + 32, n, :, :],
                                 W.rearrange("(jj c i) n -> jj i c n", jj=KD, c=KD)[jj]).then_inc(w_in, 16)
            sp.dma_start(cs[:], t.const["cs"].rearrange("a p t -> p a t")).then_inc(const_in, 16)
            sp.dma_start(swap[:], t.const["swap"]).then_inc(const_in, 16)
            sp.dma_start(half[:], t.const["half"]).then_inc(const_in, 16)
            sp.dma_start(maskf[:], t.const["mask"]).then_inc(const_in, 16)
            for n, l in enumerate(lambdas):
                sp.dma_start(lam[:, n, :], l.unsqueeze(0).broadcast_to([P, DQ])).then_inc(const_in, 16)
            sp.wait_ge(w_in, N_W)

            def load(b, g):
                sp.dma_start(hb[:], t.hsT[:, :, bass.ds(b, 1), :].rearrange("p k o t -> p (k o) t")).then_inc(hb_in, 16)
                for n in range(2):
                    sp.dma_start(wqk[:, n, :, :], w[:, n, :, bass.ds(g * P, P)]).then_inc(hb_in, 16)

            with sp.Fori(0, B) as b:
                with sp.Fori(0, KD) as g:
                    sp.wait_ge(w_free, b * KD + g + 1)
                    load(b, g)

        @block.gpsimd
        def _(pool):
            pool.wait_ge(const_in, N_C)
            with pool.Fori(0, B) as b:
                with pool.Fori(0, KD) as g:
                    it = b * KD + g
                    for n in range(2):
                        pool.wait_ge(raw, it * 2 + n + 1)
                        nc.gpsimd.tensor_tensor(cc[:, n, :], qk[:, n, :], cs[:, 0, :], ALU.mult).then_inc(cosed, 1)

        @block.tensor
        def _(pe):
            pe.wait_ge(w_in, N_W)
            pe.wait_ge(const_ready, 2)
            with pe.Fori(0, B) as b:
                with pe.Fori(0, KD) as g:
                    it = b * KD + g
                    pe.wait_ge(hb_in, it * 48 + 48)
                    for n in range(2):
                        for k in range(KD):
                            last = nc.tensor.matmul(core.ps[:, n, :], wqk[:, n, k, :], hb[:, k, :], start=(k == 0), stop=(k == KD - 1))
                        last.then_inc(projected, 1)
                    for tt in range(TT):
                        for k in range(KD):
                            last = nc.tensor.matmul(core.ps[:, 2, tt * P:(tt + 1) * P], hb[:, k, tt * P:(tt + 1) * P],
                                                    w[:, 2, k, bass.ds(g * P, P)], start=(k == 0), stop=(k == KD - 1))
                    last.then_inc(v_done, 1)
                    for n, bank in enumerate((core.ps[:, 3, :], core.pt[:, 0, :])):
                        pe.wait_ge(raw, it * 2 + n + 1)
                        nc.tensor.matmul(bank, swap[:], qk[:, n, :], start=True, stop=True).then_inc(swapped, 1)
                    pe.wait_ge(keys_ready, it * 2 + 2)
                    pe.wait_ge(v_ready, it * 1 + 1)
                    core.tensor(pe, it, rot[:, 0, :], v, t.ident[:], identb[:], maskb[:])

        @block.scalar
        def _(act):
            nc.scalar.preload_act_table_set("exp_and_others")
            act.wait_ge(lstep, 2)
            nc.scalar.activation(le[:], ls[:], ACT.Exp).then_inc(lstep, 1)
            with act.Fori(0, B) as b:
                with act.Fori(0, KD) as g:
                    it = b * KD + g
                    for n in range(2):
                        act.wait_ge(projected, it * 2 + n + 1)
                        nc.scalar.activation(qk[:, n, :], core.ps[:, n, :], ACT.Copy).then_inc(raw, 1)
                    act.wait_ge(v_done, it * 1 + 1)
                    nc.scalar.activation(v[:].rearrange("p t d -> p (t d)"), core.ps[:, 2, :], ACT.Copy).then_inc(v_ready, 1)
                    act.wait_ge(v_ready, it * 1 + 1)
                    act.sem_inc(w_free, 1)
                    core.scalar(act, it)

        @block.vector
        def _(dve):
            nc.vector.memset(nlam[:, 1:2], 0.0).then_inc(w_free, 1)
            dve.wait_ge(const_in, N_C)
            nc.vector.tensor_copy(maskb[:], maskf[:]).then_inc(const_ready, 1)
            nc.vector.tensor_copy(identb[:], t.ident[:]).then_inc(const_ready, 1)
            nc.vector.tensor_tensor(lp[:], lam[:, 0:4:2, :], lam[:, 1:4:2, :], ALU.mult).then_inc(lstep, 1)
            dve.wait_ge(lstep, 1)
            nc.vector.tensor_reduce(ls[:], lp[:], AX, ALU.add).then_inc(lstep, 1)
            dve.wait_ge(lstep, 3)
            nc.vector.tensor_tensor(nlam[:, 0:1], le[:, 1:2], le[:, 0:1], ALU.subtract).then_inc(lstep, 1)
            dve.wait_ge(lstep, 4)
            nc.vector.tensor_scalar(nlam[:, 1:2], nlam[:, 0:1], -LAMBDA_INIT, None, ALU.add).then_inc(lstep, 1)
            dve.wait_ge(lstep, 5)
            with dve.Fori(0, B) as b:
                with dve.Fori(0, KD) as g:
                    it = b * KD + g
                    for n, bank in enumerate((core.ps[:, 3, :], core.pt[:, 0, :])):
                        dve.wait_ge(swapped, it * 2 + n + 1)
                        nc.vector.tensor_tensor(sw[:, n, :], bank, cs[:, 1, :], ALU.mult).then_inc(sined, 1)
                        dve.wait_ge(sined, it * 2 + n + 1)
                        dve.wait_ge(cosed, it * 2 + n + 1)
                        last = nc.vector.tensor_tensor(rot[:, n, :], sw[:, n, :], cc[:, n, :], ALU.add)
                        last.then_inc(rotated, 1)
                    dve.wait_ge(rotated, it * 2 + 2)
                    for n in range(2):
                        nc.vector.tensor_scalar(keys[:, n, :], rot[:, 1, :], half[:, n:n + 1], None, ALU.mult).then_inc(keys_ready, 1)

                    def write(u):
                        h, i = u // TT, u % TT
                        nc.vector.tensor_scalar(lr[:, u % 4:u % 4 + 1], core.rec[:, u % 4, 1:2], nlam[:, 1:2], None, ALU.mult).then_inc(scaled, 1)
                        dve.wait_ge(scaled, it * (2 * core.NU) + 2 * u + 1)
                        nc.vector.tensor_scalar(o2[:, u % 4, :], core.o[:, u % 2, 1, :], lr[:, u % 4:u % 4 + 1], None, ALU.mult).then_inc(scaled, 1)
                        dve.wait_ge(scaled, it * (2 * core.NU) + 2 * u + 2)
                        dst = t.A[:, i, :, :].rearrange("p b f -> p (b f)")[:, bass.ds(b * D + g * P + h * DH, DH)]
                        return nc.vector.scalar_tensor_tensor(dst, core.o[:, u % 2, 0, :], core.rec[:, u % 4, 0:1], o2[:, u % 4, :],
                                                              op0=ALU.mult, op1=ALU.add)

                    core.vector(dve, it, write)


def filter_stage(nc, t, x, Wout, rms_weight, cond, W_emb, b_emb, g_norm):
    with ExitStack() as ctx:
        sem = ctx.enter_context(Sems(nc, "fi_"))

        def sb(name, shape, dt=F32):
            return ctx.enter_context(nc.sbuf_tensor("fi_" + name, shape, dt))

        filt, wout, wemb = sb("filt", [P, TT, T]), sb("wout", [P, KD, D]), sb("wemb", [P, KD, 2 * D])
        rmsw, condT, bg = sb("rmsw", [P, 1, D]), sb("condT", [P, KD, B]), sb("bg", [P, 3, KD])
        gs1, gain, shift = sb("gs1", [P, KD, B]), sb("gain", [P, KD, B]), sb("shift", [P, KD, B])
        xb = sb("xb", [P, TT, D])
        sq, y, yT = sb("sq", [P, TT, D]), sb("y", [P, TT, D]), sb("yT", [P, KD, T])
        ss, rs = sb("ss", [P, TT * H]), sb("rs", [P, TT * H])
        s2, r2 = sb("s2", [P, TT]), sb("r2", [P, TT])
        gain_b, shift_b = sb("gain_b", [P, KD]), sb("shift_b", [P, KD])
        pf = ctx.enter_context(nc.psum_tensor("fi_pf", [P, 4, 512], F32))
        pt = ctx.enter_context(nc.psum_tensor("fi_pt", [P, 4, 512], F32))
        const_in, x_in = sem("const_in"), sem("x_in")
        emb_done, gain_step, gain_ready = sem("emb_done"), sem("gain_step"), sem("gain_ready")
        filtered, squared, ss_done, ms_done, ln_done, rs_done = (sem(n) for n in (
            "filtered", "squared", "ss_done", "ms_done", "ln_done", "rs_done"))
        y1_done, y_ready, yT_psum, yT_act, yT_dve = (sem(n) for n in ("y1_done", "y_ready", "yT_psum", "yT_act", "yT_dve"))
        out_done, x1_ready, sq2, ms2, ln2, rs2 = (sem(n) for n in ("out_done", "x1_ready", "sq2", "ms2", "ln2", "rs2"))
        normed, nT_psum, nT_act, nT_dve = sem("normed"), sem("nT_psum"), sem("nT_act"), sem("nT_dve")
        block = ctx.enter_context(nc.Block())
        N_C = 16 * (4 + KD + 3)

        @block.sync
        def _(sp):
            sp.dma_start(filt[:], t.const["filt"].rearrange("(s p) t -> p s t", p=P)).then_inc(const_in, 16)
            sp.dma_start(wout[:], Wout.rearrange("(k p) n -> p k n", p=P)).then_inc(const_in, 16)
            sp.dma_start(wemb[:], W_emb.rearrange("(k p) n -> p k n", p=P)).then_inc(const_in, 16)
            rms_row = rms_weight.rearrange("(a h d) -> a h d", a=1, h=1)
            sp.dma_start(rmsw[:].rearrange("p o (h d) -> p (o h) d", h=H), rms_row.broadcast_to([P, H, DH])).then_inc(const_in, 16)
            for k in range(KD):
                sp.dma_start(condT[:, k, :], cond[:, k * P:(k + 1) * P].rearrange("b p -> p b"),
                             allow_slow_non_contiguous=True).then_inc(const_in, 16)
            for n, vec in enumerate((b_emb[0:D], b_emb[D:2 * D], g_norm)):
                sp.dma_start(bg[:, n, :], vec.rearrange("(k p) -> p k", p=P), allow_slow_non_contiguous=True).then_inc(const_in, 16)
            sp.dma_start(xb[:], x[0].rearrange("(tt p) d -> p tt d", p=P)).then_inc(x_in, 16)
            with sp.Fori(1, B) as b:
                sp.wait_ge(x1_ready, b * TT)
                sp.dma_start(xb[:], x[bass.ds(b, 1), :, :].rearrange("o (tt p) d -> p (o tt) d", p=P)).then_inc(x_in, 16)

        @block.tensor
        def _(pe):
            pe.wait_ge(const_in, N_C)
            for c in range(2 * KD):
                for k in range(KD):
                    last = nc.tensor.matmul(pf[:, 0, c * B:(c + 1) * B], wemb[:, k, c * P:(c + 1) * P], condT[:, k, :],
                                            start=(k == 0), stop=(k == KD - 1))
            last.then_inc(emb_done, 1)
            pe.wait_ge(gain_ready, 3)
            with pe.Fori(0, B) as b:
                for tt in range(TT):
                    for s in range(TT):
                        last = nc.tensor.matmul(pf[:, tt, :], filt[:, s, tt * P:(tt + 1) * P],
                                                t.A[:, s, bass.ds(b, 1), :].rearrange("p o f -> p (o f)"),
                                                start=(s == 0), stop=(s == TT - 1))
                last.then_inc(filtered, 1)
                pe.wait_ge(y_ready, b * 1 + 1)
                for k in range(KD):
                    for tt in range(TT):
                        last = nc.tensor.transpose(pt[:, k, tt * P:(tt + 1) * P], y[:, tt, k * P:(k + 1) * P], t.ident[:])
                    last.then_inc(yT_psum, 1)
                pe.wait_ge(yT_act, b * 2 + 2)
                pe.wait_ge(yT_dve, b * 2 + 2)
                for tt in range(TT):
                    for k in range(KD):
                        last = nc.tensor.matmul(pf[:, tt, :], yT[:, k, tt * P:(tt + 1) * P], wout[:, k, :],
                                                start=(k == 0), stop=(k == KD - 1))
                    last.then_inc(out_done, 1)
                pe.wait_ge(normed, b * TT + TT)
                for k in range(KD):
                    for tt in range(TT):
                        last = nc.tensor.transpose(pt[:, k, tt * P:(tt + 1) * P], y[:, tt, k * P:(k + 1) * P], t.ident[:])
                    last.then_inc(nT_psum, 1)
                pe.wait_ge(nT_act, b * 2 + 2)
                pe.wait_ge(nT_dve, b * 2 + 2)

        @block.scalar
        def _(act):
            nc.scalar.preload_act_table_set("natural_log_exp_and_others")
            act.wait_ge(gain_ready, 3)
            with act.Fori(0, B) as b:
                act.wait_ge(filtered, b * 1 + 1)
                nc.scalar.activation(sq[:], pf[:], ACT.Square).then_inc(squared, 1)
                act.wait_ge(ms_done, b * 1 + 1)
                nc.scalar.activation(rs[:], ss[:], ACT.Ln).then_inc(ln_done, 1)
                act.wait_ge(ln_done, b * 1 + 1)
                nc.scalar.activation(rs[:], rs[:], ACT.Exp, scale=-0.5).then_inc(rs_done, 1)
                for k in (0, 2):
                    act.wait_ge(yT_psum, b * KD + k + 1)
                    nc.scalar.activation(yT[:, k, :], pt[:, k, :], ACT.Copy).then_inc(yT_act, 1)
                for tt in range(TT):
                    act.wait_ge(x1_ready, b * TT + tt + 1)
                    nc.scalar.activation(sq[:, tt, :], t.x1[:, bass.ds(b * TT + tt, 1), :].rearrange("p o d -> p (o d)"),
                                         ACT.Square, accum_out=s2[:, tt:tt + 1]).then_inc(sq2, 1)
                act.wait_ge(ms2, b * 1 + 1)
                nc.scalar.activation(r2[:], s2[:], ACT.Ln).then_inc(ln2, 1)
                act.wait_ge(ln2, b * 1 + 1)
                nc.scalar.activation(r2[:], r2[:], ACT.Exp, scale=-0.5).then_inc(rs2, 1)
                for k in (0, 2):
                    act.wait_ge(nT_psum, b * KD + k + 1)
                    nc.scalar.activation(t.xnT[:, bass.ds(b, 1), k, :].rearrange("p o t -> p (o t)"), pt[:, k, :], ACT.Identity,
                                         bias=shift_b[:, k:k + 1], scale=gain_b[:, k:k + 1]).then_inc(nT_act, 1)

        @block.vector
        def _(dve):
            dve.wait_ge(emb_done, 1)
            sc = pf[:, 0, 0:KD * B].rearrange("p (k b) -> p k b", b=B)
            sh = pf[:, 0, KD * B:2 * KD * B].rearrange("p (k b) -> p k b", b=B)
            nc.vector.tensor_tensor(gs1[:], sc, bg[:, 0, :].unsqueeze(2).broadcast_to([P, KD, B]), ALU.add).then_inc(gain_step, 1)
            nc.vector.tensor_tensor(shift[:], sh, bg[:, 1, :].unsqueeze(2).broadcast_to([P, KD, B]), ALU.add).then_inc(gain_ready, 1)
            dve.wait_ge(gain_step, 1)
            nc.vector.scalar_tensor_tensor(gain[:], gs1[:], 1.0, bg[:, 2, :].unsqueeze(2).broadcast_to([P, KD, B]),
                                           op0=ALU.add, op1=ALU.mult).then_inc(gain_ready, 1)
            nc.vector.tensor_scalar(rmsw[:], rmsw[:], 1.0 - LAMBDA_INIT, None, ALU.mult).then_inc(gain_ready, 1)
            dve.wait_ge(gain_ready, 3)
            heads = "p tt (h d) -> p (tt h) d"
            with dve.Fori(0, B) as b:
                dve.wait_ge(squared, b * 1 + 1)
                nc.vector.tensor_reduce(ss[:], sq[:].rearrange(heads, h=H), AX, ALU.add).then_inc(ss_done, 1)
                dve.wait_ge(ss_done, b * 1 + 1)
                nc.vector.tensor_scalar(ss[:], ss[:], 1.0 / DH, 1e-5, ALU.mult, ALU.add).then_inc(ms_done, 1)
                dve.wait_ge(rs_done, b * 1 + 1)
                nc.vector.tensor_tensor(y[:].rearrange(heads, h=H), pf[:].rearrange(heads, h=H),
                                        rs[:].unsqueeze(2).broadcast_to([P, TT * H, DH]), ALU.mult).then_inc(y1_done, 1)
                dve.wait_ge(y1_done, b * 1 + 1)
                nc.vector.tensor_tensor(y[:], y[:], rmsw[:].broadcast_to([P, TT, D]), ALU.mult).then_inc(y_ready, 1)
                for k in (1, 3):
                    dve.wait_ge(yT_psum, b * KD + k + 1)
                    nc.vector.tensor_copy(yT[:, k, :], pt[:, k, :]).then_inc(yT_dve, 1)
                dve.wait_ge(x_in, b * 16 + 16)
                for tt in range(TT):
                    dve.wait_ge(out_done, b * TT + tt + 1)
                    nc.vector.tensor_tensor(t.x1[:, bass.ds(b * TT + tt, 1), :].rearrange("p o d -> p (o d)"), pf[:, tt, :],
                                            xb[:, tt, :], ALU.add).then_inc(x1_ready, 1)
                nc.vector.tensor_copy(gain_b[:], gain[:, :, bass.ds(b, 1)].rearrange("p k o -> p (k o)"))
                nc.vector.tensor_copy(shift_b[:], shift[:, :, bass.ds(b, 1)].rearrange("p k o -> p (k o)"))
                dve.wait_ge(sq2, b * TT + TT)
                nc.vector.tensor_scalar(s2[:], s2[:], 1.0 / D, 1e-6, ALU.mult, ALU.add).then_inc(ms2, 1)
                dve.wait_ge(rs2, b * 1 + 1)
                for tt in range(TT):
                    nc.vector.tensor_scalar(y[:, tt, :], t.x1[:, bass.ds(b * TT + tt, 1), :].rearrange("p o d -> p (o d)"),
                                            r2[:, tt:tt + 1], None, ALU.mult).then_inc(normed, 1)
                for k in (1, 3):
                    dve.wait_ge(nT_psum, b * KD + k + 1)
                    nc.vector.tensor_scalar(t.xnT[:, bass.ds(b, 1), k, :].rearrange("p o t -> p (o t)"), pt[:, k, :],
                                            gain_b[:, k:k + 1], shift_b[:, k:k + 1], ALU.mult, ALU.add).then_inc(nT_dve, 1)


def full_attention_stage(nc, t, W_qkv, g_q, g_k):
    with ExitStack() as ctx:
        sem = ctx.enter_context(Sems(nc, "fa_"))

        def sb(name, shape, dt=F32):
            return ctx.enter_context(nc.sbuf_tensor("fa_" + name, shape, dt))

        w, wqk, hb = sb("w", [P, KD, 3 * D]), sb("wqk", [P, 2, KD, P]), sb("hb", [P, KD, T])
        ones, g = sb("ones", [P, P]), sb("g", [P, 2])
        sq, rs, qk, v = sb("sq", [P, 2, T]), sb("rs", [P, 2, T]), sb("qk", [P, 2, T]), sb("v", [P, TT, P])
        eps = sb("eps", [P, 1])
        NU = HG * TT // 2
        core = AttentionCore(nc, ctx, sem, "fa_", NU, lambda u: u // (TT // 2),
                             lambda u, n: (2 * (u % (TT // 2)) + n, qk[:, 1, :], T), float(DH) ** -0.5, False)
        w_in, const_in, hb_in, w_free, eps_set = sem("w_in"), sem("const_in"), sem("hb_in"), sem("w_free"), sem("eps_set")
        projected, v_done, v_ready, squared, summed, ln_done, rs_done, qk_ready = (sem(n) for n in (
            "projected", "v_done", "v_ready", "squared", "summed", "ln_done", "rs_done", "qk_ready"))
        block = ctx.enter_context(nc.Block())
        N_C = 16 * (1 + 2 * HG)

        @block.sync
        def _(sp):
            sp.dma_start(w[:], W_qkv.rearrange("(k p) n -> p k n", p=P)).then_inc(w_in, 16)
            sp.dma_start(ones[:], t.const["headones"]).then_inc(const_in, 16)
            for n, vec in enumerate((g_q, g_k)):
                for h in range(HG):
                    sp.dma_start(g[DH * h:DH * h + DH, n:n + 1], vec.unsqueeze(1)).then_inc(const_in, 16)
            sp.wait_ge(w_in, 16)
            with sp.Fori(0, B) as b:
                with sp.Fori(0, KD) as gg:
                    sp.wait_ge(w_free, b * KD + gg + 1)
                    sp.dma_start(hb[:], t.xnT[:, bass.ds(b, 1), :, :].rearrange("p o k t -> p (o k) t")).then_inc(hb_in, 16)
                    for n in range(2):
                        sp.dma_start(wqk[:, n, :, :], w[:, :, bass.ds(gg * P + n * D, P)]).then_inc(hb_in, 16)

        @block.tensor
        def _(pe):
            pe.wait_ge(w_in, 16)
            pe.wait_ge(const_in, N_C)
            with pe.Fori(0, B) as b:
                with pe.Fori(0, KD) as gg:
                    it = b * KD + gg
                    pe.wait_ge(hb_in, it * 48 + 48)
                    for n in range(2):
                        for k in range(KD):
                            last = nc.tensor.matmul(core.ps[:, n, :], wqk[:, n, k, :], hb[:, k, :], start=(k == 0), stop=(k == KD - 1))
                        last.then_inc(projected, 1)
                    for tt in range(TT):
                        for k in range(KD):
                            last = nc.tensor.matmul(core.ps[:, 2, tt * P:(tt + 1) * P], hb[:, k, tt * P:(tt + 1) * P],
                                                    w[:, k, bass.ds(gg * P + 2 * D, P)], start=(k == 0), stop=(k == KD - 1))
                    last.then_inc(v_done, 1)
                    for n, bank in enumerate((core.ps[:, 3, :], core.pt[:, 0, :])):
                        pe.wait_ge(squared, it * 2 + n + 1)
                        nc.tensor.matmul(bank, ones[:], sq[:, n, :], start=True, stop=True).then_inc(summed, 1)
                    pe.wait_ge(qk_ready, it * 2 + 2)
                    pe.wait_ge(v_ready, it * 1 + 1)
                    core.tensor(pe, it, qk[:, 0, :], v, t.ident[:], None, None)

        @block.scalar
        def _(act):
            nc.scalar.preload_act_table_set("natural_log_exp_and_others")
            act.wait_ge(eps_set, 1)
            with act.Fori(0, B) as b:
                with act.Fori(0, KD) as gg:
                    it = b * KD + gg
                    for n in range(2):
                        act.wait_ge(projected, it * 2 + n + 1)
                        nc.scalar.activation(sq[:, n, :], core.ps[:, n, :], ACT.Square).then_inc(squared, 1)
                    act.wait_ge(v_done, it * 1 + 1)
                    nc.scalar.activation(v[:].rearrange("p t d -> p (t d)"), core.ps[:, 2, :], ACT.Copy).then_inc(v_ready, 1)
                    act.wait_ge(v_ready, it * 1 + 1)
                    act.sem_inc(w_free, 1)
                    for n, bank in enumerate((core.ps[:, 3, :], core.pt[:, 0, :])):
                        act.wait_ge(summed, it * 2 + n + 1)
                        nc.scalar.activation(rs[:, n, :], bank, ACT.Ln, bias=eps[:, 0:1], scale=1.0 / DH).then_inc(ln_done, 1)
                        act.wait_ge(ln_done, it * 2 + n + 1)
                        nc.scalar.activation(rs[:, n, :], rs[:, n, :], ACT.Exp, scale=-0.5).then_inc(rs_done, 1)
                    core.scalar(act, it)

        @block.vector
        def _(dve):
            nc.vector.memset(eps[:], 1e-6).then_inc(eps_set, 1)
            dve.sem_inc(w_free, 1)
            dve.wait_ge(const_in, N_C)
            with dve.Fori(0, B) as b:
                with dve.Fori(0, KD) as gg:
                    it = b * KD + gg
                    for n in range(2):
                        dve.wait_ge(rs_done, it * 2 + n + 1)
                        nc.vector.scalar_tensor_tensor(qk[:, n, :], core.ps[:, n, :], g[:, n:n + 1], rs[:, n, :],
                                                       op0=ALU.mult, op1=ALU.mult).then_inc(qk_ready, 1)

                    def write(u):
                        h = core.head(u)
                        i = core.lane(u, 0)[0]
                        for n in range(2):
                            dst = t.A[:, i + n, :, :].rearrange("p b f -> p (b f)")[:, bass.ds(b * D + gg * P + h * DH, DH)]
                            last = nc.vector.tensor_scalar(dst, core.o[:, u % 2, n, :], core.rec[:, u % 4, n:n + 1], None, ALU.mult)
                        return last

                    core.vector(dve, it, write)




def route_stage(nc, t, W_out, gate_w, sg_w, su_w, sd_w):
    with ExitStack() as ctx:
        sem = ctx.enter_context(Sems(nc, "ro_"))

        def sb(name, shape, dt=F32):
            return ctx.enter_context(nc.sbuf_tensor("ro_" + name, shape, dt))

        NC = SI // P
        wout, stage = sb("wout", [P, KD, D]), sb("stage", [P, 4, D])
        gwT, sgT, suT, sdT = sb("gwT", [P, KD, E]), sb("sgT", [P, KD, SI]), sb("suT", [P, KD, SI]), sb("sdT", [P, NC, D])
        sdraw = sb("sdraw", [P, KD, SI])
        ob, oT, yb = sb("ob", [P, TT, D]), sb("oT", [P, KD, T]), sb("yb", [P, TT, D])
        sil, hT = sb("sil", [P, 2, T]), sb("hT", [P, NC, T])
        lf, before, ones, carry = sb("lf", [P, P]), sb("before", [P, P], BF16), sb("ones", [P, P], BF16), sb("carry", [P, E], BF16)
        iota = sb("iota", [P, E])
        lg, v8, i8 = sb("lg", [P, TT, E]), sb("v8", [P, TT, 8]), sb("i8", [P, TT, 8], U32)
        nv, ex, se, ev, rs = sb("nv", [P, TT]), sb("ex", [P, TT, E]), sb("se", [P, TT]), sb("ev", [P, TT, 8]), sb("rs", [P, TT])
        ef, oh, mask = sb("ef", [P, TT * K]), sb("oh", [P, TT * K, E], BF16), sb("mask", [P, TT, E], BF16)
        posb, pr, pk, valid, sf = sb("posb", [P, TT, E], BF16), sb("pr", [P, TT * K, E]), sb("pk", [P, TT * K]), sb("valid", [P, TT * K]), sb("sf", [P, TT * K])
        slot = sb("slot", [P, TT * K], U32)
        pa = ctx.enter_context(nc.psum_tensor("ro_pa", [P, 4, 512], F32))
        pb = ctx.enter_context(nc.psum_tensor("ro_pb", [P, 4, 512], F32))
        names = """const_in raw_in zeroed setup_psum setup_copied ready ob_in oT_psum oT_act oT_dve y_psum y_ready
            yT_psum yT_act yT_dve logits gates ups silued hidden down_done added lg_copied top8 found nv_done
            exps e_done rs_done w1_done cast1 onehot masked mask_ready placed prod_done pk_done valid_done base_done
            base2_done sf_done tick slots_ready scattered w_done carried ld""".split()
        S = {n: sem(n) for n in names}
        block = ctx.enter_context(nc.Block())
        N_C = 16 * 3

        @block.sync
        def _(sp):
            sp.dma_start(wout[:], W_out.rearrange("(k p) n -> p k n", p=P)).then_inc(S["const_in"], 16)
            sp.dma_start(lf[:], t.const["before"]).then_inc(S["const_in"], 16)
            sp.dma_start(iota[:], t.const["iota"].unsqueeze(0).broadcast_to([P, E])).then_inc(S["const_in"], 16)
            sp.dma_start(stage[0:E, 0, :], gate_w).then_inc(S["raw_in"], 16)
            sp.dma_start(stage[:, 1:4, :], sg_w.rearrange("(c p) n -> p c n", p=P)).then_inc(S["raw_in"], 16)
            sp.dma_start(sdraw[:], sd_w.rearrange("(k p) n -> p k n", p=P)).then_inc(S["raw_in"], 16)
            sp.wait_ge(S["setup_copied"], 2 * KD)
            sp.dma_start(stage[:, 1:4, :], su_w.rearrange("(c p) n -> p c n", p=P)).then_inc(S["raw_in"], 16)
            with sp.Fori(0, B) as b:
                sp.wait_ge(S["ld"], b * 1 + 1)
                sp.dma_start(ob[:], t.A[:, :, bass.ds(b, 1), :].rearrange("p t o f -> p (t o) f")).then_inc(S["ob_in"], 16)

        @block.tensor
        def _(pe):
            pe.wait_ge(S["raw_in"], 48)
            for k in range(KD):
                nc.tensor.transpose(pa[:, k, 0:E], stage[0:E, 0, k * P:(k + 1) * P], t.ident[0:E, 0:E]).then_inc(S["setup_psum"], 1)
            for k in range(KD):
                for c in range(NC):
                    last = nc.tensor.transpose(pb[:, k, c * P:(c + 1) * P], stage[:, 1 + c, k * P:(k + 1) * P], t.ident[:])
                last.then_inc(S["setup_psum"], 1)
            pe.wait_ge(S["setup_copied"], 2 * KD)
            for c in range(NC):
                for k in range(KD):
                    last = nc.tensor.transpose(pa[:, c, k * P:(k + 1) * P], sdraw[:, k, c * P:(c + 1) * P], t.ident[:])
                last.then_inc(S["setup_psum"], 1)
            pe.wait_ge(S["raw_in"], 64)
            for k in range(KD):
                for c in range(NC):
                    last = nc.tensor.transpose(pb[:, k, c * P:(c + 1) * P], stage[:, 1 + c, k * P:(k + 1) * P], t.ident[:])
                last.then_inc(S["setup_psum"], 1)
            pe.wait_ge(S["setup_copied"], 3 * KD + NC)
            pe.wait_ge(S["ready"], 3)
            with pe.Fori(0, B) as b:
                pe.wait_ge(S["ob_in"], b * 16 + 16)
                for k in range(KD):
                    for tt in range(TT):
                        last = nc.tensor.transpose(pa[:, k, tt * P:(tt + 1) * P], ob[:, tt, k * P:(k + 1) * P], t.ident[:])
                    last.then_inc(S["oT_psum"], 1)
                pe.wait_ge(S["oT_act"], b * 2 + 2)
                pe.wait_ge(S["oT_dve"], b * 2 + 2)
                for tt in range(TT):
                    for k in range(KD):
                        last = nc.tensor.matmul(pb[:, tt, :], oT[:, k, tt * P:(tt + 1) * P], wout[:, k, :], start=(k == 0), stop=(k == KD - 1))
                    last.then_inc(S["y_psum"], 1)
                pe.wait_ge(S["y_ready"], b * TT + TT)
                for k in range(KD):
                    for tt in range(TT):
                        last = nc.tensor.transpose(pa[:, k, tt * P:(tt + 1) * P], yb[:, tt, k * P:(k + 1) * P], t.ident[:])
                    last.then_inc(S["yT_psum"], 1)
                pe.wait_ge(S["yT_act"], b * 2 + 2)
                pe.wait_ge(S["yT_dve"], b * 2 + 2)
                for tt in range(TT):
                    for k in range(KD):
                        last = nc.tensor.matmul(pb[:, 0, tt * E:(tt + 1) * E], oT[:, k, tt * P:(tt + 1) * P], gwT[:, k, :], start=(k == 0), stop=(k == KD - 1))
                last.then_inc(S["logits"], 1)
                for c in range(NC):
                    if c >= 2:
                        pe.wait_ge(S["hidden"], b * NC + c - 1)
                    for wT, n, done in ((sgT, 0, "gates"), (suT, 1, "ups")):
                        for k in range(KD):
                            last = nc.tensor.matmul(pa[:, 2 * (c % 2) + n, :], wT[:, k, c * P:(c + 1) * P], oT[:, k, :], start=(k == 0), stop=(k == KD - 1))
                        last.then_inc(S[done], 1)
                pe.wait_ge(S["hidden"], b * NC + NC)
                pe.wait_ge(S["lg_copied"], b * 1 + 1)
                for tt in range(TT):
                    for c in range(NC):
                        last = nc.tensor.matmul(pb[:, tt, :], hT[:, c, tt * P:(tt + 1) * P], sdT[:, c, :], start=(c == 0), stop=(c == NC - 1))
                    last.then_inc(S["down_done"], 1)
                pe.wait_ge(S["mask_ready"], b * 1 + 1)
                for tt in range(TT):
                    acc = pa[:, 0, tt * E:(tt + 1) * E]
                    nc.tensor.matmul(acc, ones[:], carry[:], start=True, stop=False)
                    for u in range(tt):
                        nc.tensor.matmul(acc, ones[:], mask[:, u, :], start=False, stop=False)
                    last = nc.tensor.matmul(acc, before[:], mask[:, tt, :], start=False, stop=True)
                last.then_inc(S["placed"], 1)
                pe.wait_ge(S["prod_done"], b * 1 + 1)
                pe.wait_ge(S["added"], b * TT + TT)

        @block.scalar
        def _(act):
            with act.Fori(0, B) as b:
                for k in (0, 2):
                    act.wait_ge(S["oT_psum"], b * KD + k + 1)
                    nc.scalar.activation(oT[:, k, :], pa[:, k, :], ACT.Copy).then_inc(S["oT_act"], 1)
                for k in (0, 2):
                    act.wait_ge(S["yT_psum"], b * KD + k + 1)
                    nc.scalar.activation(oT[:, k, :], pa[:, k, :], ACT.Copy).then_inc(S["yT_act"], 1)
                act.wait_ge(S["nv_done"], b * 1 + 1)
                for tt in range(TT):
                    nc.scalar.activation(ex[:, tt, :], lg[:, tt, :], ACT.Exp, bias=nv[:, tt:tt + 1], accum_out=se[:, tt:tt + 1])
                    last = nc.scalar.activation(ev[:, tt, :], v8[:, tt, :], ACT.Exp, bias=nv[:, tt:tt + 1])
                last.then_inc(S["exps"], 1)
                for c in range(NC):
                    act.wait_ge(S["gates"], b * NC + c + 1)
                    if c >= 2:
                        act.wait_ge(S["hidden"], b * NC + c - 1)
                    nc.scalar.activation(sil[:, c % 2, :], pa[:, 2 * (c % 2), :], ACT.Silu).then_inc(S["silued"], 1)

        @block.gpsimd
        def _(pool):
            pool.sem_inc(S["w_done"], 1)
            with pool.Fori(0, B) as b:
                pool.wait_ge(S["slots_ready"], b * 1 + 1)
                pool.sem_inc(S["tick"], 1)
                for tt in range(TT):
                    for k in range(K):
                        nc.gpsimd.indirect_dma_start(
                            out=t.xg_dram, out_offset=bass.IndirectOffsetOnAxis(ap=slot[:, tt * K + k:tt * K + k + 1], axis=0),
                            in_=yb[:, tt, :], in_offset=None, bounds_check=SLOTS - 1, oob_is_err=False).then_inc(S["scattered"], 16)
                pool.wait_ge(S["scattered"], b * (TT * K * 16) + TT * K * 16)
                pool.sem_inc(S["w_done"], 1)

        @block.vector
        def _(dve):
            dve.sem_inc(S["ld"], 1)
            dve.sem_inc(S["carried"], 1)
            nc.vector.memset(ones[:], 1.0).then_inc(S["ready"], 1)
            nc.vector.memset(carry[:], 0.0).then_inc(S["ready"], 1)
            n = 0

            def setup(dst, src, at):
                dve.wait_ge(S["setup_psum"], at)
                nc.vector.tensor_copy(dst, src).then_inc(S["setup_copied"], 1)

            for k in range(KD):
                setup(gwT[:, k, :], pa[:, k, 0:E], k + 1)
            for k in range(KD):
                setup(sgT[:, k, :], pb[:, k, 0:SI], KD + k + 1)
            for c in range(NC):
                setup(sdT[:, c, :], pa[:, c, :], 2 * KD + c + 1)
            for k in range(KD):
                setup(suT[:, k, :], pb[:, k, 0:SI], 2 * KD + NC + k + 1)
            dve.wait_ge(S["const_in"], N_C)
            nc.vector.tensor_copy(before[:], lf[:]).then_inc(S["ready"], 1)
            with dve.Fori(0, B) as b:
                one = b * 1 + 1
                for k in (1, 3):
                    dve.wait_ge(S["oT_psum"], b * KD + k + 1)
                    nc.vector.tensor_copy(oT[:, k, :], pa[:, k, :]).then_inc(S["oT_dve"], 1)
                for tt in range(TT):
                    dve.wait_ge(S["y_psum"], b * TT + tt + 1)
                    if tt == 0:
                        dve.wait_ge(S["w_done"], one)
                    nc.vector.tensor_tensor(yb[:, tt, :], pb[:, tt, :], ob[:, tt, :], ALU.add).then_inc(S["y_ready"], 1)
                dve.wait_ge(S["y_ready"], b * TT + TT)
                dve.sem_inc(S["ld"], 1)
                for k in (1, 3):
                    dve.wait_ge(S["yT_psum"], b * KD + k + 1)
                    nc.vector.tensor_copy(oT[:, k, :], pa[:, k, :]).then_inc(S["yT_dve"], 1)
                dve.wait_ge(S["logits"], one)
                nc.vector.tensor_copy(lg[:].rearrange("p t e -> p (t e)"), pb[:, 0, 0:TT * E]).then_inc(S["lg_copied"], 1)
                dve.wait_ge(S["lg_copied"], one)
                dve.sem_inc(S["tick"], 1)
                for tt in range(TT):
                    nc.vector.max(v8[:, tt, :], lg[:, tt, :]).then_inc(S["top8"], 1)
                dve.wait_ge(S["top8"], b * TT + TT)
                nc.vector.tensor_scalar(nv[:], v8[:, :, 0], -1.0, None, ALU.mult).then_inc(S["nv_done"], 1)
                for tt in range(TT):
                    nc.vector.max_index(i8[:, tt, :], v8[:, tt, :], lg[:, tt, :]).then_inc(S["found"], 1)
                dve.wait_ge(S["found"], b * TT + TT)
                k24 = "p (t k) -> p t k"
                nc.vector.tensor_copy(ef[:].rearrange(k24, k=K), i8[:, :, 0:K]).then_inc(S["cast1"], 1)
                dve.wait_ge(S["cast1"], one)
                nc.vector.tensor_tensor(oh[:], iota[:].unsqueeze(1).broadcast_to([P, TT * K, E]),
                                        ef[:].unsqueeze(2).broadcast_to([P, TT * K, E]), ALU.is_equal).then_inc(S["onehot"], 1)
                dve.wait_ge(S["onehot"], one)
                with nc.allow_low_precision("a sum of at most one 1 is exact"):
                    for tt in range(TT):
                        nc.vector.tensor_reduce(mask[:, tt, :], oh[:, tt * K:(tt + 1) * K, :].rearrange("p k e -> p e k"), AX,
                                                ALU.add).then_inc(S["masked"], 1)
                dve.wait_ge(S["masked"], b * TT + TT)
                dve.wait_ge(S["carried"], b * TT + 1)
                dve.sem_inc(S["mask_ready"], 1)
                for c in range(NC):
                    dve.wait_ge(S["silued"], b * NC + c + 1)
                    dve.wait_ge(S["ups"], b * NC + c + 1)
                    nc.vector.tensor_tensor(hT[:, c, :], sil[:, c % 2, :], pa[:, 2 * (c % 2) + 1, :], ALU.mult).then_inc(S["hidden"], 1)
                dve.wait_ge(S["exps"], one)
                nc.vector.reciprocal(rs[:], se[:]).then_inc(S["rs_done"], 1)
                dve.wait_ge(S["rs_done"], one)
                wk = t.wk[:, bass.ds(b, 1), :].rearrange("p o k -> p (o k)")
                nc.vector.tensor_tensor(wk.rearrange(k24, k=K), ev[:, :, 0:K], rs[:].unsqueeze(2).broadcast_to([P, TT, K]),
                                        ALU.mult).then_inc(S["w1_done"], 1)
                for tt in range(TT):
                    dve.wait_ge(S["down_done"], b * TT + tt + 1)
                    x1 = t.x1[:, bass.ds(b * TT + tt, 1), :].rearrange("p o d -> p (o d)")
                    nc.vector.tensor_tensor(x1, x1, pb[:, tt, :], ALU.add).then_inc(S["added"], 1)
                dve.wait_ge(S["placed"], one)
                for tt in range(TT):
                    last = nc.vector.tensor_tensor(pr[:, tt * K:(tt + 1) * K, :], oh[:, tt * K:(tt + 1) * K, :],
                                                   pa[:, 0, tt * E:(tt + 1) * E].unsqueeze(1).broadcast_to([P, K, E]), ALU.mult)
                last.then_inc(S["prod_done"], 1)
                dve.wait_ge(S["prod_done"], one)
                nc.vector.tensor_reduce(pk[:], pr[:], AX, ALU.add).then_inc(S["pk_done"], 1)
                dve.wait_ge(S["pk_done"], one)
                nc.vector.tensor_scalar(valid[:], pk[:], float(CAP), None, ALU.is_lt).then_inc(S["valid_done"], 1)
                nc.vector.scalar_tensor_tensor(sf[:], ef[:], float(CAP), pk[:], op0=ALU.mult, op1=ALU.add).then_inc(S["base_done"], 1)
                dve.wait_ge(S["valid_done"], one)
                dve.wait_ge(S["base_done"], one)
                nc.vector.scalar_tensor_tensor(sf[:], sf[:], -float(SLOTS), valid[:], op0=ALU.add, op1=ALU.mult).then_inc(S["base2_done"], 1)
                dve.wait_ge(S["base2_done"], one)
                nc.vector.tensor_scalar(sf[:], sf[:], float(SLOTS), None, ALU.add).then_inc(S["sf_done"], 1)
                dve.wait_ge(S["sf_done"], one)
                nc.vector.tensor_copy(slot[:], sf[:]).then_inc(S["slots_ready"], 1)
                nc.vector.tensor_copy(t.slot[:, bass.ds(b, 1), :].rearrange("p o k -> p (o k)"), sf[:])
                dve.wait_ge(S["w1_done"], one)
                nc.vector.tensor_tensor(wk, wk, valid[:], ALU.mult)
                for tt in range(TT):
                    dve.wait_ge(S["carried"], b * TT + tt + 1)
                    nc.vector.tensor_tensor(carry[:], carry[:], mask[:, tt, :], ALU.add).then_inc(S["carried"], 1)


def expert_stage(nc, t, gate_up, down):
    with ExitStack() as ctx:
        sem = ctx.enter_context(Sems(nc, "ex_"))
        U = 4

        def sb(name, shape, dt=F32):
            return ctx.enter_context(nc.sbuf_tensor("ex_" + name, shape, dt))

        HC = I // 2
        wg, wd, xg = sb("wg", [P, U, KD, 2 * I]), sb("wd", [HC, U, 2, D]), sb("xg", [P, U, D])
        xT, sil, hid, hT, eo = sb("xT", [P, 2, KD, P]), sb("sil", [P, 2, I]), sb("hid", [P, 2, I]), sb("hT", [HC, 2, 2, P]), sb("eo", [P, 2, D])
        px = ctx.enter_context(nc.psum_tensor("ex_px", [P, 2, 512], F32))
        pg = ctx.enter_context(nc.psum_tensor("ex_pg", [P, 2, 512], F32))
        ph = ctx.enter_context(nc.psum_tensor("ex_ph", [P, 2, 512], F32))
        pd = ctx.enter_context(nc.psum_tensor("ex_pd", [P, 2, 512], F32))
        w_in = [sem(f"w_in{u}") for u in range(U)]
        xT_psum, xT_ready, gu_done, silued, hid_ready, hT_psum, hT_ready, down_done, eo_ready = (sem(n) for n in (
            "xT_psum", "xT_ready", "gu_done", "silued", "hid_ready", "hT_psum", "hT_ready", "down_done", "eo_ready"))
        stored = [sem("stored0"), sem("stored1")]
        block = ctx.enter_context(nc.Block())
        NL = E // U

        def load(sp, e, u):
            sp.dma_start(xg[:, u, :], t.xg_dram[bass.ds(e * CAP, CAP), :]).then_inc(w_in[u], 16)
            sp.dma_start(wg[:, u, :, :], gate_up[bass.ds(e, 1), :, :].rearrange("o (k p) i -> p (o k) i", p=P)).then_inc(w_in[u], 16)
            sp.dma_start(wd[:, u, :, :], down[bass.ds(e, 1), :, :].rearrange("o (c q) h -> q (o c) h", q=HC)).then_inc(w_in[u], 16)

        def wait(eng, s, q, n):
            eng.wait_ge(s, q * U + n)

        @block.sync
        def _(sp):
            for u in range(U):
                load(sp, u, u)
            with sp.Fori(0, NL - 1) as q:
                for u in range(U):
                    wait(sp, down_done, q, u + 1)
                    load(sp, q * U + (U + u), u)

        @block.tensor
        def _(pe):
            def hidden(q, u, first):
                wait_in = 48 * 1
                pe.wait_ge(w_in[u], q * wait_in + wait_in)
                if not first or u >= 2:
                    wait(pe, xT_ready, q, u - 1)
                for k in range(KD):
                    last = nc.tensor.transpose(px[:, u % 2, k * P:(k + 1) * P], xg[:, u, k * P:(k + 1) * P], t.ident[:])
                last.then_inc(xT_psum, 1)
                wait(pe, xT_ready, q, u + 1)
                if not first or u >= 2:
                    wait(pe, hid_ready, q, u - 1)
                for k in range(KD):
                    last = nc.tensor.matmul(pg[:, u % 2, 0:2 * I], xT[:, u % 2, k, :], wg[:, u, k, :], start=(k == 0), stop=(k == KD - 1))
                last.then_inc(gu_done, 1)

            def output(q, u, first):
                s = u % U
                wait(pe, hid_ready, q, u + 1)
                if not first or u >= 2:
                    wait(pe, hT_ready, q, u - 1)
                for c in range(2):
                    last = nc.tensor.transpose(ph[0:HC, s % 2, c * P:(c + 1) * P], hid[:, s % 2, c * HC:(c + 1) * HC], t.ident[:])
                last.then_inc(hT_psum, 1)
                wait(pe, hT_ready, q, u + 1)
                if not first or u >= 2:
                    wait(pe, eo_ready, q, u - 1)
                for c in range(2):
                    last = nc.tensor.matmul(pd[:, s % 2, :], hT[:, s % 2, c, :], wd[:, s, c, :], start=(c == 0), stop=(c == 1))
                last.then_inc(down_done, 1)

            for u in range(U):
                hidden(0, u, True)
                if u:
                    output(0, u - 1, True)
            with pe.Fori(1, NL) as q:
                for u in range(U):
                    hidden(q, u, False)
                    output(q, u - 1, False)
            output(NL - 1, U - 1, False)

        @block.scalar
        def _(act):
            nc.scalar.preload_act_table_set("silu_and_others")

            def step(q, u, first, body=True):
                if body:
                    wait(act, gu_done, q, u + 1)
                    if not first or u >= 2:
                        wait(act, hid_ready, q, u - 1)
                    nc.scalar.activation(sil[:, u % 2, :], pg[:, u % 2, 0:I], ACT.Silu).then_inc(silued, 1)
                if not first or u >= 1:
                    v = u - 1
                    s = v % 2
                    wait(act, down_done, q, v + 1)
                    if not first or v >= 2:
                        act.wait_ge(stored[s], q * (16 * U // 2) + 16 * (v // 2))
                    nc.scalar.activation(eo[:, s, :], pd[:, s, :], ACT.Copy).then_inc(eo_ready, 1)

            for u in range(U):
                step(0, u, True)
            with act.Fori(1, NL) as q:
                for u in range(U):
                    step(q, u, False)
            step(NL, 0, False, body=False)

        @block.gpsimd
        def _(pool):
            with pool.Fori(0, NL) as q:
                for u in range(U):
                    wait(pool, eo_ready, q, u + 1)
                    nc.gpsimd.dma_start(t.eo_dram[bass.ds((q * U + u) * CAP, CAP), :], eo[:, u % 2, :]).then_inc(stored[u % 2], 16)
            for s in range(2):
                pool.wait_ge(stored[s], 16 * E // 2)

        @block.vector
        def _(dve):
            def step(q, u, first, body=True):
                if body:
                    wait(dve, xT_psum, q, u + 1)
                    if not first or u >= 2:
                        wait(dve, gu_done, q, u - 1)
                    nc.vector.tensor_copy(xT[:, u % 2, :, :].rearrange("p k t -> p (k t)"), px[:, u % 2, :]).then_inc(xT_ready, 1)
                    wait(dve, silued, q, u + 1)
                    if not first or u >= 2:
                        wait(dve, hT_psum, q, u - 1)
                    nc.vector.tensor_tensor(hid[:, u % 2, :], sil[:, u % 2, :], pg[:, u % 2, I:2 * I], ALU.mult).then_inc(hid_ready, 1)
                if not first or u >= 1:
                    v = u - 1
                    wait(dve, hT_psum, q, v + 1)
                    if not first or v >= 2:
                        wait(dve, down_done, q, v - 1)
                    nc.vector.tensor_copy(hT[:, v % 2, :, :].rearrange("p c t -> p (c t)"), ph[0:HC, v % 2, 0:2 * P]).then_inc(hT_ready, 1)

            for u in range(U):
                step(0, u, True)
            with dve.Fori(1, NL) as q:
                for u in range(U):
                    step(q, u, False)
            step(NL, 0, False, body=False)


def combine_stage(nc, t, out):
    with ExitStack() as ctx:
        sem = ctx.enter_context(Sems(nc, "co_"))
        got = ctx.enter_context(nc.sbuf_tensor("co_got", [P, 4, K, D], F32))
        idx = ctx.enter_context(nc.sbuf_tensor("co_idx", [P, B * TT * K], U32))
        acc = ctx.enter_context(nc.sbuf_tensor("co_acc", [P, 4, D], F32))
        gathered = [sem(f"gathered{i}") for i in range(4)]
        tick, idx_ready, summed, chain = sem("tick"), sem("idx_ready"), sem("summed"), sem("chain")
        stored = [sem(f"stored{i}") for i in range(4)]
        block = ctx.enter_context(nc.Block())
        out_t = out.rearrange("b t d -> (b t) d")

        @block.gpsimd
        def _(pool):
            with pool.Fori(0, B) as b:
                pool.wait_ge(idx_ready, b * 1 + 1)
                pool.sem_inc(tick, 1)
                for tt in range(TT):
                    pool.wait_ge(summed, b * TT + tt + 1)
                    pool.sem_inc(tick, 1)
                    for k in range(K):
                        nc.gpsimd.indirect_dma_start(
                            out=got[:, tt, k, :], out_offset=None, in_=t.eo_dram,
                            in_offset=bass.IndirectOffsetOnAxis(ap=idx[:, tt * K + k:tt * K + k + 1], axis=0)).then_inc(gathered[tt], 16)

        @block.sync
        def _(sp):
            with sp.Fori(0, B) as b:
                for tt in range(TT):
                    sp.wait_ge(summed, b * TT + tt + TT + 1)
                    sp.dma_start(out_t[bass.ds((b * TT + tt) * P, P), :], acc[:, tt, :]).then_inc(stored[tt], 16)
            for tt in range(TT):
                sp.wait_ge(stored[tt], 16 * B)

        @block.vector
        def _(dve):
            dve.sem_inc(summed, TT)
            nc.vector.tensor_copy(idx[:, 0:TT * K], t.slot[:, 0, :]).then_inc(idx_ready, 1)

            def tile(b, tt, first):
                dve.wait_ge(gathered[tt], b * (16 * K) + 16 * K)
                if not first:
                    dve.wait_ge(stored[tt], b * 16)
                src = t.x1[:, bass.ds(b * TT + tt, 1), :].rearrange("p o d -> p (o d)")
                wk = t.wk[:, bass.ds(b, 1), :].rearrange("p o k -> p (o k)")
                for k in range(K):
                    last = nc.vector.scalar_tensor_tensor(acc[:, tt, :], got[:, tt, k, :], wk[:, tt * K + k:tt * K + k + 1], src,
                                                          op0=ALU.mult, op1=ALU.add)
                    src = acc[:, tt, :]
                    if k < K - 1:
                        last.then_inc(chain, 1)
                        dve.wait_ge(chain, (b * TT + tt) * (K - 1) + k + 1)
                last.then_inc(summed, 1)

            for tt in range(TT):
                tile(0, tt, True)
            with dve.Fori(1, B) as b:
                nc.vector.tensor_copy(idx[:, 0:TT * K], t.slot[:, bass.ds(b, 1), :].rearrange("p o k -> p (o k)")).then_inc(idx_ready, 1)
                for tt in range(TT):
                    tile(b, tt, False)


def constants():
    f = np.float32
    p = np.arange(P)
    freq = 1.0 / 10000.0 ** (np.arange(0, DQ, 2, dtype=f) / f(DQ))
    angle = np.outer(np.arange(T, dtype=f), freq).astype(f)
    of = (p % DQ) // 2
    swap = np.zeros((P, P), f)
    swap[p[1::2], p[0::2]] = -1.0
    swap[p[0::2], p[1::2]] = 1.0
    nf = T // 2 + 1
    filt = np.exp(-0.5 * (np.linspace(0.0, 1.0, nf) / 0.15) ** 2)
    weight = np.full(nf, 2.0)
    weight[0] = weight[-1] = 1.0
    col = (weight * filt) @ np.cos(2 * np.pi * np.arange(nf)[:, None] * np.arange(T) / T) / T
    return {
        "ident": np.eye(P, dtype=f),
        "cs": np.stack([np.cos(angle)[:, of].T, np.sin(angle)[:, of].T]).astype(f),
        "swap": swap,
        "half": np.stack([p % DH < DQ, p % DH >= DQ], 1).astype(f),
        "mask": np.where(p[None, :] > p[:, None], -1e30, 0.0).astype(f),
        "filt": col[(np.arange(T)[:, None] - np.arange(T)) % T].astype(f),
        "headones": (p[:, None] // DH == p // DH).astype(f),
        "before": (p[:, None] < p).astype(f),
        "iota": np.arange(E, dtype=f),
    }


class Held:
    pass


def program(nc, a, out):
    t = Held()
    with ExitStack() as ctx:
        def sb(stack, name, shape, dt=F32):
            return stack.enter_context(nc.sbuf_tensor(name, shape, dt))

        t.xg_dram = nc.dram_tensor("xg", (SLOTS, D), F32, kind="Internal").ap()
        t.eo_dram = nc.dram_tensor("eo", (SLOTS + 1, D), F32, kind="Internal").ap()
        t.const = a
        t.ident = sb(ctx, "ident", [P, P])
        wide = sb(ctx, "wide", [P, KD * B * T])
        t.hsT = wide[:, :].rearrange("p (k b t) -> p k b t", k=KD, b=B)
        t.x1 = wide[:, :].rearrange("p (n d) -> p n d", d=D)
        with ExitStack() as gru:
            t.h, t.bhn, t.giT = sb(gru, "h", [P, ST, 2]), sb(gru, "bhn", [P, ST]), sb(gru, "giT", [P, T, 3 * ST])
            gate_inputs_stage(nc, t, a["x"], a["L0_cond_W_ih"], a["L0_cond_b_ih"], a["L0_cond_b_hh"])
            gru_stage(nc, t, a["cond_2048"], a["L0_cond_W_hh"])
        t.A = sb(ctx, "A", [P, TT, B, D])
        t.slot, t.wk = sb(ctx, "slot", [P, B, TT * K], U32), sb(ctx, "wk", [P, B, TT * K])
        diff_attention_stage(nc, t, a["L0_attn_Wq"], a["L0_attn_Wk"], a["L0_attn_Wv"],
                             [a["L0_attn_lambda_" + n] for n in ("q1", "k1", "q2", "k2")])
        with ExitStack() as mid:
            t.xnT = sb(mid, "xnT", [P, B, KD, T])
            filter_stage(nc, t, a["x"], a["L0_attn_Wout"], a["L0_attn_rms_weight"], a["cond_2048"],
                         a["L0_cond2_W_emb"], a["L0_cond2_b_emb"], a["L0_cond2_g_norm"])
            full_attention_stage(nc, t, a["L0_cond2_W_qkv"], a["L0_cond2_g_q"], a["L0_cond2_g_k"])
        route_stage(nc, t, a["L0_cond2_W_out"], a["L0_ffn_gate_w"], a["L0_ffn_shared_gate_w"], a["L0_ffn_shared_up_w"],
                    a["L0_ffn_shared_down_w"])
        expert_stage(nc, t, a["L0_ffn_gate_up_proj"], a["L0_ffn_down_proj"])
        combine_stage(nc, t, out)


INPUTS = ["x", "cond_2048", "L0_cond_W_ih", "L0_cond_W_hh", "L0_cond_b_ih", "L0_cond_b_hh", "L0_attn_Wq", "L0_attn_Wk",
          "L0_attn_Wv", "L0_attn_Wout", "L0_attn_lambda_q1", "L0_attn_lambda_k1", "L0_attn_lambda_q2",
          "L0_attn_lambda_k2", "L0_attn_rms_weight", "L0_cond2_W_emb", "L0_cond2_b_emb", "L0_cond2_g_norm",
          "L0_cond2_W_qkv", "L0_cond2_g_q", "L0_cond2_g_k", "L0_cond2_W_out", "L0_ffn_gate_w", "L0_ffn_gate_up_proj",
          "L0_ffn_down_proj", "L0_ffn_shared_gate_w", "L0_ffn_shared_up_w", "L0_ffn_shared_down_w"]
CONSTANTS = ["ident", "cs", "swap", "half", "mask", "filt", "headones", "before", "iota"]


def kernel(**inputs):
    import concourse.bacc as bacc
    from concourse.bass_utils import run_bass_kernel_spmd

    nc = bacc.Bacc("TRN2", target_bir_lowering=False, num_devices=1)
    arrays, aps = {}, {}
    consts = constants()
    for name in INPUTS + CONSTANTS:
        a = np.ascontiguousarray(inputs[name] if name in inputs else consts[name])
        arrays["in_" + name] = a
        aps[name] = nc.dram_tensor("in_" + name, a.shape, mybir.dt.from_np(a.dtype), kind="ExternalInput").ap()
    out = nc.dram_tensor("out_0", (B, T, D), F32, kind="ExternalOutput").ap()
    program(nc, aps, out)
    r = run_bass_kernel_spmd(nc, [arrays], core_ids=[0])
    return r.results[0]["out_0"]
```

```python
import math
from contextlib import ExitStack

import numpy as np
import concourse.bass as bass
from concourse import mybir

F32 = mybir.dt.float32
BF16 = mybir.dt.bfloat16
U32 = mybir.dt.uint32
I32 = mybir.dt.int32
ALU = mybir.AluOpType
ACT = mybir.ActivationFunctionType
AX = mybir.AxisListType.X

P = 128
B, T, D = 4, 512, 512
KD = D // P
TT = T // P
NTILE = B * TT
H = 16
DH = D // H
G3 = 3 * D
GC = G3 // P
ST = KD * B
HG = P // DH
DQ = DH // 2
LAMBDA_INIT = 0.8 - 0.6 * math.exp(-0.3 * 12)
E, K, CAP = 64, 6, 128
SLOTS = E * CAP
I = 192
SI = 2 * I


class Sems:

    def __init__(self, nc, prefix):
        self.nc, self.prefix, self.held = nc, prefix, []

    def __call__(self, name):
        self.held.append(self.nc.alloc_semaphore(name=self.prefix + name))
        return self.held[-1]

    def __enter__(self):
        return self

    def __exit__(self, *failed):
        if not failed[0]:
            self.nc.clear_and_free_semaphores(self.held)
            self.nc.all_engine_barrier()


def gate_inputs_stage(nc, t, x, W_ih, b_ih, b_hh):
    with ExitStack() as ctx:
        sem = ctx.enter_context(Sems(nc, "gi_"))
        wih = ctx.enter_context(nc.sbuf_tensor("wih", [P, KD, G3], F32))
        wraw = ctx.enter_context(nc.sbuf_tensor("wraw", [P, 2, G3], F32))
        xin = ctx.enter_context(nc.sbuf_tensor("gi_xin", [P, TT, D], F32))
        xT = ctx.enter_context(nc.sbuf_tensor("gi_xT", [P, KD, T], F32))
        bias = ctx.enter_context(nc.sbuf_tensor("gi_bias", [P, 2, GC], F32))
        pt = ctx.enter_context(nc.psum_tensor("gi_pt", [P, 2, T], F32))
        pg = ctx.enter_context(nc.psum_tensor("gi_pg", [P, 4, T], F32))
        x_in, w_in, b_in = sem("x_in"), [sem("w_in0"), sem("w_in1")], sem("b_in")
        xT_psum, xT_ready = sem("xT_psum"), sem("xT_ready")
        w_spread, bias_ready = sem("w_spread"), sem("bias_ready")
        gi_psum, gi_even, gi_odd = sem("gi_psum"), sem("gi_even"), sem("gi_odd")
        block = ctx.enter_context(nc.Block())

        @block.sync
        def _(sp):
            sp.dma_start(t.ident[:], t.const["ident"]).then_inc(b_in, 16)
            for n, bvec in enumerate((b_ih, b_hh)):
                for j in range(KD):
                    for g in range(3):
                        sp.dma_start(bias[32 * j:32 * j + 32, n, g * KD:(g + 1) * KD],
                                     bvec.rearrange("(g j c i) -> g j i c", g=3, j=KD, c=KD)[g, j],
                                     allow_slow_non_contiguous=True).then_inc(b_in, 16)
            sp.dma_start(xin[:], x[0, :, :].rearrange("(tt p) d -> p tt d", p=P)).then_inc(x_in, 16)
            with sp.Fori(1, B) as b:
                sp.wait_ge(xT_psum, b * KD)
                sp.dma_start(xin[:], x[bass.ds(b, 1), :, :].rearrange("o (tt p) d -> p (o tt) d", p=P)).then_inc(x_in, 16)

        @block.gpsimd
        def _(pool):
            for k in range(KD):
                if k >= 2:
                    pool.wait_ge(w_spread, 3 * (k - 1))
                pool.dma_start(wraw[:, k % 2, :], W_ih[k * P:(k + 1) * P, :]).then_inc(w_in[k % 2], 16)

        @block.tensor
        def _(pe):
            pe.wait_ge(b_in, 16 * (1 + 6 * KD))
            with pe.Fori(0, B) as b:
                pe.wait_ge(x_in, b * 16 + 16)
                for k in range(KD):
                    if k >= 2:
                        pe.wait_ge(xT_ready, b * KD + (k - 1))
                    for tt in range(TT):
                        last = nc.tensor.transpose(pt[:, k % 2, tt * P:(tt + 1) * P], xin[:, tt, k * P:(k + 1) * P], t.ident[:])
                    last.then_inc(xT_psum, 1)
                pe.wait_ge(w_spread, 3 * KD)
                pe.wait_ge(xT_ready, b * KD + KD)
                for c in range(GC):
                    if c >= 4:
                        pe.wait_ge(gi_even if c % 2 == 0 else gi_odd, b * (GC // 2) + (c - 4) // 2 + 1)
                    for k in range(KD):
                        last = nc.tensor.matmul(pg[:, c % 4, :], wih[:, k, c * P:(c + 1) * P], xT[:, k, :],
                                                start=(k == 0), stop=(k == KD - 1))
                    last.then_inc(gi_psum, 1)
                pe.wait_ge(gi_even, b * (GC // 2) + GC // 2)
                pe.wait_ge(gi_odd, b * (GC // 2) + GC // 2)

        def evict(eng, b, c, out_sem):
            eng.wait_ge(gi_psum, b * GC + c + 1)
            dst = t.giT[:, :, bass.ds(b + c * B, 1)].rearrange("p t o -> p (t o)")
            if c % 2 == 0:
                nc.scalar.activation(dst, pg[:, c % 4, :], ACT.Identity, bias=bias[:, 0, c:c + 1]).then_inc(out_sem, 1)
            else:
                nc.vector.tensor_scalar(dst, pg[:, c % 4, :], bias[:, 0, c:c + 1], None, ALU.add).then_inc(out_sem, 1)

        @block.scalar
        def _(act):
            act.wait_ge(bias_ready, 1)
            with act.Fori(0, B) as b:
                for c in range(0, GC, 2):
                    evict(act, b, c, gi_even)

        @block.vector
        def _(dve):
            dve.wait_ge(b_in, 16 * (1 + 6 * KD))
            nc.vector.tensor_tensor(bias[:, 0, 0:2 * KD], bias[:, 0, 0:2 * KD], bias[:, 1, 0:2 * KD], ALU.add).then_inc(bias_ready, 1)
            for k in range(KD):
                dve.wait_ge(w_in[k % 2], 16 * (k // 2 + 1))
                for g in range(3):
                    nc.vector.tensor_copy(wih[:, k, g * D:(g + 1) * D].rearrange("p (c j i) -> p c j i", c=KD, j=KD),
                                          wraw[:, k % 2, g * D:(g + 1) * D].rearrange("p (j c i) -> p c j i", c=KD, j=KD)
                                          ).then_inc(w_spread, 1)
            dve.wait_ge(bias_ready, 1)
            with dve.Fori(0, B) as b:
                for k in range(KD):
                    dve.wait_ge(xT_psum, b * KD + k + 1)
                    nc.vector.tensor_copy(xT[:, k, :], pt[:, k % 2, :]).then_inc(xT_ready, 1)
                for c in range(1, GC, 2):
                    evict(dve, b, c, gi_odd)


def gru_stage(nc, t, h0, W_hh, b_hh):
    with ExitStack() as ctx:
        sem = ctx.enter_context(Sems(nc, "gru_"))

        def sb(name, shape):
            return ctx.enter_context(nc.sbuf_tensor("gru_" + name, shape, F32))

        whh = sb("whh", [P, KD, KD, 3, P])
        bias, one = sb("bias", [P, KD, P]), sb("one", [P, 2 * B])
        trz, pre = sb("trz", [P, 2 * KD, 32]), sb("pre", [P, 2 * ST])
        tn, rz, narg = sb("tn", [P, KD, 32]), sb("rz", [P, 2, KD, 32]), sb("narg", [P, KD, 32])
        d0, d1 = sb("d0", [P, ST, 4]), sb("d1", [P, ST, 4])
        hin, zeros = sb("hin", [P, KD, B]), sb("zeros", [P, 1, D])
        zero_set, cleared = sem("zero_set"), sem("cleared")
        prz = ctx.enter_context(nc.psum_tensor("gru_prz", [P, 4 * P], F32))
        pn = ctx.enter_context(nc.psum_tensor("gru_pn", [P, 4 * P], F32))
        WARM = 3
        warm = ctx.enter_context(nc.sbuf_tensor("gru_warm", [P, 4 * P], BF16))
        pw = ctx.enter_context(nc.psum_tensor("gru_pw", [P, 4 * P], F32))
        loaded_pool = sem("loaded_pool")
        loaded, h_ready, hs_kept = sem("loaded"), sem("h_ready"), sem("hs_kept")
        rz_rows, n_rows = sem("rz_rows"), sem("n_rows")
        trz_done, pre_done, rz_act = sem("trz_done"), sem("pre_done"), sem("rz_act")
        tn_done, gin_ready, side, bias_set = sem("tn_done"), sem("gin_ready"), sem("side"), sem("bias_set")
        narg_done, tanh_done = sem("narg_done"), sem("tanh_done")
        block = ctx.enter_context(nc.Block())
        state = t.h[:, :, 3]

        def cb(ap):
            return ap.rearrange("p (c b) -> p c b", b=B)

        def load(queue, cs, done):
            for jj in range(KD):
                rows = W_hh.rearrange("(jj c i) n -> jj i c n", jj=KD, c=KD)[jj]
                for c in cs:
                    for g in range(3):
                        queue.dma_start(whh[32 * jj:32 * jj + 32, c, :, g, :],
                                        rows[:, c, g * D:(g + 1) * D].rearrange("i (j f) -> i j f", j=KD)).then_inc(done, 16)

        @block.sync
        def _(sp):
            load(sp, (0, 1), loaded)
            sp.wait_ge(bias_set, 3)
            sp.dma_start(bias[0:1, :, :].rearrange("p j f -> p (j f)"), b_hh[2 * D:3 * D].unsqueeze(0)).then_inc(loaded, 16)

        LOADS_POOL = 16 * 3 * KD
        LOADS = 16 * (KD * (3 * KD + KD) + 1) - LOADS_POOL

        @block.gpsimd
        def _(pool):
            load(pool, (3,), loaded_pool)
            nc.gpsimd.memset(zeros[:], 0.0).then_inc(zero_set, 1)
            pool.wait_ge(zero_set, 1)
            pool.wait_ge(h_ready, 1)
            R = 16
            xg = t.xg_dram.rearrange("(n r p) d -> n p r d", r=R, p=P)
            for n in range(SLOTS // (R * P)):
                pool.dma_start(xg[n], zeros[:].broadcast_to([P, R, D])).then_inc(cleared, 16)
            pool.dma_start(t.eo_dram[SLOTS:SLOTS + 1, :], zeros[0:1, 0, :]).then_inc(cleared, 16)
            pool.wait_ge(cleared, 16 * (SLOTS // (R * P) + 1))

        @block.tensor
        def _(pe):
            pe.wait_ge(loaded, LOADS)
            pe.wait_ge(loaded_pool, LOADS_POOL)

            def add_bias():
                for j in range(KD):
                    nc.tensor.matmul(pn[32 * j:32 * j + 2 * B, 0:P], one[:], bias[:, j, :], start=True, stop=False)

            def step(s):
                pe.wait_ge(h_ready, s * 1 + 1)
                for rows, g0, g1, done in ((prz, 0, 2, rz_rows), (pn, 2, 3, n_rows)):
                    for c in range(KD):
                        for j in range(KD):
                            last = nc.tensor.matmul(rows[32 * j:32 * j + 2 * B, 0:(g1 - g0) * P],
                                                    t.h[:, c * B:(c + 1) * B, 1:4:2].rearrange("p b o -> p (b o)"),
                                                    whh[:, c, j, g0:g1, :].rearrange("p g f -> p (g f)"),
                                                    start=(c == 0 and g0 == 0), stop=(c == KD - 1))
                    last.then_inc(done, 1)

            pe.wait_ge(h_ready, 1)
            add_bias()
            with pe.Fori(0, T - 1) as s:
                step(s)
                for _ in range(WARM):
                    nc.tensor.matmul(pw[:, :], warm[:, 0:P], warm[:, :], start=True, stop=True)
                pe.wait_ge(tn_done, s * 1 + 1)
                add_bias()
            step(T - 1)

        @block.scalar
        def _(act):
            for jj in range(KD):
                for c in range(KD):
                    act.dma_start(hin[32 * jj:32 * jj + 32, c, :],
                                  h0[:, jj * P + 32 * c:jj * P + 32 * c + 32].rearrange("b i -> i b"),
                                  allow_slow_non_contiguous=True).then_inc(loaded, 16)
            load(act, (2,), loaded)
            nc.scalar.preload_act_table_set("sigmoid_and_others")
            act.wait_ge(side, 4)
            with act.Fori(0, T) as s:
                gi = t.giT[:, bass.ds(s, 1), :].rearrange("p o c -> p (o c)")
                nc.scalar.activation(rz[:, 0, :, 1:2 * B:2], cb(gi[:, 2 * ST:3 * ST]), ACT.Copy).then_inc(gin_ready, 1)
                act.wait_ge(pre_done, s * 1 + 1)
                nc.scalar.activation(rz[:, :, :, 0:2 * B:2].rearrange("p g c b -> p (g c) b"), cb(pre[:]), ACT.Sigmoid).then_inc(rz_act, 1)
                act.wait_ge(narg_done, s * 1 + 1)
                nc.scalar.activation(cb(d1[:, :, 2]), narg[:, :, 1:2 * B:2], ACT.Tanh).then_inc(tanh_done, 1)

        @block.vector
        def _(dve):
            nc.vector.memset(bias[:], 0.0).then_inc(bias_set, 1)
            nc.vector.memset(one[:], 0.0).then_inc(bias_set, 1)
            dve.wait_ge(bias_set, 2)
            nc.vector.memset(one[0:1, 1:2 * B:2], 1.0).then_inc(bias_set, 1)
            nc.vector.memset(warm[:], 0.0)
            nc.vector.memset(prz[:], 0.0)
            nc.vector.memset(pn[:], 0.0)
            nc.vector.memset(t.h[:], 0.0).then_inc(side, 1)
            nc.vector.memset(d0[:], 0.0).then_inc(side, 1)
            nc.vector.memset(rz[:], 0.0).then_inc(side, 1)
            nc.vector.memset(d1[:], 0.0).then_inc(side, 1)
            dve.wait_ge(side, 4)
            dve.wait_ge(loaded, LOADS)
            dve.wait_ge(loaded_pool, LOADS_POOL)
            nc.vector.tensor_copy(state, hin[:].rearrange("p c b -> p (c b)")).then_inc(h_ready, 1)
            with dve.Fori(0, T) as s:
                gi = t.giT[:, bass.ds(s, 1), :].rearrange("p o c -> p (o c)")
                dve.wait_ge(rz_rows, s * 1 + 1)
                nc.vector.transpose(trz[:].rearrange("p c x -> p (c x)"), prz[:, 0:2 * P]).then_inc(trz_done, 1)
                dve.wait_ge(trz_done, s * 1 + 1)
                nc.vector.tensor_tensor(cb(pre[:]), trz[:, :, 1:2 * B:2], cb(gi[:, 0:2 * ST]), ALU.add).then_inc(pre_done, 1)
                dve.wait_ge(n_rows, s * 1 + 1)
                nc.vector.transpose(tn[:].rearrange("p c x -> p (c x)"), pn[:, 0:P]).then_inc(tn_done, 1)
                dve.wait_ge(rz_act, s * 1 + 1)
                dve.wait_ge(gin_ready, s * 1 + 1)
                dve.wait_ge(tn_done, s * 1 + 1)
                nc.vector.tensor_tensor_scan(narg[:].rearrange("p c x -> p (c x)"), tn[:].rearrange("p c x -> p (c x)"),
                                             rz[:, 0, :, :].rearrange("p c x -> p (c x)"), 0.0, ALU.mult, ALU.add).then_inc(narg_done, 1)
                z = rz[:, 1, :, 0:2 * B:2]
                nc.vector.tensor_scalar(cb(d0[:, :, 3]), z, -1.0, 1.0, ALU.mult, ALU.add).then_inc(side, 1)
                nc.vector.tensor_tensor(cb(d1[:, :, 3]), z, cb(state), ALU.mult).then_inc(side, 1)
                dve.wait_ge(side, s * 2 + 6)
                dve.wait_ge(tanh_done, s * 1 + 1)
                nc.vector.tensor_tensor_scan(t.h[:].rearrange("p c o -> p (c o)"), d0[:].rearrange("p c o -> p (c o)"),
                                             d1[:].rearrange("p c o -> p (c o)"), 0.0, ALU.mult, ALU.add).then_inc(h_ready, 1)
                dve.wait_ge(h_ready, s * 1 + 2)
                nc.vector.tensor_copy(t.hsT[:, :, :, bass.ds(s, 1)].rearrange("p k b o -> p (k b o)"), state).then_inc(hs_kept, 1)
            dve.wait_ge(hs_kept, T)


class AttentionCore:

    def __init__(self, nc, ctx, sem, prefix, NA, scale, causal):
        self.nc, self.NA, self.scale, self.causal = nc, NA, scale, causal

        def sb(name, shape, dt=F32):
            return ctx.enter_context(nc.sbuf_tensor(prefix + name, shape, dt))

        self.probT = sb("probT", [P, 2, HG, T])
        self.mx, self.spread = sb("mx", [P, TT, NA, HG]), sb("spread", [P, TT, NA, HG, DH])
        self.qp, self.kp = sb("qp", [P, HG, T]), sb("kp", [P, NA, HG, T])
        self.ones, self.rec = sb("ones", [P, P]), sb("rec", [P, NA, T])
        self.err = sb("err", [P, NA, T])
        self.ps = ctx.enter_context(nc.psum_tensor(prefix + "ps", [P, 8, T], F32))
        self.core_set, self.scored, self.max_done, self.spread_done = (sem(n) for n in ("core_set", "scored", "max_done", "spread_done"))
        self.max_cols, self.negm_act, self.negm_dve = sem("max_cols"), sem("negm_act"), sem("negm_dve")
        self.keys_scored, self.exp_done, self.refined, self.banks_free = (sem(n) for n in ("keys_scored", "exp_done", "refined", "banks_free"))
        self.product, self.ln_done, self.rec_done, self.cleared = sem("product"), sem("ln_done_core"), sem("rec_done"), sem("cleared")
        self.SET = 4 + NA * HG
        self.groups = [(i, a) for i in range(TT) for a in range(NA)]
        self.rows = [(h, a) for h in range(HG) for a in range(NA)]
        self.queries = [(i, a) for i in reversed(range(TT)) for a in range(NA)]

    def slot_of(self, h, a):
        return (h + 1 + a) % HG

    def setup(self, dve):
        nc = self.nc
        nc.vector.memset(self.ones[:], 1.0).then_inc(self.core_set, 1)
        nc.vector.memset(self.spread[:], 0.0).then_inc(self.core_set, 1)
        nc.vector.memset(self.kp[:], 0.0).then_inc(self.core_set, 1)
        nc.vector.memset(self.qp[:], 0.0).then_inc(self.core_set, 1)
        dve.wait_ge(self.core_set, 4)
        for a in range(self.NA):
            for h in range(HG):
                r = DH * self.slot_of(h, a)
                nc.vector.memset(self.kp[r:r + 1, a, h, :], 1.0).then_inc(self.core_set, 1)
        dve.wait_ge(self.core_set, self.SET)
        dve.sem_inc(self.cleared, 1)

    def tensor(self, pe, it, v, ident, identb, mask, maskT):
        nc, NA, NG = self.nc, self.NA, len(self.groups)
        slots = [slice(DH * h, DH * h + DH) for h in range(HG)]
        pe.wait_ge(self.cleared, it * (HG * NA) + 1)
        for m, (i, a) in enumerate(self.queries):
            L = (i + 1) * P if self.causal else T
            bank = 4 * (m % 2)
            if m == 1:
                pe.wait_ge(self.banks_free, it * 1 + 1)
            if m >= 2:
                pe.wait_ge(self.max_done, it * NG + m - 1)
            for h, sl in enumerate(slots):
                last = nc.tensor.matmul(self.ps[:, bank + self.slot_of(h, a), 0:L], self.qp[:, h, i * P:(i + 1) * P],
                                        self.kp[:, a, h, 0:L], start=True, stop=not self.causal)
            if self.causal:
                for h in range(HG):
                    last = nc.tensor.matmul(self.ps[:, bank + h, i * P:L], identb, mask, start=False, stop=True)
            last.then_inc(self.scored, 1)
        pe.wait_ge(self.spread_done, it * 1 + 1)
        for a in range(NA):
            for i in range(TT):
                last = nc.tensor.transpose(self.ps[:, 6 + a, i * P:(i + 1) * P],
                                           self.spread[:, i, a, :, :].rearrange("p h d -> p (h d)"), ident)
        last.then_inc(self.max_cols, 1)
        for n in range(NG + 1):
            if n < NG:
                kt, a = self.groups[n]
                q0 = kt * P if self.causal else 0
                if n:
                    pe.wait_ge(self.exp_done, it * NG + n)
                for h in range(HG):
                    if n == 0:
                        pe.wait_ge(self.negm_act, it * (HG * NA // 2) + ((h + 1) * NA + 1) // 2)
                        if (h + 1) * NA // 2:
                            pe.wait_ge(self.negm_dve, it * (HG * NA // 2) + (h + 1) * NA // 2)
                    last = nc.tensor.matmul(self.ps[:, h, q0:T], self.kp[:, a, h, kt * P:(kt + 1) * P], self.qp[:, h, q0:T],
                                            start=True, stop=not self.causal)
                if self.causal:
                    for h in range(HG):
                        last = nc.tensor.matmul(self.ps[:, h, q0:q0 + P], identb, maskT, start=False, stop=True)
                last.then_inc(self.keys_scored, 1)
            if n:
                kt, a = self.groups[n - 1]
                q0 = kt * P if self.causal else 0
                pe.wait_ge(self.exp_done, it * NG + n)
                for bank, values in ((4 + a, v), (6 + a, None)):
                    for h, sl in enumerate(slots):
                        lhsT = self.ones[:, 0:DH] if values is None else v[:, kt, sl]
                        last = nc.tensor.matmul(self.ps[sl, bank, q0:T], lhsT, self.probT[:, (n - 1) % 2, h, q0:T],
                                                start=(kt == 0), stop=(kt == TT - 1))
                last.then_inc(self.product, 1)

    def scalar(self, act, it):
        nc, NG = self.nc, len(self.groups)
        act.wait_ge(self.max_cols, it * 1 + 1)
        for h, a in self.rows[0::2]:
            r = DH * self.slot_of(h, a)
            nc.scalar.activation(self.qp[r:r + 1, h, :], self.ps[r:r + 1, 6 + a, :], ACT.Copy).then_inc(self.negm_act, 1)
        for n, (kt, a) in enumerate(self.groups):
            q0 = kt * P if self.causal else 0
            act.wait_ge(self.keys_scored, it * NG + n + 1)
            if n >= 2:
                act.wait_ge(self.product, it * NG + n - 1)
            nc.scalar.activation(self.probT[:, n % 2, :, q0:T], self.ps[:, 0:HG, q0:T], ACT.Exp, scale=self.scale).then_inc(self.exp_done, 1)
        act.wait_ge(self.product, it * NG + NG)
        nc.scalar.activation(self.rec[:], self.ps[:, 6:6 + self.NA, :], ACT.Ln).then_inc(self.ln_done, 1)
        act.wait_ge(self.ln_done, it * 1 + 1)
        nc.scalar.activation(self.rec[:], self.rec[:], ACT.Exp, scale=-1.0).then_inc(self.rec_done, 1)

    def vector(self, dve, it):
        nc, NG = self.nc, len(self.groups)
        for m, (i, a) in enumerate(self.queries):
            L = (i + 1) * P if self.causal else T
            bank = 4 * (m % 2)
            dve.wait_ge(self.scored, it * NG + m + 1)
            nc.vector.tensor_reduce(self.mx[:, i, a, :], self.ps[:, bank:bank + HG, 0:L], AX, ALU.max).then_inc(self.max_done, 1)
        dve.wait_ge(self.max_done, it * NG + NG)
        nc.vector.tensor_scalar(self.spread[:, :, :, :, 0].rearrange("p i a h -> p (i a h)"),
                                self.mx[:].rearrange("p i a h -> p (i a h)"), -1.0, None, ALU.mult).then_inc(self.spread_done, 1)
        dve.wait_ge(self.max_cols, it * 1 + 1)
        for h, a in self.rows[1::2]:
            r = DH * self.slot_of(h, a)
            nc.vector.tensor_copy(self.qp[r:r + 1, h, :], self.ps[r:r + 1, 6 + a, :]).then_inc(self.negm_dve, 1)
        dve.wait_ge(self.keys_scored, it * NG + NG)
        for a in range(self.NA):
            for h in range(HG):
                r = DH * self.slot_of(h, a)
                nc.vector.memset(self.qp[r:r + 1, h, :], 0.0).then_inc(self.cleared, 1)
        dve.wait_ge(self.rec_done, it * 1 + 1)
        nc.vector.tensor_tensor(self.err[:], self.ps[:, 6:6 + self.NA, :], self.rec[:], ALU.mult).then_inc(self.refined, 1)
        dve.wait_ge(self.refined, it * 2 + 1)
        nc.vector.scalar_tensor_tensor(self.rec[:], self.err[:], -2.0, self.rec[:], op0=ALU.add, op1=ALU.mult).then_inc(self.refined, 1)
        dve.wait_ge(self.refined, it * 2 + 2)


def diff_attention_stage(nc, t, Wq, Wk, Wv, lambdas):
    with ExitStack() as ctx:
        sem = ctx.enter_context(Sems(nc, "da_"))

        def sb(name, shape, dt=F32):
            return ctx.enter_context(nc.sbuf_tensor("da_" + name, shape, dt))

        w = sb("w", [P, 3, KD, D])
        wg = sb("wg", [P, 3, KD, P])
        hb = sb("hb", [P, KD, T])
        cs = sb("cs", [P, 2, T])
        swap, half = sb("swap", [P, P]), sb("half", [P, 2])
        qk, rot, sw, cc = sb("qk", [P, 2, T]), sb("rot", [P, T]), sb("sw", [P, 2, T]), sb("cc", [P, 2, T])
        v = sb("v", [P, TT, P])
        identb, maskb = sb("identb", [P, P], BF16), sb("maskb", [P, P], BF16)
        maskf = sb("maskf", [P, 2, P])
        lam = sb("lam", [P, 4, DQ])
        lp, ls, le, nlam = sb("lp", [P, 2, DQ]), sb("ls", [P, 2]), sb("le", [P, 2]), sb("nlam", [P, 2])
        o1, o2, aT, maskTb = sb("o1", [P, T]), sb("o2", [P, T]), sb("aT", [P, T]), sb("maskTb", [P, P], BF16)
        core = AttentionCore(nc, ctx, sem, "da_", 2, float(DQ) ** -0.5, True)
        w_in, const_in, hb_in, w_free = sem("w_in"), sem("const_in"), sem("hb_in"), sem("w_free")
        const_ready, lstep = sem("const_ready"), sem("lstep")
        projected, v_done, raw, v_ready = sem("projected"), sem("v_done"), sem("raw"), sem("v_ready")
        swapped, cosed, sined, rotated, keys_ready, keys2_ready = (sem(n) for n in (
            "swapped", "cosed", "sined", "rotated", "keys_ready", "keys2_ready"))
        scaled, aT_ready, a_psum, a_written = sem("scaled"), sem("aT_ready"), sem("a_psum"), core.banks_free
        block = ctx.enter_context(nc.Block())
        N_W, N_C = 16 * 3 * KD, 16 * (1 + 1 + 1 + 1 + 4)
        NIT, NG = B * KD, len(core.groups)

        @block.sync
        def _(sp):
            for n, W in enumerate((Wq, Wk, Wv)):
                for jj in range(KD):
                    sp.dma_start(w[32 * jj:32 * jj + 32, n, :, :],
                                 W.rearrange("(jj c i) n -> jj i c n", jj=KD, c=KD)[jj]).then_inc(w_in, 16)
            sp.dma_start(cs[:], t.const["cs"].rearrange("a p t -> p a t")).then_inc(const_in, 16)
            sp.dma_start(swap[:], t.const["swap"]).then_inc(const_in, 16)
            sp.dma_start(half[:], t.const["half"]).then_inc(const_in, 16)
            sp.dma_start(maskf[:], t.const["mask"].rearrange("a p c -> p a c")).then_inc(const_in, 16)
            for n, l in enumerate(lambdas):
                sp.dma_start(lam[:, n, :], l.unsqueeze(0).broadcast_to([P, DQ])).then_inc(const_in, 16)
            sp.wait_ge(w_in, N_W)

            with sp.Fori(0, B) as b:
                with sp.Fori(0, KD) as g:
                    sp.wait_ge(w_free, b * KD + g + 1)
                    sp.dma_start(hb[:], t.hsT[:, :, bass.ds(b, 1), :].rearrange("p k o t -> p (k o) t")).then_inc(hb_in, 16)
                    for n in range(3):
                        sp.dma_start(wg[:, n, :, :], w[:, n, :, bass.ds(g * P, P)]).then_inc(hb_in, 16)

        @block.gpsimd
        def _(pool):
            pool.wait_ge(const_in, N_C)
            with pool.Fori(0, NIT) as it:
                for n in (1, 0):
                    pool.wait_ge(raw, it * 2 + (2 - n))
                    nc.gpsimd.tensor_tensor(cc[:, n, :], qk[:, n, :], cs[:, 0, :], ALU.mult).then_inc(cosed, 1)

        @block.tensor
        def _(pe):
            pe.wait_ge(w_in, N_W)
            pe.wait_ge(const_ready, 3)
            pe.wait_ge(core.core_set, core.SET)

            def project(it):
                pe.wait_ge(hb_in, it * 64 + 64)
                for n in (1, 0):
                    for k in range(KD):
                        last = nc.tensor.matmul(core.ps[:, n, :], wg[:, n, k, :], hb[:, k, :], start=(k == 0), stop=(k == KD - 1))
                    last.then_inc(projected, 1)
                for n in (1, 0):
                    pe.wait_ge(raw, it * 2 + (2 - n))
                    nc.tensor.matmul(core.ps[:, 3 - n, :], swap[:], qk[:, n, :], start=True, stop=True).then_inc(swapped, 1)
                for tt in range(TT):
                    for k in range(KD):
                        last = nc.tensor.matmul(core.ps[:, 1, tt * P:(tt + 1) * P], hb[:, k, tt * P:(tt + 1) * P],
                                                wg[:, 2, k, :], start=(k == 0), stop=(k == KD - 1))
                last.then_inc(v_done, 1)

            def attend(it):
                pe.wait_ge(rotated, it * (HG + 1) + HG + 1)
                pe.wait_ge(keys_ready, it * HG + HG)
                pe.wait_ge(keys2_ready, it * HG + HG)
                pe.wait_ge(v_ready, it * 1 + 1)
                core.tensor(pe, it, v, t.ident[:], identb[:], maskb[:], maskTb[:])

            def output(it):
                pe.wait_ge(aT_ready, it * 1 + 1)
                for i in range(TT):
                    last = nc.tensor.transpose(core.ps[:, 4, i * P:(i + 1) * P], aT[:, i * P:(i + 1) * P], t.ident[:])
                last.then_inc(a_psum, 1)

            project(0)
            with pe.Fori(0, NIT - 1) as it:
                attend(it)
                pe.wait_ge(core.exp_done, it * NG + NG)
                project(it + 1)
                output(it)
            attend(NIT - 1)
            output(NIT - 1)

        @block.scalar
        def _(act):
            nc.scalar.preload_act_table_set("natural_log_exp_and_others")
            act.wait_ge(lstep, 2)
            nc.scalar.activation(le[:], ls[:], ACT.Exp).then_inc(lstep, 1)

            def project(it):
                for n in (1, 0):
                    act.wait_ge(projected, it * 2 + (2 - n))
                    nc.scalar.activation(qk[:, n, :], core.ps[:, n, :], ACT.Copy).then_inc(raw, 1)

            def second_keys(it):
                act.wait_ge(rotated, it * (HG + 1) + 1)
                for h in range(HG):
                    sl = slice(DH * h, DH * h + DH)
                    nc.scalar.activation(core.kp[sl, 1, h, :], rot[sl, :], ACT.Copy, scale=half[sl, 1:2]).then_inc(keys2_ready, 1)
                act.wait_ge(v_done, it * 1 + 1)
                nc.scalar.activation(v[:].rearrange("p t d -> p (t d)"), core.ps[:, 1, :], ACT.Copy).then_inc(v_ready, 1)
                act.wait_ge(v_ready, it * 1 + 1)
                act.sem_inc(w_free, 1)

            def output(it):
                act.wait_ge(a_psum, it * 1 + 1)
                nc.scalar.activation(t.A[:].rearrange("p i b f -> p i (b f)")[:, :, bass.ds(it * P, P)],
                                     core.ps[:, 4, :].rearrange("p (i f) -> p i f", f=P), ACT.Copy).then_inc(a_written, 1)

            project(0)
            second_keys(0)
            with act.Fori(0, NIT - 1) as it:
                core.scalar(act, it)
                project(it + 1)
                second_keys(it + 1)
                output(it)
            core.scalar(act, NIT - 1)
            output(NIT - 1)

        @block.vector
        def _(dve):
            dve.sem_inc(w_free, 1)
            dve.sem_inc(a_written, 1)
            core.setup(dve)
            dve.wait_ge(const_in, N_C)
            nc.vector.tensor_copy(maskb[:], maskf[:, 0, :]).then_inc(const_ready, 1)
            nc.vector.tensor_copy(maskTb[:], maskf[:, 1, :]).then_inc(const_ready, 1)
            nc.vector.tensor_copy(identb[:], t.ident[:]).then_inc(const_ready, 1)
            nc.vector.tensor_tensor(lp[:], lam[:, 0:4:2, :], lam[:, 1:4:2, :], ALU.mult).then_inc(lstep, 1)
            dve.wait_ge(lstep, 1)
            nc.vector.tensor_reduce(ls[:], lp[:], AX, ALU.add).then_inc(lstep, 1)
            dve.wait_ge(lstep, 3)
            nc.vector.tensor_tensor(nlam[:, 0:1], le[:, 1:2], le[:, 0:1], ALU.subtract).then_inc(lstep, 1)
            dve.wait_ge(lstep, 4)
            nc.vector.tensor_scalar(nlam[:, 1:2], nlam[:, 0:1], -LAMBDA_INIT, None, ALU.add).then_inc(lstep, 1)
            dve.wait_ge(lstep, 5)

            def project(it):
                for n in (1, 0):
                    dve.wait_ge(swapped, it * 2 + (2 - n))
                    nc.vector.tensor_tensor(sw[:, n, :], core.ps[:, 3 - n, :], cs[:, 1, :], ALU.mult).then_inc(sined, 1)
                    dve.wait_ge(sined, it * 2 + (2 - n))
                    dve.wait_ge(cosed, it * 2 + (2 - n))
                    if n == 0:
                        for h in range(HG):
                            sl = slice(DH * h, DH * h + DH)
                            nc.vector.tensor_tensor(core.qp[sl, h, :], sw[sl, n, :], cc[sl, n, :], ALU.add).then_inc(rotated, 1)
                    else:
                        nc.vector.tensor_tensor(rot[:], sw[:, n, :], cc[:, n, :], ALU.add).then_inc(rotated, 1)
                        dve.wait_ge(rotated, it * (HG + 1) + 1)
                        for h in range(HG):
                            sl = slice(DH * h, DH * h + DH)
                            nc.vector.tensor_scalar(core.kp[sl, 0, h, :], rot[sl, :], half[sl, 0:1], None, ALU.mult).then_inc(keys_ready, 1)

            def attend(it):
                core.vector(dve, it)
                for n, o in enumerate((o1, o2)):
                    nc.vector.scalar_tensor_tensor(o[:], core.ps[:, 4 + n, :], -1.0, core.rec[:, n, :],
                                                   op0=ALU.mult, op1=ALU.mult).then_inc(scaled, 1)
                dve.wait_ge(scaled, it * 2 + 2)
                nc.vector.scalar_tensor_tensor(aT[:], o2[:], nlam[:, 1:2], o1[:], op0=ALU.mult, op1=ALU.add).then_inc(aT_ready, 1)

            project(0)
            with dve.Fori(0, NIT - 1) as it:
                attend(it)
                project(it + 1)
            attend(NIT - 1)


def filter_stage(nc, t, x, Wout, rms_weight, cond, W_emb, b_emb, g_norm):
    with ExitStack() as ctx:
        sem = ctx.enter_context(Sems(nc, "fi_"))

        def sb(name, shape, dt=F32):
            return ctx.enter_context(nc.sbuf_tensor("fi_" + name, shape, dt))

        filt, wout, wemb = sb("filt", [P, TT, T]), sb("wout", [P, KD, D]), sb("wemb", [P, KD, 2 * D])
        rmsw, condT, bg = sb("rmsw", [P, 1, D]), sb("condT", [P, KD, B]), sb("bg", [P, 3, KD])
        gs1, gain, shift = sb("gs1", [P, KD, B]), sb("gain", [P, KD, B]), sb("shift", [P, KD, B])
        xb = sb("xb", [P, TT, D])
        sq, y, yT = sb("sq", [P, TT, D]), sb("y", [P, TT, D]), sb("yT", [P, KD, T])
        ss, rs = sb("ss", [P, TT * H]), sb("rs", [P, TT * H])
        s2, r2 = sb("s2", [P, TT]), sb("r2", [P, TT])
        gain_b, shift_b = sb("gain_b", [P, KD]), sb("shift_b", [P, KD])
        pf = ctx.enter_context(nc.psum_tensor("fi_pf", [P, 4, 512], F32))
        pt = ctx.enter_context(nc.psum_tensor("fi_pt", [P, 4, 512], F32))
        const_in, x_in = sem("const_in"), sem("x_in")
        emb_done, gain_step, gain_ready = sem("emb_done"), sem("gain_step"), sem("gain_ready")
        filtered, squared, ss_done, ms_done, ln_done, rs_done = (sem(n) for n in (
            "filtered", "squared", "ss_done", "ms_done", "ln_done", "rs_done"))
        y1_done, y_ready, yT_psum, yT_act, yT_dve = (sem(n) for n in ("y1_done", "y_ready", "yT_psum", "yT_act", "yT_dve"))
        out_done, x1_ready, sq2, ms2, ln2, rs2 = (sem(n) for n in ("out_done", "x1_ready", "sq2", "ms2", "ln2", "rs2"))
        normed, nT_psum, nT_act, nT_dve = sem("normed"), sem("nT_psum"), sem("nT_act"), sem("nT_dve")
        block = ctx.enter_context(nc.Block())
        N_C = 16 * (4 + KD + 3)

        @block.sync
        def _(sp):
            sp.dma_start(filt[:], t.const["filt"].rearrange("(s p) t -> p s t", p=P)).then_inc(const_in, 16)
            sp.dma_start(wout[:], Wout.rearrange("(k p) n -> p k n", p=P)).then_inc(const_in, 16)
            sp.dma_start(wemb[:], W_emb.rearrange("(k p) n -> p k n", p=P)).then_inc(const_in, 16)
            rms_row = rms_weight.rearrange("(a h d) -> a h d", a=1, h=1)
            sp.dma_start(rmsw[:].rearrange("p o (h d) -> p (o h) d", h=H), rms_row.broadcast_to([P, H, DH])).then_inc(const_in, 16)
            for k in range(KD):
                sp.dma_start(condT[:, k, :], cond[:, k * P:(k + 1) * P].rearrange("b p -> p b"),
                             allow_slow_non_contiguous=True).then_inc(const_in, 16)
            for n, vec in enumerate((b_emb[0:D], b_emb[D:2 * D], g_norm)):
                sp.dma_start(bg[:, n, :], vec.rearrange("(k p) -> p k", p=P), allow_slow_non_contiguous=True).then_inc(const_in, 16)
            sp.dma_start(xb[:], x[0].rearrange("(tt p) d -> p tt d", p=P)).then_inc(x_in, 16)
            with sp.Fori(1, B) as b:
                sp.wait_ge(x1_ready, b * TT)
                sp.dma_start(xb[:], x[bass.ds(b, 1), :, :].rearrange("o (tt p) d -> p (o tt) d", p=P)).then_inc(x_in, 16)

        @block.tensor
        def _(pe):
            pe.wait_ge(const_in, N_C)
            for c in range(2 * KD):
                for k in range(KD):
                    last = nc.tensor.matmul(pf[:, 0, c * B:(c + 1) * B], wemb[:, k, c * P:(c + 1) * P], condT[:, k, :],
                                            start=(k == 0), stop=(k == KD - 1))
            last.then_inc(emb_done, 1)
            pe.wait_ge(gain_ready, 3)
            with pe.Fori(0, B) as b:
                for tt in range(TT):
                    for s in range(TT):
                        last = nc.tensor.matmul(pf[:, tt, :], filt[:, s, tt * P:(tt + 1) * P],
                                                t.A[:, s, bass.ds(b, 1), :].rearrange("p o f -> p (o f)"),
                                                start=(s == 0), stop=(s == TT - 1))
                last.then_inc(filtered, 1)
                pe.wait_ge(y_ready, b * 1 + 1)
                for k in range(KD):
                    for tt in range(TT):
                        last = nc.tensor.transpose(pt[:, k, tt * P:(tt + 1) * P], y[:, tt, k * P:(k + 1) * P], t.ident[:])
                    last.then_inc(yT_psum, 1)
                pe.wait_ge(yT_act, b * 2 + 2)
                pe.wait_ge(yT_dve, b * 2 + 2)
                for tt in range(TT):
                    for k in range(KD):
                        last = nc.tensor.matmul(pf[:, tt, :], yT[:, k, tt * P:(tt + 1) * P], wout[:, k, :],
                                                start=(k == 0), stop=(k == KD - 1))
                    last.then_inc(out_done, 1)
                pe.wait_ge(normed, b * TT + TT)
                for k in range(KD):
                    for tt in range(TT):
                        last = nc.tensor.transpose(pt[:, k, tt * P:(tt + 1) * P], y[:, tt, k * P:(k + 1) * P], t.ident[:])
                    last.then_inc(nT_psum, 1)
                pe.wait_ge(nT_act, b * 2 + 2)
                pe.wait_ge(nT_dve, b * 2 + 2)

        @block.scalar
        def _(act):
            nc.scalar.preload_act_table_set("natural_log_exp_and_others")
            act.wait_ge(gain_ready, 3)
            with act.Fori(0, B) as b:
                act.wait_ge(filtered, b * 1 + 1)
                nc.scalar.activation(sq[:], pf[:], ACT.Square).then_inc(squared, 1)
                act.wait_ge(ms_done, b * 1 + 1)
                nc.scalar.activation(rs[:], ss[:], ACT.Ln).then_inc(ln_done, 1)
                act.wait_ge(ln_done, b * 1 + 1)
                nc.scalar.activation(rs[:], rs[:], ACT.Exp, scale=-0.5).then_inc(rs_done, 1)
                for k in (0, 2):
                    act.wait_ge(yT_psum, b * KD + k + 1)
                    nc.scalar.activation(yT[:, k, :], pt[:, k, :], ACT.Copy).then_inc(yT_act, 1)
                for tt in range(TT):
                    act.wait_ge(x1_ready, b * TT + tt + 1)
                    nc.scalar.activation(sq[:, tt, :], t.x1[:, bass.ds(b * TT + tt, 1), :].rearrange("p o d -> p (o d)"),
                                         ACT.Square, accum_out=s2[:, tt:tt + 1]).then_inc(sq2, 1)
                act.wait_ge(ms2, b * 1 + 1)
                nc.scalar.activation(r2[:], s2[:], ACT.Ln).then_inc(ln2, 1)
                act.wait_ge(ln2, b * 1 + 1)
                nc.scalar.activation(r2[:], r2[:], ACT.Exp, scale=-0.5).then_inc(rs2, 1)
                for k in (0, 2):
                    act.wait_ge(nT_psum, b * KD + k + 1)
                    nc.scalar.activation(t.xnT[:, bass.ds(b, 1), k, :].rearrange("p o t -> p (o t)"), pt[:, k, :], ACT.Identity,
                                         bias=shift_b[:, k:k + 1], scale=gain_b[:, k:k + 1]).then_inc(nT_act, 1)

        @block.vector
        def _(dve):
            dve.wait_ge(emb_done, 1)
            sc = pf[:, 0, 0:KD * B].rearrange("p (k b) -> p k b", b=B)
            sh = pf[:, 0, KD * B:2 * KD * B].rearrange("p (k b) -> p k b", b=B)
            nc.vector.tensor_tensor(gs1[:], sc, bg[:, 0, :].unsqueeze(2).broadcast_to([P, KD, B]), ALU.add).then_inc(gain_step, 1)
            nc.vector.tensor_tensor(shift[:], sh, bg[:, 1, :].unsqueeze(2).broadcast_to([P, KD, B]), ALU.add).then_inc(gain_ready, 1)
            dve.wait_ge(gain_step, 1)
            nc.vector.scalar_tensor_tensor(gain[:], gs1[:], 1.0, bg[:, 2, :].unsqueeze(2).broadcast_to([P, KD, B]),
                                           op0=ALU.add, op1=ALU.mult).then_inc(gain_ready, 1)
            nc.vector.tensor_scalar(rmsw[:], rmsw[:], 1.0 - LAMBDA_INIT, None, ALU.mult).then_inc(gain_ready, 1)
            dve.wait_ge(gain_ready, 3)
            heads = "p tt (h d) -> p (tt h) d"
            with dve.Fori(0, B) as b:
                dve.wait_ge(squared, b * 1 + 1)
                nc.vector.tensor_reduce(ss[:], sq[:].rearrange(heads, h=H), AX, ALU.add).then_inc(ss_done, 1)
                dve.wait_ge(ss_done, b * 1 + 1)
                nc.vector.tensor_scalar(ss[:], ss[:], 1.0 / DH, 1e-5, ALU.mult, ALU.add).then_inc(ms_done, 1)
                dve.wait_ge(rs_done, b * 1 + 1)
                nc.vector.tensor_tensor(y[:].rearrange(heads, h=H), pf[:].rearrange(heads, h=H),
                                        rs[:].unsqueeze(2).broadcast_to([P, TT * H, DH]), ALU.mult).then_inc(y1_done, 1)
                dve.wait_ge(y1_done, b * 1 + 1)
                nc.vector.tensor_tensor(y[:], y[:], rmsw[:].broadcast_to([P, TT, D]), ALU.mult).then_inc(y_ready, 1)
                for k in (1, 3):
                    dve.wait_ge(yT_psum, b * KD + k + 1)
                    nc.vector.tensor_copy(yT[:, k, :], pt[:, k, :]).then_inc(yT_dve, 1)
                dve.wait_ge(x_in, b * 16 + 16)
                for tt in range(TT):
                    dve.wait_ge(out_done, b * TT + tt + 1)
                    nc.vector.tensor_tensor(t.x1[:, bass.ds(b * TT + tt, 1), :].rearrange("p o d -> p (o d)"), pf[:, tt, :],
                                            xb[:, tt, :], ALU.add).then_inc(x1_ready, 1)
                nc.vector.tensor_copy(gain_b[:], gain[:, :, bass.ds(b, 1)].rearrange("p k o -> p (k o)"))
                nc.vector.tensor_copy(shift_b[:], shift[:, :, bass.ds(b, 1)].rearrange("p k o -> p (k o)"))
                dve.wait_ge(sq2, b * TT + TT)
                nc.vector.tensor_scalar(s2[:], s2[:], 1.0 / D, 1e-6, ALU.mult, ALU.add).then_inc(ms2, 1)
                dve.wait_ge(rs2, b * 1 + 1)
                for tt in range(TT):
                    nc.vector.tensor_scalar(y[:, tt, :], t.x1[:, bass.ds(b * TT + tt, 1), :].rearrange("p o d -> p (o d)"),
                                            r2[:, tt:tt + 1], None, ALU.mult).then_inc(normed, 1)
                for k in (1, 3):
                    dve.wait_ge(nT_psum, b * KD + k + 1)
                    nc.vector.tensor_scalar(t.xnT[:, bass.ds(b, 1), k, :].rearrange("p o t -> p (o t)"), pt[:, k, :],
                                            gain_b[:, k:k + 1], shift_b[:, k:k + 1], ALU.mult, ALU.add).then_inc(nT_dve, 1)


def full_attention_stage(nc, t, W_qkv, g_q, g_k):
    with ExitStack() as ctx:
        sem = ctx.enter_context(Sems(nc, "fa_"))

        def sb(name, shape, dt=F32):
            return ctx.enter_context(nc.sbuf_tensor("fa_" + name, shape, dt))

        w, wg, hb = sb("w", [P, KD, 3 * D]), sb("wg", [P, 3, KD, P]), sb("hb", [P, KD, T])
        ones, g = sb("headones", [P, P]), sb("g", [P, 2])
        sq, rs, v = sb("sq", [P, 2, T]), sb("rs", [P, 2, T]), sb("v", [P, TT, P])
        eps = sb("eps", [P, 1])
        core = AttentionCore(nc, ctx, sem, "fa_", 1, float(DH) ** -0.5, False)
        oT_written = core.banks_free
        w_in, const_in, hb_in, w_free, eps_set = sem("w_in"), sem("const_in"), sem("hb_in"), sem("w_free"), sem("eps_set")
        projected, v_done, v_ready, squared, summed, ln_done, rs_done, qk_ready = (sem(n) for n in (
            "projected", "v_done", "v_ready", "squared", "summed", "ln_done", "rs_done", "qk_ready"))
        block = ctx.enter_context(nc.Block())
        N_C = 16 * (1 + 2 * HG)
        NIT, NG = B * KD, len(core.groups)

        @block.sync
        def _(sp):
            sp.dma_start(w[:], W_qkv.rearrange("(k p) n -> p k n", p=P)).then_inc(w_in, 16)
            sp.dma_start(ones[:], t.const["headones"]).then_inc(const_in, 16)
            for n, vec in enumerate((g_q, g_k)):
                for h in range(HG):
                    sp.dma_start(g[DH * h:DH * h + DH, n:n + 1], vec.unsqueeze(1)).then_inc(const_in, 16)
            sp.wait_ge(w_in, 16)
            with sp.Fori(0, B) as b:
                with sp.Fori(0, KD) as gg:
                    sp.wait_ge(w_free, b * KD + gg + 1)
                    sp.dma_start(hb[:], t.xnT[:, bass.ds(b, 1), :, :].rearrange("p o k t -> p (o k) t")).then_inc(hb_in, 16)
                    for n in range(3):
                        sp.dma_start(wg[:, n, :, :], w[:, :, bass.ds(gg * P + n * D, P)]).then_inc(hb_in, 16)

        @block.tensor
        def _(pe):
            pe.wait_ge(w_in, 16)
            pe.wait_ge(const_in, N_C)
            pe.wait_ge(core.core_set, core.SET)

            def project(it):
                pe.wait_ge(hb_in, it * 64 + 64)
                for n in (1, 0):
                    for k in range(KD):
                        last = nc.tensor.matmul(core.ps[:, n, :], wg[:, n, k, :], hb[:, k, :], start=(k == 0), stop=(k == KD - 1))
                    last.then_inc(projected, 1)
                for n in (1, 0):
                    pe.wait_ge(squared, it * 2 + (2 - n))
                    nc.tensor.matmul(core.ps[:, 3 - n, :], ones[:], sq[:, n, :], start=True, stop=True).then_inc(summed, 1)
                for tt in range(TT):
                    for k in range(KD):
                        last = nc.tensor.matmul(core.ps[:, 5, tt * P:(tt + 1) * P], hb[:, k, tt * P:(tt + 1) * P],
                                                wg[:, 2, k, :], start=(k == 0), stop=(k == KD - 1))
                last.then_inc(v_done, 1)

            def attend(it):
                pe.wait_ge(qk_ready, it * (2 * HG) + 2 * HG)
                pe.wait_ge(v_ready, it * 1 + 1)
                core.tensor(pe, it, v, t.ident[:], None, None, None)

            project(0)
            with pe.Fori(0, NIT - 1) as it:
                attend(it)
                pe.wait_ge(core.exp_done, it * NG + NG)
                project(it + 1)
            attend(NIT - 1)

        @block.scalar
        def _(act):
            nc.scalar.preload_act_table_set("natural_log_exp_and_others")
            act.wait_ge(eps_set, 1)

            def project(it):
                for n in (1, 0):
                    act.wait_ge(projected, it * 2 + (2 - n))
                    nc.scalar.activation(sq[:, n, :], core.ps[:, n, :], ACT.Square).then_inc(squared, 1)
                for n in (1, 0):
                    act.wait_ge(summed, it * 2 + (2 - n))
                    nc.scalar.activation(rs[:, n, :], core.ps[:, 3 - n, :], ACT.Ln, bias=eps[:, 0:1], scale=1.0 / DH).then_inc(ln_done, 1)
                    act.wait_ge(ln_done, it * 2 + (2 - n))
                    nc.scalar.activation(rs[:, n, :], rs[:, n, :], ACT.Exp, scale=-0.5).then_inc(rs_done, 1)
                act.wait_ge(v_done, it * 1 + 1)
                nc.scalar.activation(v[:].rearrange("p t d -> p (t d)"), core.ps[:, 5, :], ACT.Copy).then_inc(v_ready, 1)
                act.wait_ge(v_ready, it * 1 + 1)
                act.sem_inc(w_free, 1)

            project(0)
            with act.Fori(0, NIT - 1) as it:
                core.scalar(act, it)
                project(it + 1)
            core.scalar(act, NIT - 1)

        @block.vector
        def _(dve):
            nc.vector.memset(eps[:], 1e-6).then_inc(eps_set, 1)
            dve.sem_inc(w_free, 1)
            dve.sem_inc(oT_written, 1)
            core.setup(dve)
            dve.wait_ge(const_in, N_C)

            def project(it):
                for n in (1, 0):
                    dve.wait_ge(rs_done, it * 2 + (2 - n))
                    for h in range(HG):
                        sl = slice(DH * h, DH * h + DH)
                        dst = core.qp[sl, h, :] if n == 0 else core.kp[sl, 0, h, :]
                        nc.vector.scalar_tensor_tensor(dst, core.ps[sl, n, :], g[sl, n:n + 1], rs[sl, n, :],
                                                       op0=ALU.mult, op1=ALU.mult).then_inc(qk_ready, 1)

            def attend(it, b, k):
                core.vector(dve, it)
                nc.vector.scalar_tensor_tensor(t.oT[:, k, b, :].rearrange("p k o t -> p (k o t)"), core.ps[:, 4, :], -1.0,
                                               core.rec[:, 0, :], op0=ALU.mult, op1=ALU.mult).then_inc(oT_written, 1)

            project(0)
            with dve.Fori(0, B - 1) as b:
                with dve.Fori(0, KD) as k:
                    attend(b * KD + k, bass.ds(b, 1), bass.ds(k, 1))
                    project(b * KD + k + 1)
            with dve.Fori(0, KD - 1) as k:
                attend(k + (B - 1) * KD, slice(B - 1, B), bass.ds(k, 1))
                project(k + (B - 1) * KD + 1)
            attend(NIT - 1, slice(B - 1, B), slice(KD - 1, KD))


def route_stage(nc, t, W_out, gate_w, sg_w, su_w, sd_w):
    with ExitStack() as ctx:
        sem = ctx.enter_context(Sems(nc, "ro_"))

        def sb(name, shape, dt=F32):
            return ctx.enter_context(nc.sbuf_tensor("ro_" + name, shape, dt))

        NC = SI // P
        wout, stage = sb("wout", [P, KD, D]), sb("stage", [P, 4, D])
        gwT, sgT, suT, sdT = sb("gwT", [P, KD, E]), sb("sgT", [P, KD, SI]), sb("suT", [P, KD, SI]), sb("sdT", [P, NC, D])
        sdraw = sb("sdraw", [P, KD, SI])
        ob, yT, yb = sb("ob", [P, KD, T]), sb("yT", [P, KD, T]), sb("yb", [P, TT, D])
        sil, hT = sb("sil", [P, 2, T]), sb("hT", [P, NC, T])
        lf, before, ones, carry = sb("lf", [P, P]), sb("before", [P, P], BF16), sb("ones", [P, P], BF16), sb("carry", [P, E], BF16)
        iota = sb("iota", [P, E])
        lg, v8, i8 = sb("lg", [P, TT, E]), sb("v8", [P, TT, 8]), sb("i8", [P, TT, 8], U32)
        nv, ex, se, ev, rs = sb("nv", [P, TT]), sb("ex", [P, TT, E]), sb("se", [P, TT]), sb("ev", [P, TT, 8]), sb("rs", [P, TT])
        ef, oh, mask = sb("ef", [P, TT * K]), sb("oh", [P, TT * K, E], BF16), sb("mask", [P, TT, E], BF16)
        posb, pr, pk, valid, sf = sb("posb", [P, TT, E], BF16), sb("pr", [P, TT * K, E]), sb("pk", [P, TT * K]), sb("valid", [P, TT * K]), sb("sf", [P, TT * K])
        slot = sb("slot", [P, TT * K], U32)
        pa = ctx.enter_context(nc.psum_tensor("ro_pa", [P, 4, 512], F32))
        pb = ctx.enter_context(nc.psum_tensor("ro_pb", [P, 4, 512], F32))
        names = """const_in raw_in zeroed setup_psum setup_copied ready ob_in y_psum y_ready
            yT_psum yT_act yT_dve logits gates ups silued hidden down_done added lg_copied top8 found nv_done
            exps e_done rs_done w1_done cast1 onehot masked mask_ready placed prod_done pk_done valid_done base_done
            base2_done sf_done tick slots_ready scattered w_done carried ld""".split()
        S = {n: sem(n) for n in names}
        block = ctx.enter_context(nc.Block())
        N_C = 16 * 3

        @block.sync
        def _(sp):
            sp.dma_start(wout[:], W_out.rearrange("(k p) n -> p k n", p=P)).then_inc(S["const_in"], 16)
            sp.dma_start(lf[:], t.const["before"]).then_inc(S["const_in"], 16)
            sp.dma_start(iota[:], t.const["iota"].unsqueeze(0).broadcast_to([P, E])).then_inc(S["const_in"], 16)
            sp.dma_start(stage[0:E, 0, :], gate_w).then_inc(S["raw_in"], 16)
            sp.dma_start(stage[:, 1:4, :], sg_w.rearrange("(c p) n -> p c n", p=P)).then_inc(S["raw_in"], 16)
            sp.dma_start(sdraw[:], sd_w.rearrange("(k p) n -> p k n", p=P)).then_inc(S["raw_in"], 16)
            sp.wait_ge(S["setup_copied"], 2 * KD)
            sp.dma_start(stage[:, 1:4, :], su_w.rearrange("(c p) n -> p c n", p=P)).then_inc(S["raw_in"], 16)
            with sp.Fori(0, B) as b:
                sp.wait_ge(S["ld"], b * 1 + 1)
                sp.dma_start(ob[:], t.oT[:, :, bass.ds(b, 1), :].rearrange("p k o t -> p (k o) t")).then_inc(S["ob_in"], 16)

        @block.tensor
        def _(pe):
            pe.wait_ge(S["raw_in"], 48)
            for k in range(KD):
                nc.tensor.transpose(pa[:, k, 0:E], stage[0:E, 0, k * P:(k + 1) * P], t.ident[0:E, 0:E]).then_inc(S["setup_psum"], 1)
            for k in range(KD):
                for c in range(NC):
                    last = nc.tensor.transpose(pb[:, k, c * P:(c + 1) * P], stage[:, 1 + c, k * P:(k + 1) * P], t.ident[:])
                last.then_inc(S["setup_psum"], 1)
            pe.wait_ge(S["setup_copied"], 2 * KD)
            for c in range(NC):
                for k in range(KD):
                    last = nc.tensor.transpose(pa[:, c, k * P:(k + 1) * P], sdraw[:, k, c * P:(c + 1) * P], t.ident[:])
                last.then_inc(S["setup_psum"], 1)
            pe.wait_ge(S["raw_in"], 64)
            for k in range(KD):
                for c in range(NC):
                    last = nc.tensor.transpose(pb[:, k, c * P:(c + 1) * P], stage[:, 1 + c, k * P:(k + 1) * P], t.ident[:])
                last.then_inc(S["setup_psum"], 1)
            pe.wait_ge(S["setup_copied"], 3 * KD + NC)
            pe.wait_ge(S["ready"], 3 + KD)
            with pe.Fori(0, B) as b:
                pe.wait_ge(S["ob_in"], b * 16 + 16)
                for tt in range(TT):
                    for k in range(KD):
                        last = nc.tensor.matmul(pb[:, tt, :], ob[:, k, tt * P:(tt + 1) * P], wout[:, k, :], start=(k == 0), stop=(k == KD - 1))
                    last.then_inc(S["y_psum"], 1)
                pe.wait_ge(S["y_ready"], b * TT + TT)
                for k in range(KD):
                    for tt in range(TT):
                        last = nc.tensor.transpose(pa[:, k, tt * P:(tt + 1) * P], yb[:, tt, k * P:(k + 1) * P], t.ident[:])
                    last.then_inc(S["yT_psum"], 1)
                pe.wait_ge(S["yT_act"], b * 2 + 2)
                pe.wait_ge(S["yT_dve"], b * 2 + 2)
                for tt in range(TT):
                    for k in range(KD):
                        last = nc.tensor.matmul(pb[:, 0, tt * E:(tt + 1) * E], yT[:, k, tt * P:(tt + 1) * P], gwT[:, k, :], start=(k == 0), stop=(k == KD - 1))
                last.then_inc(S["logits"], 1)
                for c in range(NC):
                    if c >= 2:
                        pe.wait_ge(S["hidden"], b * NC + c - 1)
                    for wT, n, done in ((sgT, 0, "gates"), (suT, 1, "ups")):
                        for k in range(KD):
                            last = nc.tensor.matmul(pa[:, 2 * (c % 2) + n, :], wT[:, k, c * P:(c + 1) * P], yT[:, k, :], start=(k == 0), stop=(k == KD - 1))
                        last.then_inc(S[done], 1)
                pe.wait_ge(S["hidden"], b * NC + NC)
                pe.wait_ge(S["lg_copied"], b * 1 + 1)
                for tt in range(TT):
                    for c in range(NC):
                        last = nc.tensor.matmul(pb[:, tt, :], hT[:, c, tt * P:(tt + 1) * P], sdT[:, c, :], start=(c == 0), stop=(c == NC - 1))
                    last.then_inc(S["down_done"], 1)
                pe.wait_ge(S["mask_ready"], b * 1 + 1)
                for tt in range(TT):
                    acc = pa[:, 0, tt * E:(tt + 1) * E]
                    nc.tensor.matmul(acc, ones[:], carry[:], start=True, stop=False)
                    for u in range(tt):
                        nc.tensor.matmul(acc, ones[:], mask[:, u, :], start=False, stop=False)
                    last = nc.tensor.matmul(acc, before[:], mask[:, tt, :], start=False, stop=True)
                last.then_inc(S["placed"], 1)
                pe.wait_ge(S["prod_done"], b * 1 + 1)
                pe.wait_ge(S["added"], b * TT + TT)

        @block.scalar
        def _(act):
            with act.Fori(0, B) as b:
                for k in (0, 2):
                    act.wait_ge(S["yT_psum"], b * KD + k + 1)
                    nc.scalar.activation(yT[:, k, :], pa[:, k, :], ACT.Copy).then_inc(S["yT_act"], 1)
                act.wait_ge(S["nv_done"], b * 1 + 1)
                for tt in range(TT):
                    nc.scalar.activation(ex[:, tt, :], lg[:, tt, :], ACT.Exp, bias=nv[:, tt:tt + 1], accum_out=se[:, tt:tt + 1])
                    last = nc.scalar.activation(ev[:, tt, :], v8[:, tt, :], ACT.Exp, bias=nv[:, tt:tt + 1])
                last.then_inc(S["exps"], 1)
                for c in range(NC):
                    act.wait_ge(S["gates"], b * NC + c + 1)
                    if c >= 2:
                        act.wait_ge(S["hidden"], b * NC + c - 1)
                    nc.scalar.activation(sil[:, c % 2, :], pa[:, 2 * (c % 2), :], ACT.Silu).then_inc(S["silued"], 1)

        @block.gpsimd
        def _(pool):
            pool.sem_inc(S["w_done"], 1)
            with pool.Fori(0, B) as b:
                pool.wait_ge(S["slots_ready"], b * 1 + 1)
                pool.sem_inc(S["tick"], 1)
                for tt in range(TT):
                    for k in range(K):
                        nc.gpsimd.indirect_dma_start(
                            out=t.xg_dram, out_offset=bass.IndirectOffsetOnAxis(ap=slot[:, tt * K + k:tt * K + k + 1], axis=0),
                            in_=yb[:, tt, :], in_offset=None, bounds_check=SLOTS - 1, oob_is_err=False).then_inc(S["scattered"], 16)
                pool.wait_ge(S["scattered"], b * (TT * K * 16) + TT * K * 16)
                pool.sem_inc(S["w_done"], 1)

        @block.vector
        def _(dve):
            dve.sem_inc(S["ld"], 1)
            dve.sem_inc(S["carried"], 1)
            nc.vector.memset(ones[:], 1.0).then_inc(S["ready"], 1)
            nc.vector.memset(carry[:], 0.0).then_inc(S["ready"], 1)
            n = 0

            def setup(dst, src, at):
                dve.wait_ge(S["setup_psum"], at)
                nc.vector.tensor_copy(dst, src).then_inc(S["setup_copied"], 1)

            for k in range(KD):
                setup(gwT[:, k, :], pa[:, k, 0:E], k + 1)
            for k in range(KD):
                setup(sgT[:, k, :], pb[:, k, 0:SI], KD + k + 1)
            for c in range(NC):
                setup(sdT[:, c, :], pa[:, c, :], 2 * KD + c + 1)
            for k in range(KD):
                setup(suT[:, k, :], pb[:, k, 0:SI], 2 * KD + NC + k + 1)
            dve.wait_ge(S["const_in"], N_C)
            nc.vector.tensor_copy(before[:], lf[:]).then_inc(S["ready"], 1)
            for k in range(KD):
                diag = wout[:, k, k * P:(k + 1) * P]
                nc.vector.tensor_tensor(diag, diag, t.ident[:], ALU.add).then_inc(S["ready"], 1)
            with dve.Fori(0, B) as b:
                one = b * 1 + 1
                for tt in range(TT):
                    dve.wait_ge(S["y_psum"], b * TT + tt + 1)
                    if tt == 0:
                        dve.wait_ge(S["w_done"], one)
                    nc.vector.tensor_copy(yb[:, tt, :], pb[:, tt, :]).then_inc(S["y_ready"], 1)
                dve.wait_ge(S["y_ready"], b * TT + TT)
                dve.sem_inc(S["ld"], 1)
                for k in (1, 3):
                    dve.wait_ge(S["yT_psum"], b * KD + k + 1)
                    nc.vector.tensor_copy(yT[:, k, :], pa[:, k, :]).then_inc(S["yT_dve"], 1)
                dve.wait_ge(S["logits"], one)
                nc.vector.tensor_copy(lg[:].rearrange("p t e -> p (t e)"), pb[:, 0, 0:TT * E]).then_inc(S["lg_copied"], 1)
                dve.wait_ge(S["lg_copied"], one)
                dve.sem_inc(S["tick"], 1)
                for tt in range(TT):
                    nc.vector.max(v8[:, tt, :], lg[:, tt, :]).then_inc(S["top8"], 1)
                dve.wait_ge(S["top8"], b * TT + TT)
                nc.vector.tensor_scalar(nv[:], v8[:, :, 0], -1.0, None, ALU.mult).then_inc(S["nv_done"], 1)
                for tt in range(TT):
                    nc.vector.max_index(i8[:, tt, :], v8[:, tt, :], lg[:, tt, :]).then_inc(S["found"], 1)
                dve.wait_ge(S["found"], b * TT + TT)
                k24 = "p (t k) -> p t k"
                nc.vector.tensor_copy(ef[:].rearrange(k24, k=K), i8[:, :, 0:K]).then_inc(S["cast1"], 1)
                dve.wait_ge(S["cast1"], one)
                nc.vector.tensor_tensor(oh[:], iota[:].unsqueeze(1).broadcast_to([P, TT * K, E]),
                                        ef[:].unsqueeze(2).broadcast_to([P, TT * K, E]), ALU.is_equal).then_inc(S["onehot"], 1)
                dve.wait_ge(S["onehot"], one)
                with nc.allow_low_precision("a sum of at most one 1 is exact"):
                    for tt in range(TT):
                        nc.vector.tensor_reduce(mask[:, tt, :], oh[:, tt * K:(tt + 1) * K, :].rearrange("p k e -> p e k"), AX,
                                                ALU.add).then_inc(S["masked"], 1)
                dve.wait_ge(S["masked"], b * TT + TT)
                dve.wait_ge(S["carried"], b * TT + 1)
                dve.sem_inc(S["mask_ready"], 1)
                for c in range(NC):
                    dve.wait_ge(S["silued"], b * NC + c + 1)
                    dve.wait_ge(S["ups"], b * NC + c + 1)
                    nc.vector.tensor_tensor(hT[:, c, :], sil[:, c % 2, :], pa[:, 2 * (c % 2) + 1, :], ALU.mult).then_inc(S["hidden"], 1)
                dve.wait_ge(S["exps"], one)
                nc.vector.reciprocal(rs[:], se[:]).then_inc(S["rs_done"], 1)
                dve.wait_ge(S["rs_done"], one)
                wk = t.wk[:, bass.ds(b, 1), :].rearrange("p o k -> p (o k)")
                nc.vector.tensor_tensor(wk.rearrange(k24, k=K), ev[:, :, 0:K], rs[:].unsqueeze(2).broadcast_to([P, TT, K]),
                                        ALU.mult).then_inc(S["w1_done"], 1)
                for tt in range(TT):
                    dve.wait_ge(S["down_done"], b * TT + tt + 1)
                    x1 = t.x1[:, bass.ds(b * TT + tt, 1), :].rearrange("p o d -> p (o d)")
                    nc.vector.tensor_tensor(x1, x1, pb[:, tt, :], ALU.add).then_inc(S["added"], 1)
                dve.wait_ge(S["placed"], one)
                for tt in range(TT):
                    last = nc.vector.tensor_tensor(pr[:, tt * K:(tt + 1) * K, :], oh[:, tt * K:(tt + 1) * K, :],
                                                   pa[:, 0, tt * E:(tt + 1) * E].unsqueeze(1).broadcast_to([P, K, E]), ALU.mult)
                last.then_inc(S["prod_done"], 1)
                dve.wait_ge(S["prod_done"], one)
                nc.vector.tensor_reduce(pk[:], pr[:], AX, ALU.add).then_inc(S["pk_done"], 1)
                dve.wait_ge(S["pk_done"], one)
                nc.vector.tensor_scalar(valid[:], pk[:], float(CAP), None, ALU.is_lt).then_inc(S["valid_done"], 1)
                nc.vector.scalar_tensor_tensor(sf[:], ef[:], float(CAP), pk[:], op0=ALU.mult, op1=ALU.add).then_inc(S["base_done"], 1)
                dve.wait_ge(S["valid_done"], one)
                dve.wait_ge(S["base_done"], one)
                nc.vector.scalar_tensor_tensor(sf[:], sf[:], -float(SLOTS), valid[:], op0=ALU.add, op1=ALU.mult).then_inc(S["base2_done"], 1)
                dve.wait_ge(S["base2_done"], one)
                nc.vector.tensor_scalar(sf[:], sf[:], float(SLOTS), None, ALU.add).then_inc(S["sf_done"], 1)
                dve.wait_ge(S["sf_done"], one)
                nc.vector.tensor_copy(slot[:], sf[:]).then_inc(S["slots_ready"], 1)
                nc.vector.tensor_copy(t.slot[:, bass.ds(b, 1), :].rearrange("p o k -> p (o k)"), sf[:])
                dve.wait_ge(S["w1_done"], one)
                nc.vector.tensor_tensor(wk, wk, valid[:], ALU.mult)
                for tt in range(TT):
                    dve.wait_ge(S["carried"], b * TT + tt + 1)
                    nc.vector.tensor_tensor(carry[:], carry[:], mask[:, tt, :], ALU.add).then_inc(S["carried"], 1)


def expert_stage(nc, t, gate_up, down):
    with ExitStack() as ctx:
        sem = ctx.enter_context(Sems(nc, "ex_"))
        U = 4

        def sb(name, shape, dt=F32):
            return ctx.enter_context(nc.sbuf_tensor("ex_" + name, shape, dt))

        HC = I // 2
        wg, wd, xg = sb("wg", [P, U, KD, 2 * I]), sb("wd", [HC, U, 2, D]), sb("xg", [P, U, D])
        xT, sil, hid, hT, eo = sb("xT", [P, 2, KD, P]), sb("sil", [P, 2, I]), sb("hid", [P, 2, I]), sb("hT", [HC, 2, 2, P]), sb("eo", [P, 2, D])
        px = ctx.enter_context(nc.psum_tensor("ex_px", [P, 2, 512], F32))
        pg = ctx.enter_context(nc.psum_tensor("ex_pg", [P, 2, 512], F32))
        ph = ctx.enter_context(nc.psum_tensor("ex_ph", [P, 2, 512], F32))
        pd = ctx.enter_context(nc.psum_tensor("ex_pd", [P, 2, 512], F32))
        w_in = [sem(f"w_in{u}") for u in range(U)]
        xT_psum, xT_ready, gu_done, silued, hid_ready, hT_psum, hT_ready, down_done, eo_ready = (sem(n) for n in (
            "xT_psum", "xT_ready", "gu_done", "silued", "hid_ready", "hT_psum", "hT_ready", "down_done", "eo_ready"))
        stored = [sem("stored0"), sem("stored1")]
        block = ctx.enter_context(nc.Block())
        NL = E // U

        def load(sp, e, u):
            sp.dma_start(xg[:, u, :], t.xg_dram[bass.ds(e * CAP, CAP), :]).then_inc(w_in[u], 16)
            sp.dma_start(wg[:, u, :, :], gate_up[bass.ds(e, 1), :, :].rearrange("o (k p) i -> p (o k) i", p=P)).then_inc(w_in[u], 16)
            sp.dma_start(wd[:, u, :, :], down[bass.ds(e, 1), :, :].rearrange("o (c q) h -> q (o c) h", q=HC)).then_inc(w_in[u], 16)

        def wait(eng, s, q, n):
            eng.wait_ge(s, q * U + n)

        @block.sync
        def _(sp):
            for u in range(U):
                load(sp, u, u)
            with sp.Fori(0, NL - 1) as q:
                for u in range(U):
                    wait(sp, down_done, q, u + 1)
                    load(sp, q * U + (U + u), u)

        @block.tensor
        def _(pe):
            def hidden(q, u, first):
                wait_in = 48 * 1
                pe.wait_ge(w_in[u], q * wait_in + wait_in)
                if not first or u >= 2:
                    wait(pe, xT_ready, q, u - 1)
                for k in range(KD):
                    last = nc.tensor.transpose(px[:, u % 2, k * P:(k + 1) * P], xg[:, u, k * P:(k + 1) * P], t.ident[:])
                last.then_inc(xT_psum, 1)
                wait(pe, xT_ready, q, u + 1)
                if not first or u >= 2:
                    wait(pe, hid_ready, q, u - 1)
                for k in range(KD):
                    last = nc.tensor.matmul(pg[:, u % 2, 0:2 * I], xT[:, u % 2, k, :], wg[:, u, k, :], start=(k == 0), stop=(k == KD - 1))
                last.then_inc(gu_done, 1)

            def output(q, u, first):
                s = u % U
                wait(pe, hid_ready, q, u + 1)
                if not first or u >= 2:
                    wait(pe, hT_ready, q, u - 1)
                for c in range(2):
                    last = nc.tensor.transpose(ph[0:HC, s % 2, c * P:(c + 1) * P], hid[:, s % 2, c * HC:(c + 1) * HC], t.ident[:])
                last.then_inc(hT_psum, 1)
                wait(pe, hT_ready, q, u + 1)
                if not first or u >= 2:
                    wait(pe, eo_ready, q, u - 1)
                for c in range(2):
                    last = nc.tensor.matmul(pd[:, s % 2, :], hT[:, s % 2, c, :], wd[:, s, c, :], start=(c == 0), stop=(c == 1))
                last.then_inc(down_done, 1)

            for u in range(U):
                hidden(0, u, True)
                if u:
                    output(0, u - 1, True)
            with pe.Fori(1, NL) as q:
                for u in range(U):
                    hidden(q, u, False)
                    output(q, u - 1, False)
            output(NL - 1, U - 1, False)

        @block.scalar
        def _(act):
            nc.scalar.preload_act_table_set("silu_and_others")

            def step(q, u, first, body=True):
                if body:
                    wait(act, gu_done, q, u + 1)
                    if not first or u >= 2:
                        wait(act, hid_ready, q, u - 1)
                    nc.scalar.activation(sil[:, u % 2, :], pg[:, u % 2, 0:I], ACT.Silu).then_inc(silued, 1)
                if not first or u >= 1:
                    v = u - 1
                    s = v % 2
                    wait(act, down_done, q, v + 1)
                    if not first or v >= 2:
                        act.wait_ge(stored[s], q * (16 * U // 2) + 16 * (v // 2))
                    nc.scalar.activation(eo[:, s, :], pd[:, s, :], ACT.Copy).then_inc(eo_ready, 1)

            for u in range(U):
                step(0, u, True)
            with act.Fori(1, NL) as q:
                for u in range(U):
                    step(q, u, False)
            step(NL, 0, False, body=False)

        @block.gpsimd
        def _(pool):
            with pool.Fori(0, NL) as q:
                for u in range(U):
                    wait(pool, eo_ready, q, u + 1)
                    nc.gpsimd.dma_start(t.eo_dram[bass.ds((q * U + u) * CAP, CAP), :], eo[:, u % 2, :]).then_inc(stored[u % 2], 16)
            for s in range(2):
                pool.wait_ge(stored[s], 16 * E // 2)

        @block.vector
        def _(dve):
            def step(q, u, first, body=True):
                if body:
                    wait(dve, xT_psum, q, u + 1)
                    if not first or u >= 2:
                        wait(dve, gu_done, q, u - 1)
                    nc.vector.tensor_copy(xT[:, u % 2, :, :].rearrange("p k t -> p (k t)"), px[:, u % 2, :]).then_inc(xT_ready, 1)
                    wait(dve, silued, q, u + 1)
                    if not first or u >= 2:
                        wait(dve, hT_psum, q, u - 1)
                    nc.vector.tensor_tensor(hid[:, u % 2, :], sil[:, u % 2, :], pg[:, u % 2, I:2 * I], ALU.mult).then_inc(hid_ready, 1)
                if not first or u >= 1:
                    v = u - 1
                    wait(dve, hT_psum, q, v + 1)
                    if not first or v >= 2:
                        wait(dve, down_done, q, v - 1)
                    nc.vector.tensor_copy(hT[:, v % 2, :, :].rearrange("p c t -> p (c t)"), ph[0:HC, v % 2, 0:2 * P]).then_inc(hT_ready, 1)

            for u in range(U):
                step(0, u, True)
            with dve.Fori(1, NL) as q:
                for u in range(U):
                    step(q, u, False)
            step(NL, 0, False, body=False)


def combine_stage(nc, t, out):
    with ExitStack() as ctx:
        sem = ctx.enter_context(Sems(nc, "co_"))
        got = ctx.enter_context(nc.sbuf_tensor("co_got", [P, 4, K, D], F32))
        idx = ctx.enter_context(nc.sbuf_tensor("co_idx", [P, B * TT * K], U32))
        acc = ctx.enter_context(nc.sbuf_tensor("co_acc", [P, 4, D], F32))
        gathered = [sem(f"gathered{i}") for i in range(4)]
        tick, idx_ready, summed, chain = sem("tick"), sem("idx_ready"), sem("summed"), sem("chain")
        stored = [sem(f"stored{i}") for i in range(4)]
        block = ctx.enter_context(nc.Block())
        out_t = out.rearrange("b t d -> (b t) d")

        @block.gpsimd
        def _(pool):
            with pool.Fori(0, B) as b:
                pool.wait_ge(idx_ready, b * 1 + 1)
                pool.sem_inc(tick, 1)
                for tt in range(TT):
                    pool.wait_ge(summed, b * TT + tt + 1)
                    pool.sem_inc(tick, 1)
                    for k in range(K):
                        nc.gpsimd.indirect_dma_start(
                            out=got[:, tt, k, :], out_offset=None, in_=t.eo_dram,
                            in_offset=bass.IndirectOffsetOnAxis(ap=idx[:, tt * K + k:tt * K + k + 1], axis=0)).then_inc(gathered[tt], 16)

        @block.sync
        def _(sp):
            with sp.Fori(0, B) as b:
                for tt in range(TT):
                    sp.wait_ge(summed, b * TT + tt + TT + 1)
                    sp.dma_start(out_t[bass.ds((b * TT + tt) * P, P), :], acc[:, tt, :]).then_inc(stored[tt], 16)
            for tt in range(TT):
                sp.wait_ge(stored[tt], 16 * B)

        @block.vector
        def _(dve):
            dve.sem_inc(summed, TT)
            nc.vector.tensor_copy(idx[:, 0:TT * K], t.slot[:, 0, :]).then_inc(idx_ready, 1)

            def tile(b, tt, first):
                dve.wait_ge(gathered[tt], b * (16 * K) + 16 * K)
                if not first:
                    dve.wait_ge(stored[tt], b * 16)
                src = t.x1[:, bass.ds(b * TT + tt, 1), :].rearrange("p o d -> p (o d)")
                wk = t.wk[:, bass.ds(b, 1), :].rearrange("p o k -> p (o k)")
                for k in range(K):
                    last = nc.vector.scalar_tensor_tensor(acc[:, tt, :], got[:, tt, k, :], wk[:, tt * K + k:tt * K + k + 1], src,
                                                          op0=ALU.mult, op1=ALU.add)
                    src = acc[:, tt, :]
                    if k < K - 1:
                        last.then_inc(chain, 1)
                        dve.wait_ge(chain, (b * TT + tt) * (K - 1) + k + 1)
                last.then_inc(summed, 1)

            for tt in range(TT):
                tile(0, tt, True)
            with dve.Fori(1, B) as b:
                nc.vector.tensor_copy(idx[:, 0:TT * K], t.slot[:, bass.ds(b, 1), :].rearrange("p o k -> p (o k)")).then_inc(idx_ready, 1)
                for tt in range(TT):
                    tile(b, tt, False)


def constants():
    f = np.float32
    p = np.arange(P)
    freq = 1.0 / 10000.0 ** (np.arange(0, DQ, 2, dtype=f) / f(DQ))
    angle = np.outer(np.arange(T, dtype=f), freq).astype(f)
    of = (p % DQ) // 2
    swap = np.zeros((P, P), f)
    swap[p[1::2], p[0::2]] = -1.0
    swap[p[0::2], p[1::2]] = 1.0
    nf = T // 2 + 1
    filt = np.exp(-0.5 * (np.linspace(0.0, 1.0, nf) / 0.15) ** 2)
    weight = np.full(nf, 2.0)
    weight[0] = weight[-1] = 1.0
    col = (weight * filt) @ np.cos(2 * np.pi * np.arange(nf)[:, None] * np.arange(T) / T) / T
    return {
        "ident": np.eye(P, dtype=f),
        "cs": np.stack([np.cos(angle)[:, of].T, np.sin(angle)[:, of].T]).astype(f),
        "swap": swap,
        "half": np.stack([p % DH < DQ, p % DH >= DQ], 1).astype(f),
        "mask": np.stack([np.where(p[None, :] > p[:, None], -1e30, 0.0), np.where(p[None, :] < p[:, None], -1e30, 0.0)]).astype(f),
        "filt": col[(np.arange(T)[:, None] - np.arange(T)) % T].astype(f),
        "headones": (p[:, None] // DH == p // DH).astype(f),
        "before": (p[:, None] < p).astype(f),
        "iota": np.arange(E, dtype=f),
    }


class Held:
    pass


def program(nc, a, out):
    t = Held()
    with ExitStack() as ctx:
        def sb(stack, name, shape, dt=F32):
            return stack.enter_context(nc.sbuf_tensor(name, shape, dt))

        t.xg_dram = nc.dram_tensor("xg", (SLOTS, D), F32, kind="Internal").ap()
        t.eo_dram = nc.dram_tensor("eo", (SLOTS + 1, D), F32, kind="Internal").ap()
        t.const = a
        t.ident = sb(ctx, "ident", [P, P])
        wide = sb(ctx, "wide", [P, KD * B * T])
        t.hsT = wide[:, :].rearrange("p (k b t) -> p k b t", k=KD, b=B)
        t.x1 = wide[:, :].rearrange("p (n d) -> p n d", d=D)
        with ExitStack() as gru:
            t.h, t.giT = sb(gru, "h", [P, ST, 4]), sb(gru, "giT", [P, T, 3 * ST])
            gate_inputs_stage(nc, t, a["x"], a["L0_cond_W_ih"], a["L0_cond_b_ih"], a["L0_cond_b_hh"])
            gru_stage(nc, t, a["cond_2048"], a["L0_cond_W_hh"], a["L0_cond_b_hh"])
        t.A = sb(ctx, "A", [P, TT, B, D])
        t.slot, t.wk = sb(ctx, "slot", [P, B, TT * K], U32), sb(ctx, "wk", [P, B, TT * K])
        diff_attention_stage(nc, t, a["L0_attn_Wq"], a["L0_attn_Wk"], a["L0_attn_Wv"],
                             [a["L0_attn_lambda_" + n] for n in ("q1", "k1", "q2", "k2")])
        t.oT = t.A[:].rearrange("p i b f -> p (i b f)").rearrange("p (k b t) -> p k b t", k=KD, b=B)
        with ExitStack() as mid:
            t.xnT = sb(mid, "xnT", [P, B, KD, T])
            filter_stage(nc, t, a["x"], a["L0_attn_Wout"], a["L0_attn_rms_weight"], a["cond_2048"],
                         a["L0_cond2_W_emb"], a["L0_cond2_b_emb"], a["L0_cond2_g_norm"])
            full_attention_stage(nc, t, a["L0_cond2_W_qkv"], a["L0_cond2_g_q"], a["L0_cond2_g_k"])
        route_stage(nc, t, a["L0_cond2_W_out"], a["L0_ffn_gate_w"], a["L0_ffn_shared_gate_w"], a["L0_ffn_shared_up_w"],
                    a["L0_ffn_shared_down_w"])
        expert_stage(nc, t, a["L0_ffn_gate_up_proj"], a["L0_ffn_down_proj"])
        combine_stage(nc, t, out)


INPUTS = ["x", "cond_2048", "L0_cond_W_ih", "L0_cond_W_hh", "L0_cond_b_ih", "L0_cond_b_hh", "L0_attn_Wq", "L0_attn_Wk",
          "L0_attn_Wv", "L0_attn_Wout", "L0_attn_lambda_q1", "L0_attn_lambda_k1", "L0_attn_lambda_q2",
          "L0_attn_lambda_k2", "L0_attn_rms_weight", "L0_cond2_W_emb", "L0_cond2_b_emb", "L0_cond2_g_norm",
          "L0_cond2_W_qkv", "L0_cond2_g_q", "L0_cond2_g_k", "L0_cond2_W_out", "L0_ffn_gate_w", "L0_ffn_gate_up_proj",
          "L0_ffn_down_proj", "L0_ffn_shared_gate_w", "L0_ffn_shared_up_w", "L0_ffn_shared_down_w"]
CONSTANTS = ["ident", "cs", "swap", "half", "mask", "filt", "headones", "before", "iota"]


def kernel(**inputs):
    import concourse.bacc as bacc
    from concourse.bass_utils import run_bass_kernel_spmd

    nc = bacc.Bacc("TRN2", target_bir_lowering=False, num_devices=1)
    arrays, aps = {}, {}
    consts = constants()
    for name in INPUTS + CONSTANTS:
        a = np.ascontiguousarray(inputs[name] if name in inputs else consts[name])
        arrays["in_" + name] = a
        aps[name] = nc.dram_tensor("in_" + name, a.shape, mybir.dt.from_np(a.dtype), kind="ExternalInput").ap()
    out = nc.dram_tensor("out_0", (B, T, D), F32, kind="ExternalOutput").ap()
    program(nc, aps, out)
    r = run_bass_kernel_spmd(nc, [arrays], core_ids=[0])
    return r.results[0]["out_0"]
```

```python
import math
from contextlib import ExitStack

import numpy as np
import concourse.bass as bass
from concourse import mybir

F32 = mybir.dt.float32
BF16 = mybir.dt.bfloat16
U32 = mybir.dt.uint32
I32 = mybir.dt.int32
ALU = mybir.AluOpType
ACT = mybir.ActivationFunctionType
AX = mybir.AxisListType.X

P = 128
B, T, D = 4, 512, 512
KD = D // P
TT = T // P
NTILE = B * TT
H = 16
DH = D // H
G3 = 3 * D
GC = G3 // P
ST = KD * B
HG = P // DH
DQ = DH // 2
LAMBDA_INIT = 0.8 - 0.6 * math.exp(-0.3 * 12)
E, K, CAP = 64, 6, 128
SLOTS = E * CAP
I = 192
SI = 2 * I


class Sems:

    def __init__(self, nc, prefix):
        self.nc, self.prefix, self.held = nc, prefix, []

    def __call__(self, name):
        self.held.append(self.nc.alloc_semaphore(name=self.prefix + name))
        return self.held[-1]

    def __enter__(self):
        return self

    def __exit__(self, *failed):
        if not failed[0]:
            self.nc.clear_and_free_semaphores(self.held)
            self.nc.all_engine_barrier()


def gate_inputs_stage(nc, t, x, W_ih, b_ih, b_hh):
    with ExitStack() as ctx:
        sem = ctx.enter_context(Sems(nc, "gi_"))
        wih = ctx.enter_context(nc.sbuf_tensor("wih", [P, KD, G3], F32))
        wraw = t.ahead[:, 0:2 * G3].rearrange("p (a n) -> p a n", a=2)
        xin = ctx.enter_context(nc.sbuf_tensor("gi_xin", [P, TT, D], F32))
        xT = t.ahead[:, 2 * G3:2 * G3 + KD * T].rearrange("p (k t) -> p k t", k=KD)
        bias = ctx.enter_context(nc.sbuf_tensor("gi_bias", [P, 2, GC], F32))
        pt = ctx.enter_context(nc.psum_tensor("gi_pt", [P, 2, T], F32))
        pg = ctx.enter_context(nc.psum_tensor("gi_pg", [P, 4, T], F32))
        x_in, w_in, b_in = sem("x_in"), [sem("w_in0"), sem("w_in1")], sem("b_in")
        ident_in = sem("ident_in")
        xT_psum, xT_ready = sem("xT_psum"), sem("xT_ready")
        w_spread, bias_ready = sem("w_spread"), sem("bias_ready")
        gi_psum, gi_even, gi_odd = sem("gi_psum"), sem("gi_even"), sem("gi_odd")
        block = ctx.enter_context(nc.Block())

        @block.sync
        def _(sp):
            sp.dma_start(t.ident[:], t.const["ident"]).then_inc(ident_in, 16)
            sp.dma_start(xin[:], x[0, :, :].rearrange("(tt p) d -> p tt d", p=P)).then_inc(x_in, 16)
            with sp.Fori(1, B) as b:
                sp.wait_ge(xT_psum, b * KD)
                sp.dma_start(xin[:], x[bass.ds(b, 1), :, :].rearrange("o (tt p) d -> p (o tt) d", p=P)).then_inc(x_in, 16)

        @block.gpsimd
        def _(pool):
            for k in range(KD):
                if k >= 2:
                    pool.wait_ge(w_spread, 3 * (k - 1))
                pool.dma_start(wraw[:, k % 2, :], W_ih[k * P:(k + 1) * P, :]).then_inc(w_in[k % 2], 16)

        @block.tensor
        def _(pe):
            pe.wait_ge(ident_in, 16)
            with pe.Fori(0, B) as b:
                pe.wait_ge(x_in, b * 16 + 16)
                for k in range(KD):
                    if k >= 2:
                        pe.wait_ge(xT_ready, b * KD + (k - 1))
                    for tt in range(TT):
                        last = nc.tensor.transpose(pt[:, k % 2, tt * P:(tt + 1) * P], xin[:, tt, k * P:(k + 1) * P], t.ident[:])
                    last.then_inc(xT_psum, 1)
                pe.wait_ge(w_spread, 3 * KD)
                pe.wait_ge(xT_ready, b * KD + KD)
                for c in range(GC):
                    if c >= 4:
                        pe.wait_ge(gi_even if c % 2 == 0 else gi_odd, b * (GC // 2) + (c - 4) // 2 + 1)
                    for k in range(KD):
                        last = nc.tensor.matmul(pg[:, c % 4, :], wih[:, k, c * P:(c + 1) * P], xT[:, k, :],
                                                start=(k == 0), stop=(k == KD - 1))
                    last.then_inc(gi_psum, 1)
                pe.wait_ge(gi_even, b * (GC // 2) + GC // 2)
                pe.wait_ge(gi_odd, b * (GC // 2) + GC // 2)

        def evict(eng, b, c, out_sem):
            eng.wait_ge(gi_psum, b * GC + c + 1)
            dst = t.giT[:, :, bass.ds(b + c * B, 1)].rearrange("p t o -> p (t o)")
            if c % 2 == 0:
                nc.scalar.activation(dst, pg[:, c % 4, :], ACT.Identity, bias=bias[:, 0, c:c + 1]).then_inc(out_sem, 1)
            else:
                nc.vector.tensor_scalar(dst, pg[:, c % 4, :], bias[:, 0, c:c + 1], None, ALU.add).then_inc(out_sem, 1)

        @block.scalar
        def _(act):
            for n, bvec in enumerate((b_ih, b_hh)):
                for j in range(KD):
                    for g in range(3):
                        act.dma_start(bias[32 * j:32 * j + 32, n, g * KD:(g + 1) * KD],
                                     bvec.rearrange("(g j c i) -> g j i c", g=3, j=KD, c=KD)[g, j],
                                     allow_slow_non_contiguous=True).then_inc(b_in, 16)
            act.wait_ge(bias_ready, 1)
            with act.Fori(0, B) as b:
                for c in range(0, GC, 2):
                    evict(act, b, c, gi_even)

        @block.vector
        def _(dve):
            dve.wait_ge(b_in, 16 * (6 * KD))
            nc.vector.tensor_tensor(bias[:, 0, 0:2 * KD], bias[:, 0, 0:2 * KD], bias[:, 1, 0:2 * KD], ALU.add).then_inc(bias_ready, 1)
            for k in range(KD):
                dve.wait_ge(w_in[k % 2], 16 * (k // 2 + 1))
                for g in range(3):
                    nc.vector.tensor_copy(wih[:, k, g * D:(g + 1) * D].rearrange("p (c j i) -> p c j i", c=KD, j=KD),
                                          wraw[:, k % 2, g * D:(g + 1) * D].rearrange("p (j c i) -> p c j i", c=KD, j=KD)
                                          ).then_inc(w_spread, 1)
            dve.wait_ge(bias_ready, 1)
            with dve.Fori(0, B) as b:
                for k in range(KD):
                    dve.wait_ge(xT_psum, b * KD + k + 1)
                    nc.vector.tensor_copy(xT[:, k, :], pt[:, k % 2, :]).then_inc(xT_ready, 1)
                for c in range(1, GC, 2):
                    evict(dve, b, c, gi_odd)


def gru_stage(nc, t, h0, W_hh, b_hh, next_weights):
    with ExitStack() as ctx:
        sem = ctx.enter_context(Sems(nc, "gru_"))

        def sb(name, shape):
            return ctx.enter_context(nc.sbuf_tensor("gru_" + name, shape, F32))

        whh = sb("whh", [P, KD, 3, KD, P])
        bias, one = sb("bias", [P, KD, P]), sb("one", [P, 2 * B])
        trz, pre = sb("trz", [P, 2 * KD, 32]), sb("pre", [P, 2 * ST])
        tn, rz, narg = sb("tn", [P, KD, 32]), sb("rz", [P, 2, KD, 32]), sb("narg", [P, KD, 32])
        d0, d1 = sb("d0", [P, ST, 4]), sb("d1", [P, ST, 4])
        hin, zeros = sb("hin", [P, KD, B]), sb("zeros", [P, 1, D])
        zero_set, cleared = sem("zero_set"), sem("cleared")
        prz = ctx.enter_context(nc.psum_tensor("gru_prz", [P, 4 * P], F32))
        pn = ctx.enter_context(nc.psum_tensor("gru_pn", [P, 4 * P], F32))
        WARM = 3
        warm = ctx.enter_context(nc.sbuf_tensor("gru_warm", [P, 4 * P], BF16))
        pw = ctx.enter_context(nc.psum_tensor("gru_pw", [P, 4 * P], F32))
        loaded_pool, ahead_in = sem("loaded_pool"), sem("ahead_in")
        loaded, h_ready, hs_kept = sem("loaded"), sem("h_ready"), sem("hs_kept")
        rz_rows, n_rows = sem("rz_rows"), sem("n_rows")
        trz_done, pre_done, rz_act = sem("trz_done"), sem("pre_done"), sem("rz_act")
        tn_done, gin_ready, side, bias_set = sem("tn_done"), sem("gin_ready"), sem("side"), sem("bias_set")
        narg_done, tanh_done = sem("narg_done"), sem("tanh_done")
        block = ctx.enter_context(nc.Block())
        state = t.h[:, :, 3]

        def cb(ap):
            return ap.rearrange("p (c b) -> p c b", b=B)

        def load(queue, cs, done):
            for jj in range(KD):
                rows = W_hh.rearrange("(jj c i) n -> jj i c n", jj=KD, c=KD)[jj]
                for c in cs:
                    queue.dma_start(whh[32 * jj:32 * jj + 32, c, :, :, :].rearrange("i g j f -> i (g j f)"),
                                    rows[:, c, :]).then_inc(done, 16)

        @block.sync
        def _(sp):
            load(sp, (0, 1), loaded)
            sp.wait_ge(bias_set, 3)
            sp.dma_start(bias[0:1, :, :].rearrange("p j f -> p (j f)"), b_hh[2 * D:3 * D].unsqueeze(0)).then_inc(loaded, 16)
            sp.wait_ge(h_ready, 1)
            w = t.ahead[:].rearrange("p (n c f) -> p n c f", n=3, c=KD)
            for n, W in enumerate(next_weights):
                for jj in range(KD):
                    sp.dma_start(w[32 * jj:32 * jj + 32, n, :, :],
                                 W.rearrange("(jj c i) n -> jj i c n", jj=KD, c=KD)[jj]).then_inc(ahead_in, 16)
            sp.wait_ge(ahead_in, 16 * 3 * KD)

        LOADS_POOL = 16 * KD
        LOADS = 16 * (KD * (KD - 1) + KD * KD + 1)

        @block.gpsimd
        def _(pool):
            load(pool, (3,), loaded_pool)
            nc.gpsimd.memset(zeros[:], 0.0).then_inc(zero_set, 1)
            pool.wait_ge(zero_set, 1)
            pool.wait_ge(h_ready, 1)
            R = 16
            xg = t.xg_dram.rearrange("(n r p) d -> n p r d", r=R, p=P)
            for n in range(SLOTS // (R * P)):
                pool.dma_start(xg[n], zeros[:].broadcast_to([P, R, D])).then_inc(cleared, 16)
            pool.dma_start(t.eo_dram[SLOTS:SLOTS + 1, :], zeros[0:1, 0, :]).then_inc(cleared, 16)
            pool.wait_ge(cleared, 16 * (SLOTS // (R * P) + 1))

        @block.tensor
        def _(pe):
            pe.wait_ge(loaded, LOADS)
            pe.wait_ge(loaded_pool, LOADS_POOL)

            def add_bias():
                for j in range(KD):
                    nc.tensor.matmul(pn[32 * j:32 * j + 2 * B, 0:P], one[:], bias[:, j, :], start=True, stop=False)

            def step(s):
                pe.wait_ge(h_ready, s * 1 + 1)
                for rows, g0, g1, done in ((prz, 0, 2, rz_rows), (pn, 2, 3, n_rows)):
                    for c in range(KD):
                        for j in range(KD):
                            last = nc.tensor.matmul(rows[32 * j:32 * j + 2 * B, 0:(g1 - g0) * P].rearrange("p (g f) -> p g f", f=P),
                                                    t.h[:, c * B:(c + 1) * B, 1:4:2].rearrange("p b o -> p (b o)"),
                                                    whh[:, c, g0:g1, j, :],
                                                    start=(c == 0 and g0 == 0), stop=(c == KD - 1))
                    last.then_inc(done, 1)

            pe.wait_ge(h_ready, 1)
            add_bias()
            with pe.Fori(0, T - 1) as s:
                step(s)
                for _ in range(WARM):
                    nc.tensor.matmul(pw[:, :], warm[:, 0:P], warm[:, :], start=True, stop=True)
                pe.wait_ge(tn_done, s * 1 + 1)
                add_bias()
            step(T - 1)

        @block.scalar
        def _(act):
            for jj in range(KD):
                for c in range(KD):
                    act.dma_start(hin[32 * jj:32 * jj + 32, c, :],
                                  h0[:, jj * P + 32 * c:jj * P + 32 * c + 32].rearrange("b i -> i b"),
                                  allow_slow_non_contiguous=True).then_inc(loaded, 16)
            load(act, (2,), loaded)
            nc.scalar.preload_act_table_set("sigmoid_and_others")
            act.wait_ge(side, 4)
            with act.Fori(0, T) as s:
                gi = t.giT[:, bass.ds(s, 1), :].rearrange("p o c -> p (o c)")
                nc.scalar.activation(rz[:, 0, :, 1:2 * B:2], cb(gi[:, 2 * ST:3 * ST]), ACT.Copy).then_inc(gin_ready, 1)
                act.wait_ge(pre_done, s * 1 + 1)
                nc.scalar.activation(rz[:, :, :, 0:2 * B:2].rearrange("p g c b -> p (g c) b"), cb(pre[:]), ACT.Sigmoid).then_inc(rz_act, 1)
                act.wait_ge(narg_done, s * 1 + 1)
                nc.scalar.activation(cb(d1[:, :, 2]), narg[:, :, 1:2 * B:2], ACT.Tanh).then_inc(tanh_done, 1)

        @block.vector
        def _(dve):
            nc.vector.memset(bias[:], 0.0).then_inc(bias_set, 1)
            nc.vector.memset(one[:], 0.0).then_inc(bias_set, 1)
            dve.wait_ge(bias_set, 2)
            nc.vector.memset(one[0:1, 1:2 * B:2], 1.0).then_inc(bias_set, 1)
            nc.vector.memset(warm[:], 0.0)
            nc.vector.memset(prz[:], 0.0)
            nc.vector.memset(pn[:], 0.0)
            nc.vector.memset(t.h[:], 0.0).then_inc(side, 1)
            nc.vector.memset(d0[:], 0.0).then_inc(side, 1)
            nc.vector.memset(rz[:], 0.0).then_inc(side, 1)
            nc.vector.memset(d1[:], 0.0).then_inc(side, 1)
            dve.wait_ge(side, 4)
            dve.wait_ge(loaded, LOADS)
            dve.wait_ge(loaded_pool, LOADS_POOL)
            nc.vector.tensor_copy(state, hin[:].rearrange("p c b -> p (c b)")).then_inc(h_ready, 1)
            with dve.Fori(0, T) as s:
                gi = t.giT[:, bass.ds(s, 1), :].rearrange("p o c -> p (o c)")
                dve.wait_ge(rz_rows, s * 1 + 1)
                nc.vector.transpose(trz[:].rearrange("p c x -> p (c x)"), prz[:, 0:2 * P]).then_inc(trz_done, 1)
                dve.wait_ge(trz_done, s * 1 + 1)
                nc.vector.tensor_tensor(cb(pre[:]), trz[:, :, 1:2 * B:2], cb(gi[:, 0:2 * ST]), ALU.add).then_inc(pre_done, 1)
                dve.wait_ge(n_rows, s * 1 + 1)
                nc.vector.transpose(tn[:].rearrange("p c x -> p (c x)"), pn[:, 0:P]).then_inc(tn_done, 1)
                dve.wait_ge(rz_act, s * 1 + 1)
                dve.wait_ge(gin_ready, s * 1 + 1)
                dve.wait_ge(tn_done, s * 1 + 1)
                nc.vector.tensor_tensor_scan(narg[:].rearrange("p c x -> p (c x)"), tn[:].rearrange("p c x -> p (c x)"),
                                             rz[:, 0, :, :].rearrange("p c x -> p (c x)"), 0.0, ALU.mult, ALU.add).then_inc(narg_done, 1)
                z = rz[:, 1, :, 0:2 * B:2]
                nc.vector.tensor_scalar(cb(d0[:, :, 3]), z, -1.0, 1.0, ALU.mult, ALU.add).then_inc(side, 1)
                nc.vector.tensor_tensor(cb(d1[:, :, 3]), z, cb(state), ALU.mult).then_inc(side, 1)
                dve.wait_ge(side, s * 2 + 6)
                dve.wait_ge(tanh_done, s * 1 + 1)
                nc.vector.tensor_tensor_scan(t.h[:].rearrange("p c o -> p (c o)"), d0[:].rearrange("p c o -> p (c o)"),
                                             d1[:].rearrange("p c o -> p (c o)"), 0.0, ALU.mult, ALU.add).then_inc(h_ready, 1)
                dve.wait_ge(h_ready, s * 1 + 2)
                nc.vector.tensor_copy(t.hsT[:, :, :, bass.ds(s, 1)].rearrange("p k b o -> p (k b o)"), state).then_inc(hs_kept, 1)
            dve.wait_ge(hs_kept, T)


class AttentionCore:

    def __init__(self, nc, ctx, sem, prefix, NA, scale, causal):
        self.nc, self.NA, self.scale, self.causal = nc, NA, scale, causal

        def sb(name, shape, dt=F32):
            return ctx.enter_context(nc.sbuf_tensor(prefix + name, shape, dt))

        self.probT = sb("probT", [P, 2, HG, T])
        self.mx, self.spread = sb("mx", [P, TT, NA, HG]), sb("spread", [P, TT, NA, HG, DH])
        self.qp, self.kp = sb("qp", [P, HG, T]), sb("kp", [P, NA, HG, T])
        self.ones, self.rec = sb("ones", [P, P]), sb("rec", [P, NA, T])
        self.err, self.total = sb("err", [P, NA, T]), sb("total", [P, NA, HG, T])
        self.warm = sb("warm", [P, T], BF16)
        self.added, self.summed_up = sem("added"), sem("summed_up")
        self.ps = ctx.enter_context(nc.psum_tensor(prefix + "ps", [P, 8, T], F32))
        self.core_set, self.scored, self.max_done, self.spread_done = (sem(n) for n in ("core_set", "scored", "max_done", "spread_done"))
        self.max_cols, self.negm_act, self.negm_dve = sem("max_cols"), sem("negm_act"), sem("negm_dve")
        self.keys_scored, self.exp_done, self.refined, self.banks_free = (sem(n) for n in ("keys_scored", "exp_done", "refined", "banks_free"))
        self.product, self.ln_done, self.rec_done, self.cleared = sem("product"), sem("ln_done_core"), sem("rec_done"), sem("cleared")
        self.SET = 4 + NA * HG
        self.groups = [(i, a) for i in range(TT) for a in range(NA)]
        self.rows = [(h, a) for h in range(HG) for a in range(NA)]
        self.queries = [(i, a) for i in reversed(range(TT)) for a in range(NA)]

    def slot_of(self, h, a):
        return (h + 1 + a) % HG

    def setup(self, dve):
        nc = self.nc
        nc.vector.memset(self.warm[:], 0.0)
        nc.vector.memset(self.ones[:], 1.0).then_inc(self.core_set, 1)
        nc.vector.memset(self.spread[:], 0.0).then_inc(self.core_set, 1)
        nc.vector.memset(self.kp[:], 0.0).then_inc(self.core_set, 1)
        nc.vector.memset(self.qp[:], 0.0).then_inc(self.core_set, 1)
        dve.wait_ge(self.core_set, 4)
        for a in range(self.NA):
            for h in range(HG):
                r = DH * self.slot_of(h, a)
                nc.vector.memset(self.kp[r:r + 1, a, h, :], 1.0).then_inc(self.core_set, 1)
        dve.wait_ge(self.core_set, self.SET)
        dve.sem_inc(self.cleared, 1)

    def keep_warm(self, bank, n):
        for _ in range(n):
            self.nc.tensor.matmul(self.ps[:, bank, :], self.warm[:, 0:P], self.warm[:], start=True, stop=True)

    def tensor(self, pe, it, v, ident, identb, mask, maskT):
        nc, NA, NG = self.nc, self.NA, len(self.groups)
        slots = [slice(DH * h, DH * h + DH) for h in range(HG)]
        pe.wait_ge(self.cleared, it * (HG * NA) + 1)
        for m, (i, a) in enumerate(self.queries):
            L = (i + 1) * P if self.causal else T
            bank = 4 * (m % 2)
            if m == 1:
                pe.wait_ge(self.banks_free, it * 1 + 1)
            if m >= 2:
                pe.wait_ge(self.max_done, it * NG + m - 1)
            for h, sl in enumerate(slots):
                last = nc.tensor.matmul(self.ps[:, bank + self.slot_of(h, a), 0:L], self.qp[:, h, i * P:(i + 1) * P],
                                        self.kp[:, a, h, 0:L], start=True, stop=not self.causal)
            if self.causal:
                for h in range(HG):
                    last = nc.tensor.matmul(self.ps[:, bank + h, i * P:L], identb, mask, start=False, stop=True)
            last.then_inc(self.scored, 1)
        pe.wait_ge(self.max_done, it * NG + NG - 1)
        self.keep_warm(0, 3)
        pe.wait_ge(self.spread_done, it * 1 + 1)
        for a in range(NA):
            for i in range(TT):
                last = nc.tensor.transpose(self.ps[:, 6 + a, i * P:(i + 1) * P],
                                           self.spread[:, i, a, :, :].rearrange("p h d -> p (h d)"), ident)
        last.then_inc(self.max_cols, 1)
        self.keep_warm(4, 5)
        for n in range(NG + 1):
            if n < NG:
                kt, a = self.groups[n]
                q0 = kt * P if self.causal else 0
                for half in range(2):
                    if n:
                        pe.wait_ge(self.exp_done, it * (2 * NG) + 2 * n - 1 + half)
                    heads = (2 * half, 2 * half + 1)
                    for h in heads:
                        if n == 0:
                            pe.wait_ge(self.negm_act, it * (HG * NA // 2) + ((h + 1) * NA + 1) // 2)
                            if (h + 1) * NA // 2:
                                pe.wait_ge(self.negm_dve, it * (HG * NA // 2) + (h + 1) * NA // 2)
                        last = nc.tensor.matmul(self.ps[:, h, q0:T], self.kp[:, a, h, kt * P:(kt + 1) * P], self.qp[:, h, q0:T],
                                                start=True, stop=not self.causal)
                    if self.causal:
                        for h in heads:
                            last = nc.tensor.matmul(self.ps[:, h, q0:q0 + P], identb, maskT, start=False, stop=True)
                    last.then_inc(self.keys_scored, 1)
            if n:
                kt, a = self.groups[n - 1]
                q0 = kt * P if self.causal else 0
                pe.wait_ge(self.exp_done, it * (2 * NG) + 2 * n)
                for h, sl in enumerate(slots):
                    last = nc.tensor.matmul(self.ps[sl, 4 + a, q0:T], v[:, kt, sl], self.probT[:, (n - 1) % 2, h, q0:T],
                                            start=(kt == 0), stop=(kt == TT - 1))
                last.then_inc(self.product, 1)
        for a in range(NA):
            pe.wait_ge(self.added, it * NG + NG - NA + 1 + a)
            for h, sl in enumerate(slots):
                last = nc.tensor.matmul(self.ps[sl, 6 + a, :], self.ones[:, 0:DH], self.total[:, a, h, :], start=True, stop=True)
        last.then_inc(self.summed_up, 1)

    def scalar(self, act, it):
        nc, NG = self.nc, len(self.groups)
        act.wait_ge(self.max_cols, it * 1 + 1)
        for h, a in self.rows[0::2]:
            r = DH * self.slot_of(h, a)
            nc.scalar.activation(self.qp[r:r + 1, h, :], self.ps[r:r + 1, 6 + a, :], ACT.Copy).then_inc(self.negm_act, 1)
        for n, (kt, a) in enumerate(self.groups):
            q0 = kt * P if self.causal else 0
            if n >= 2:
                act.wait_ge(self.product, it * NG + n - 1)
                act.wait_ge(self.added, it * NG + n - 1)
            for half in range(2):
                heads = slice(2 * half, 2 * half + 2)
                act.wait_ge(self.keys_scored, it * (2 * NG) + 2 * n + half + 1)
                nc.scalar.activation(self.probT[:, n % 2, heads, q0:T], self.ps[:, heads, q0:T], ACT.Exp,
                                     scale=self.scale).then_inc(self.exp_done, 1)
        act.wait_ge(self.summed_up, it * 1 + 1)
        nc.scalar.activation(self.rec[:], self.ps[:, 6:6 + self.NA, :], ACT.Ln).then_inc(self.ln_done, 1)
        act.wait_ge(self.ln_done, it * 1 + 1)
        nc.scalar.activation(self.rec[:], self.rec[:], ACT.Exp, scale=-1.0).then_inc(self.rec_done, 1)

    def vector(self, dve, it):
        nc, NG = self.nc, len(self.groups)
        for m, (i, a) in enumerate(self.queries):
            L = (i + 1) * P if self.causal else T
            bank = 4 * (m % 2)
            dve.wait_ge(self.scored, it * NG + m + 1)
            nc.vector.tensor_reduce(self.mx[:, i, a, :], self.ps[:, bank:bank + HG, 0:L], AX, ALU.max).then_inc(self.max_done, 1)
        dve.wait_ge(self.max_done, it * NG + NG)
        nc.vector.tensor_scalar(self.spread[:, :, :, :, 0].rearrange("p i a h -> p (i a h)"),
                                self.mx[:].rearrange("p i a h -> p (i a h)"), -1.0, None, ALU.mult).then_inc(self.spread_done, 1)
        dve.wait_ge(self.max_cols, it * 1 + 1)
        for h, a in self.rows[1::2]:
            r = DH * self.slot_of(h, a)
            nc.vector.tensor_copy(self.qp[r:r + 1, h, :], self.ps[r:r + 1, 6 + a, :]).then_inc(self.negm_dve, 1)
        for n, (kt, a) in enumerate(self.groups):
            q0 = kt * P if self.causal else 0
            dve.wait_ge(self.exp_done, it * (2 * NG) + 2 * n + 2)
            if kt == 0:
                nc.vector.tensor_copy(self.total[:, a, :, :], self.probT[:, n % 2, :, :]).then_inc(self.added, 1)
            else:
                dve.wait_ge(self.added, it * NG + n - self.NA + 1)
                nc.vector.tensor_tensor(self.total[:, a, :, q0:T], self.total[:, a, :, q0:T], self.probT[:, n % 2, :, q0:T],
                                        ALU.add).then_inc(self.added, 1)
        dve.wait_ge(self.keys_scored, it * (2 * NG) + 2 * NG)
        for a in range(self.NA):
            for h in range(HG):
                r = DH * self.slot_of(h, a)
                nc.vector.memset(self.qp[r:r + 1, h, :], 0.0).then_inc(self.cleared, 1)
        dve.wait_ge(self.rec_done, it * 1 + 1)
        nc.vector.tensor_tensor(self.err[:], self.ps[:, 6:6 + self.NA, :], self.rec[:], ALU.mult).then_inc(self.refined, 1)
        dve.wait_ge(self.refined, it * 2 + 1)
        nc.vector.scalar_tensor_tensor(self.rec[:], self.err[:], -2.0, self.rec[:], op0=ALU.add, op1=ALU.mult).then_inc(self.refined, 1)
        dve.wait_ge(self.refined, it * 2 + 2)


def diff_attention_stage(nc, t, lambdas):
    with ExitStack() as ctx:
        sem = ctx.enter_context(Sems(nc, "da_"))

        def sb(name, shape, dt=F32):
            return ctx.enter_context(nc.sbuf_tensor("da_" + name, shape, dt))

        w = t.ahead[:].rearrange("p (n c f) -> p n c f", n=3, c=KD)
        wg = sb("wg", [P, 3, KD, P])
        hb = sb("hb", [P, KD, T])
        cs = sb("cs", [P, 2, T])
        swap, half = sb("swap", [P, P]), sb("half", [P, 2])
        qk, rot, sw, cc = sb("qk", [P, 2, T]), sb("rot", [P, 2, T]), sb("sw", [P, 2, T]), sb("cc", [P, 2, T])
        v = sb("v", [P, TT, P])
        identb, maskb = sb("identb", [P, P], BF16), sb("maskb", [P, P], BF16)
        maskf = sb("maskf", [P, 2, P])
        lam = sb("lam", [P, 4, DQ])
        lp, ls, le, nlam = sb("lp", [P, 2, DQ]), sb("ls", [P, 2]), sb("le", [P, 2]), sb("nlam", [P, 2])
        o1, o2, aT, maskTb = sb("o1", [P, T]), sb("o2", [P, T]), sb("aT", [P, T]), sb("maskTb", [P, P], BF16)
        core = AttentionCore(nc, ctx, sem, "da_", 2, float(DQ) ** -0.5, True)
        const_in, hb_in, w_free = sem("const_in"), sem("hb_in"), sem("w_free")
        const_ready, lstep = sem("const_ready"), sem("lstep")
        projected, v_done, raw, v_ready = sem("projected"), sem("v_done"), sem("raw"), sem("v_ready")
        swapped, cosed, sined, rotated, keys_ready, keys2_ready = (sem(n) for n in (
            "swapped", "cosed", "sined", "rotated", "keys_ready", "keys2_ready"))
        scaled, aT_ready, a_psum, a_written = sem("scaled"), sem("aT_ready"), sem("a_psum"), core.banks_free
        block = ctx.enter_context(nc.Block())
        N_C = 16 * (1 + 1 + 1 + 1 + 4)
        NIT, NG = B * KD, len(core.groups)

        @block.sync
        def _(sp):
            sp.dma_start(cs[:], t.const["cs"].rearrange("a p t -> p a t")).then_inc(const_in, 16)
            sp.dma_start(swap[:], t.const["swap"]).then_inc(const_in, 16)
            sp.dma_start(half[:], t.const["half"]).then_inc(const_in, 16)
            sp.dma_start(maskf[:], t.const["mask"].rearrange("a p c -> p a c")).then_inc(const_in, 16)
            for n, l in enumerate(lambdas):
                sp.dma_start(lam[:, n, :], l.unsqueeze(0).broadcast_to([P, DQ])).then_inc(const_in, 16)

            with sp.Fori(0, B) as b:
                with sp.Fori(0, KD) as g:
                    sp.wait_ge(w_free, b * KD + g + 1)
                    sp.dma_start(hb[:], t.hsT[:, :, bass.ds(b, 1), :].rearrange("p k o t -> p (k o) t")).then_inc(hb_in, 16)
                    for n in range(3):
                        sp.dma_start(wg[:, n, :, :], w[:, n, :, bass.ds(g * P, P)]).then_inc(hb_in, 16)

        @block.gpsimd
        def _(pool):
            pool.wait_ge(const_in, N_C)
            with pool.Fori(0, NIT) as it:
                for n in (1, 0):
                    pool.wait_ge(raw, it * 2 + (2 - n))
                    nc.gpsimd.tensor_tensor(cc[:, n, :], qk[:, n, :], cs[:, 0, :], ALU.mult).then_inc(cosed, 1)

        @block.tensor
        def _(pe):
            pe.wait_ge(const_ready, 3)
            pe.wait_ge(core.core_set, core.SET)

            def project(it):
                pe.wait_ge(hb_in, it * 64 + 64)
                for n in (1, 0):
                    for k in range(KD):
                        last = nc.tensor.matmul(core.ps[:, n, :], wg[:, n, k, :], hb[:, k, :], start=(k == 0), stop=(k == KD - 1))
                    last.then_inc(projected, 1)
                for n in (1, 0):
                    pe.wait_ge(raw, it * 2 + (2 - n))
                    nc.tensor.matmul(core.ps[:, 3 - n, :], swap[:], qk[:, n, :], start=True, stop=True).then_inc(swapped, 1)
                for tt in range(TT):
                    for k in range(KD):
                        last = nc.tensor.matmul(core.ps[:, 1, tt * P:(tt + 1) * P], hb[:, k, tt * P:(tt + 1) * P],
                                                wg[:, 2, k, :], start=(k == 0), stop=(k == KD - 1))
                last.then_inc(v_done, 1)

            def attend(it):
                pe.wait_ge(keys_ready, it * (HG + 2) + HG + 2)
                pe.wait_ge(keys2_ready, it * (HG + 2) + HG + 2)
                pe.wait_ge(v_ready, it * 1 + 1)
                core.tensor(pe, it, v, t.ident[:], identb[:], maskb[:], maskTb[:])

            def output(it):
                pe.wait_ge(aT_ready, it * 1 + 1)
                for i in range(TT):
                    last = nc.tensor.transpose(core.ps[:, 4, i * P:(i + 1) * P], aT[:, i * P:(i + 1) * P], t.ident[:])
                last.then_inc(a_psum, 1)
                core.keep_warm(5, 4)

            project(0)
            with pe.Fori(0, NIT - 1) as it:
                attend(it)
                pe.wait_ge(core.exp_done, it * (2 * NG) + 2 * NG)
                project(it + 1)
                output(it)
            attend(NIT - 1)
            output(NIT - 1)

        @block.scalar
        def _(act):
            nc.scalar.preload_act_table_set("natural_log_exp_and_others")
            act.wait_ge(lstep, 2)
            nc.scalar.activation(le[:], ls[:], ACT.Exp).then_inc(lstep, 1)

            def project(it):
                for n in (1, 0):
                    act.wait_ge(projected, it * 2 + (2 - n))
                    nc.scalar.activation(qk[:, n, :], core.ps[:, n, :], ACT.Copy).then_inc(raw, 1)

            def second_keys(it):
                act.wait_ge(rotated, it * 2 + 1)
                for h in range(HG):
                    sl = slice(DH * h, DH * h + DH)
                    nc.scalar.activation(core.kp[sl, 1, h, :], rot[sl, 1, :], ACT.Copy, scale=half[sl, 1:2]).then_inc(keys2_ready, 1)
                act.wait_ge(rotated, it * 2 + 2)
                act.wait_ge(core.cleared, it * (HG * 2) + 1)
                for h in (0, 1):
                    sl = slice(DH * h, DH * h + DH)
                    nc.scalar.activation(core.qp[sl, h, :], rot[sl, 0, :], ACT.Copy).then_inc(keys2_ready, 1)
                act.wait_ge(v_done, it * 1 + 1)
                nc.scalar.activation(v[:].rearrange("p t d -> p (t d)"), core.ps[:, 1, :], ACT.Copy).then_inc(v_ready, 1)
                act.wait_ge(v_ready, it * 1 + 1)
                act.sem_inc(w_free, 1)

            def output(it):
                act.wait_ge(a_psum, it * 1 + 1)
                nc.scalar.activation(t.A[:].rearrange("p i b f -> p i (b f)")[:, :, bass.ds(it * P, P)],
                                     core.ps[:, 4, :].rearrange("p (i f) -> p i f", f=P), ACT.Copy).then_inc(a_written, 1)

            project(0)
            second_keys(0)
            with act.Fori(0, NIT - 1) as it:
                core.scalar(act, it)
                project(it + 1)
                second_keys(it + 1)
                output(it)
            core.scalar(act, NIT - 1)
            output(NIT - 1)

        @block.vector
        def _(dve):
            dve.sem_inc(w_free, 1)
            dve.sem_inc(a_written, 1)
            core.setup(dve)
            dve.wait_ge(const_in, N_C)
            nc.vector.tensor_copy(maskb[:], maskf[:, 0, :]).then_inc(const_ready, 1)
            nc.vector.tensor_copy(maskTb[:], maskf[:, 1, :]).then_inc(const_ready, 1)
            nc.vector.tensor_copy(identb[:], t.ident[:]).then_inc(const_ready, 1)
            nc.vector.tensor_tensor(lp[:], lam[:, 0:4:2, :], lam[:, 1:4:2, :], ALU.mult).then_inc(lstep, 1)
            dve.wait_ge(lstep, 1)
            nc.vector.tensor_reduce(ls[:], lp[:], AX, ALU.add).then_inc(lstep, 1)
            dve.wait_ge(lstep, 3)
            nc.vector.tensor_tensor(nlam[:, 0:1], le[:, 1:2], le[:, 0:1], ALU.subtract).then_inc(lstep, 1)
            dve.wait_ge(lstep, 4)
            nc.vector.tensor_scalar(nlam[:, 1:2], nlam[:, 0:1], -LAMBDA_INIT, None, ALU.add).then_inc(lstep, 1)
            dve.wait_ge(lstep, 5)

            def project(it):
                for n in (1, 0):
                    dve.wait_ge(swapped, it * 2 + (2 - n))
                    nc.vector.tensor_tensor(sw[:, n, :], core.ps[:, 3 - n, :], cs[:, 1, :], ALU.mult).then_inc(sined, 1)
                    dve.wait_ge(sined, it * 2 + (2 - n))
                    dve.wait_ge(cosed, it * 2 + (2 - n))
                    nc.vector.tensor_tensor(rot[:, n, :], sw[:, n, :], cc[:, n, :], ALU.add).then_inc(rotated, 1)
                dve.wait_ge(rotated, it * 2 + 2)
                for h in range(HG):
                    sl = slice(DH * h, DH * h + DH)
                    nc.vector.tensor_scalar(core.kp[sl, 0, h, :], rot[sl, 1, :], half[sl, 0:1], None, ALU.mult).then_inc(keys_ready, 1)
                for h in (2, 3):
                    sl = slice(DH * h, DH * h + DH)
                    nc.vector.tensor_copy(core.qp[sl, h, :], rot[sl, 0, :]).then_inc(keys_ready, 1)

            def attend(it):
                core.vector(dve, it)
                for n, o in enumerate((o1, o2)):
                    nc.vector.scalar_tensor_tensor(o[:], core.ps[:, 4 + n, :], -1.0, core.rec[:, n, :],
                                                   op0=ALU.mult, op1=ALU.mult).then_inc(scaled, 1)
                dve.wait_ge(scaled, it * 2 + 2)
                nc.vector.scalar_tensor_tensor(aT[:], o2[:], nlam[:, 1:2], o1[:], op0=ALU.mult, op1=ALU.add).then_inc(aT_ready, 1)

            project(0)
            with dve.Fori(0, NIT - 1) as it:
                attend(it)
                project(it + 1)
            attend(NIT - 1)


def filter_stage(nc, t, x, Wout, rms_weight, cond, W_emb, b_emb, g_norm, W_qkv):
    with ExitStack() as ctx:
        sem = ctx.enter_context(Sems(nc, "fi_"))

        def sb(name, shape, dt=F32):
            return ctx.enter_context(nc.sbuf_tensor("fi_" + name, shape, dt))

        filt, wout, wemb = sb("filt", [P, TT, T]), sb("wout", [P, KD, D]), sb("wemb", [P, KD, 2 * D])
        rmsw, condT, bg = sb("rmsw", [P, 1, D]), sb("condT", [P, KD, B]), sb("bg", [P, 3, KD])
        gs1, gain, shift = sb("gs1", [P, KD, B]), sb("gain", [P, KD, B]), sb("shift", [P, KD, B])
        xb = sb("xb", [P, TT, D])
        sq, y, yT = sb("sq", [P, TT, D]), sb("y", [P, TT, D]), sb("yT", [P, KD, T])
        ss, rs = sb("ss", [P, TT * H]), sb("rs", [P, TT * H])
        s2, r2 = sb("s2", [P, TT]), sb("r2", [P, TT])
        gain_b, shift_b = sb("gain_b", [P, KD]), sb("shift_b", [P, KD])
        pf = ctx.enter_context(nc.psum_tensor("fi_pf", [P, 4, 512], F32))
        pt = ctx.enter_context(nc.psum_tensor("fi_pt", [P, 4, 512], F32))
        const_in, x_in, ahead_in = sem("const_in"), sem("x_in"), sem("ahead_in")
        emb_done, gain_step, gain_ready = sem("emb_done"), sem("gain_step"), sem("gain_ready")
        filtered, squared, ss_done, ms_done, ln_done, rs_done = (sem(n) for n in (
            "filtered", "squared", "ss_done", "ms_done", "ln_done", "rs_done"))
        y1_done, y_ready, yT_psum, yT_act, yT_dve = (sem(n) for n in ("y1_done", "y_ready", "yT_psum", "yT_act", "yT_dve"))
        out_done, x1_ready, sq2, ms2, ln2, rs2 = (sem(n) for n in ("out_done", "x1_ready", "sq2", "ms2", "ln2", "rs2"))
        normed, nT_psum, nT_act, nT_dve = sem("normed"), sem("nT_psum"), sem("nT_act"), sem("nT_dve")
        block = ctx.enter_context(nc.Block())
        N_C = 16 * (4 + KD + 3)

        @block.sync
        def _(sp):
            sp.dma_start(filt[:], t.const["filt"].rearrange("(s p) t -> p s t", p=P)).then_inc(const_in, 16)
            sp.dma_start(wout[:], Wout.rearrange("(k p) n -> p k n", p=P)).then_inc(const_in, 16)
            sp.dma_start(wemb[:], W_emb.rearrange("(k p) n -> p k n", p=P)).then_inc(const_in, 16)
            rms_row = rms_weight.rearrange("(a h d) -> a h d", a=1, h=1)
            sp.dma_start(rmsw[:].rearrange("p o (h d) -> p (o h) d", h=H), rms_row.broadcast_to([P, H, DH])).then_inc(const_in, 16)
            for k in range(KD):
                sp.dma_start(condT[:, k, :], cond[:, k * P:(k + 1) * P].rearrange("b p -> p b"),
                             allow_slow_non_contiguous=True).then_inc(const_in, 16)
            for n, vec in enumerate((b_emb[0:D], b_emb[D:2 * D], g_norm)):
                sp.dma_start(bg[:, n, :], vec.rearrange("(k p) -> p k", p=P), allow_slow_non_contiguous=True).then_inc(const_in, 16)
            sp.dma_start(xb[:], x[0].rearrange("(tt p) d -> p tt d", p=P)).then_inc(x_in, 16)
            sp.dma_start(t.ahead[:].rearrange("p (k n) -> p k n", k=KD), W_qkv.rearrange("(k p) n -> p k n", p=P)).then_inc(ahead_in, 16)
            with sp.Fori(1, B) as b:
                sp.wait_ge(x1_ready, b * TT)
                sp.dma_start(xb[:], x[bass.ds(b, 1), :, :].rearrange("o (tt p) d -> p (o tt) d", p=P)).then_inc(x_in, 16)
            sp.wait_ge(ahead_in, 16)

        @block.tensor
        def _(pe):
            pe.wait_ge(const_in, N_C)
            for c in range(2 * KD):
                for k in range(KD):
                    last = nc.tensor.matmul(pf[:, 0, c * B:(c + 1) * B], wemb[:, k, c * P:(c + 1) * P], condT[:, k, :],
                                            start=(k == 0), stop=(k == KD - 1))
            last.then_inc(emb_done, 1)
            pe.wait_ge(gain_ready, 3)
            with pe.Fori(0, B) as b:
                for tt in range(TT):
                    for s in range(TT):
                        last = nc.tensor.matmul(pf[:, tt, :], filt[:, s, tt * P:(tt + 1) * P],
                                                t.A[:, s, bass.ds(b, 1), :].rearrange("p o f -> p (o f)"),
                                                start=(s == 0), stop=(s == TT - 1))
                    last.then_inc(filtered, 1)
                pe.wait_ge(y_ready, b * TT + TT)
                for k in range(KD):
                    for tt in range(TT):
                        last = nc.tensor.transpose(pt[:, k, tt * P:(tt + 1) * P], y[:, tt, k * P:(k + 1) * P], t.ident[:])
                    last.then_inc(yT_psum, 1)
                pe.wait_ge(yT_act, b * 2 + 2)
                pe.wait_ge(yT_dve, b * 2 + 2)
                for tt in range(TT):
                    for k in range(KD):
                        last = nc.tensor.matmul(pf[:, tt, :], yT[:, k, tt * P:(tt + 1) * P], wout[:, k, :],
                                                start=(k == 0), stop=(k == KD - 1))
                    last.then_inc(out_done, 1)
                pe.wait_ge(normed, b * TT + TT)
                for k in range(KD):
                    for tt in range(TT):
                        last = nc.tensor.transpose(pt[:, k, tt * P:(tt + 1) * P], y[:, tt, k * P:(k + 1) * P], t.ident[:])
                    last.then_inc(nT_psum, 1)
                pe.wait_ge(nT_act, b * 2 + 2)
                pe.wait_ge(nT_dve, b * 2 + 2)

        @block.scalar
        def _(act):
            nc.scalar.preload_act_table_set("natural_log_exp_and_others")
            act.wait_ge(gain_ready, 3)
            with act.Fori(0, B) as b:
                for tt in range(TT + 1):
                    if tt < TT:
                        act.wait_ge(filtered, b * TT + tt + 1)
                        nc.scalar.activation(sq[:, tt, :], pf[:, tt, :], ACT.Square).then_inc(squared, 1)
                    if tt:
                        part = slice((tt - 1) * H, tt * H)
                        act.wait_ge(ms_done, b * TT + tt)
                        nc.scalar.activation(rs[:, part], ss[:, part], ACT.Ln).then_inc(ln_done, 1)
                        act.wait_ge(ln_done, b * TT + tt)
                        nc.scalar.activation(rs[:, part], rs[:, part], ACT.Exp, scale=-0.5).then_inc(rs_done, 1)
                for k in (0, 2):
                    act.wait_ge(yT_psum, b * KD + k + 1)
                    nc.scalar.activation(yT[:, k, :], pt[:, k, :], ACT.Copy).then_inc(yT_act, 1)
                for tt in range(TT):
                    act.wait_ge(x1_ready, b * TT + tt + 1)
                    nc.scalar.activation(sq[:, tt, :], t.x1[:, bass.ds(b * TT + tt, 1), :].rearrange("p o d -> p (o d)"),
                                         ACT.Square, accum_out=s2[:, tt:tt + 1]).then_inc(sq2, 1)
                act.wait_ge(ms2, b * 1 + 1)
                nc.scalar.activation(r2[:], s2[:], ACT.Ln).then_inc(ln2, 1)
                act.wait_ge(ln2, b * 1 + 1)
                nc.scalar.activation(r2[:], r2[:], ACT.Exp, scale=-0.5).then_inc(rs2, 1)
                for k in (0, 2):
                    act.wait_ge(nT_psum, b * KD + k + 1)
                    nc.scalar.activation(t.xnT[:, bass.ds(b, 1), k, :].rearrange("p o t -> p (o t)"), pt[:, k, :], ACT.Identity,
                                         bias=shift_b[:, k:k + 1], scale=gain_b[:, k:k + 1]).then_inc(nT_act, 1)

        @block.vector
        def _(dve):
            dve.wait_ge(emb_done, 1)
            sc = pf[:, 0, 0:KD * B].rearrange("p (k b) -> p k b", b=B)
            sh = pf[:, 0, KD * B:2 * KD * B].rearrange("p (k b) -> p k b", b=B)
            nc.vector.tensor_tensor(gs1[:], sc, bg[:, 0, :].unsqueeze(2).broadcast_to([P, KD, B]), ALU.add).then_inc(gain_step, 1)
            nc.vector.tensor_tensor(shift[:], sh, bg[:, 1, :].unsqueeze(2).broadcast_to([P, KD, B]), ALU.add).then_inc(gain_ready, 1)
            dve.wait_ge(gain_step, 1)
            nc.vector.scalar_tensor_tensor(gain[:], gs1[:], 1.0, bg[:, 2, :].unsqueeze(2).broadcast_to([P, KD, B]),
                                           op0=ALU.add, op1=ALU.mult).then_inc(gain_ready, 1)
            nc.vector.tensor_scalar(rmsw[:], rmsw[:], 1.0 - LAMBDA_INIT, None, ALU.mult).then_inc(gain_ready, 1)
            dve.wait_ge(gain_ready, 3)
            heads = "p (h d) -> p h d"
            with dve.Fori(0, B) as b:
                for tt in range(TT + 1):
                    if tt < TT:
                        part = slice(tt * H, (tt + 1) * H)
                        dve.wait_ge(squared, b * TT + tt + 1)
                        nc.vector.tensor_reduce(ss[:, part], sq[:, tt, :].rearrange(heads, h=H), AX, ALU.add).then_inc(ss_done, 1)
                        dve.wait_ge(ss_done, b * TT + tt + 1)
                        nc.vector.tensor_scalar(ss[:, part], ss[:, part], 1.0 / DH, 1e-5, ALU.mult, ALU.add).then_inc(ms_done, 1)
                    if tt:
                        u = tt - 1
                        dve.wait_ge(rs_done, b * TT + tt)
                        nc.vector.tensor_tensor(y[:, u, :].rearrange(heads, h=H), pf[:, u, :].rearrange(heads, h=H),
                                                rs[:, u * H:tt * H].unsqueeze(2).broadcast_to([P, H, DH]), ALU.mult).then_inc(y1_done, 1)
                        dve.wait_ge(y1_done, b * TT + tt)
                        nc.vector.tensor_tensor(y[:, u, :], y[:, u, :], rmsw[:, 0, :], ALU.mult).then_inc(y_ready, 1)
                for k in (1, 3):
                    dve.wait_ge(yT_psum, b * KD + k + 1)
                    nc.vector.tensor_copy(yT[:, k, :], pt[:, k, :]).then_inc(yT_dve, 1)
                dve.wait_ge(x_in, b * 16 + 16)
                for tt in range(TT):
                    dve.wait_ge(out_done, b * TT + tt + 1)
                    nc.vector.tensor_tensor(t.x1[:, bass.ds(b * TT + tt, 1), :].rearrange("p o d -> p (o d)"), pf[:, tt, :],
                                            xb[:, tt, :], ALU.add).then_inc(x1_ready, 1)
                nc.vector.tensor_copy(gain_b[:], gain[:, :, bass.ds(b, 1)].rearrange("p k o -> p (k o)"))
                nc.vector.tensor_copy(shift_b[:], shift[:, :, bass.ds(b, 1)].rearrange("p k o -> p (k o)"))
                dve.wait_ge(sq2, b * TT + TT)
                nc.vector.tensor_scalar(s2[:], s2[:], 1.0 / D, 1e-6, ALU.mult, ALU.add).then_inc(ms2, 1)
                dve.wait_ge(rs2, b * 1 + 1)
                for tt in range(TT):
                    nc.vector.tensor_scalar(y[:, tt, :], t.x1[:, bass.ds(b * TT + tt, 1), :].rearrange("p o d -> p (o d)"),
                                            r2[:, tt:tt + 1], None, ALU.mult).then_inc(normed, 1)
                for k in (1, 3):
                    dve.wait_ge(nT_psum, b * KD + k + 1)
                    nc.vector.tensor_scalar(t.xnT[:, bass.ds(b, 1), k, :].rearrange("p o t -> p (o t)"), pt[:, k, :],
                                            gain_b[:, k:k + 1], shift_b[:, k:k + 1], ALU.mult, ALU.add).then_inc(nT_dve, 1)


def full_attention_stage(nc, t, g_q, g_k):
    with ExitStack() as ctx:
        sem = ctx.enter_context(Sems(nc, "fa_"))

        def sb(name, shape, dt=F32):
            return ctx.enter_context(nc.sbuf_tensor("fa_" + name, shape, dt))

        w = t.ahead[:].rearrange("p (k n) -> p k n", k=KD)
        wg, hb = sb("wg", [P, 3, KD, P]), sb("hb", [P, KD, T])
        ones, g = sb("headones", [P, P]), sb("g", [P, 2])
        sq, rs, v = sb("sq", [P, 2, T]), sb("rs", [P, 2, T]), sb("v", [P, TT, P])
        eps, qn = sb("eps", [P, 1]), sb("qn", [P, T])
        q_normed, q_act = sem("q_normed"), sem("q_act")
        core = AttentionCore(nc, ctx, sem, "fa_", 1, float(DH) ** -0.5, False)
        oT_written = core.banks_free
        const_in, hb_in, w_free, eps_set = sem("const_in"), sem("hb_in"), sem("w_free"), sem("eps_set")
        projected, v_done, v_ready, squared, summed, ln_done, rs_done, qk_ready = (sem(n) for n in (
            "projected", "v_done", "v_ready", "squared", "summed", "ln_done", "rs_done", "qk_ready"))
        block = ctx.enter_context(nc.Block())
        N_C = 16 * (1 + 2 * HG)
        NIT, NG = B * KD, len(core.groups)

        @block.sync
        def _(sp):
            sp.dma_start(ones[:], t.const["headones"]).then_inc(const_in, 16)
            for n, vec in enumerate((g_q, g_k)):
                for h in range(HG):
                    sp.dma_start(g[DH * h:DH * h + DH, n:n + 1], vec.unsqueeze(1)).then_inc(const_in, 16)
            with sp.Fori(0, B) as b:
                with sp.Fori(0, KD) as gg:
                    sp.wait_ge(w_free, b * KD + gg + 1)
                    sp.dma_start(hb[:], t.xnT[:, bass.ds(b, 1), :, :].rearrange("p o k t -> p (o k) t")).then_inc(hb_in, 16)
                    for n in range(3):
                        sp.dma_start(wg[:, n, :, :], w[:, :, bass.ds(gg * P + n * D, P)]).then_inc(hb_in, 16)

        @block.tensor
        def _(pe):
            pe.wait_ge(const_in, N_C)
            pe.wait_ge(core.core_set, core.SET)

            def project(it):
                pe.wait_ge(hb_in, it * 64 + 64)
                def sum_squares(n):
                    pe.wait_ge(squared, it * 2 + (2 - n))
                    nc.tensor.matmul(core.ps[:, 3 - n, :], ones[:], sq[:, n, :], start=True, stop=True).then_inc(summed, 1)

                for n in (1, 0):
                    for k in range(KD):
                        last = nc.tensor.matmul(core.ps[:, n, :], wg[:, n, k, :], hb[:, k, :], start=(k == 0), stop=(k == KD - 1))
                        if n == 0 and k == 0:
                            sum_squares(1)
                    last.then_inc(projected, 1)
                sum_squares(0)
                for tt in range(TT):
                    for k in range(KD):
                        last = nc.tensor.matmul(core.ps[:, 5, tt * P:(tt + 1) * P], hb[:, k, tt * P:(tt + 1) * P],
                                                wg[:, 2, k, :], start=(k == 0), stop=(k == KD - 1))
                last.then_inc(v_done, 1)

            def attend(it):
                pe.wait_ge(qk_ready, it * (HG + 2) + HG + 2)
                pe.wait_ge(q_act, it * 2 + 2)
                pe.wait_ge(v_ready, it * 1 + 1)
                core.tensor(pe, it, v, t.ident[:], None, None, None)

            project(0)
            with pe.Fori(0, NIT - 1) as it:
                attend(it)
                pe.wait_ge(core.exp_done, it * (2 * NG) + 2 * NG)
                project(it + 1)
            attend(NIT - 1)

        @block.scalar
        def _(act):
            nc.scalar.preload_act_table_set("natural_log_exp_and_others")
            act.wait_ge(eps_set, 1)

            def project(it):
                for n in (1, 0):
                    act.wait_ge(projected, it * 2 + (2 - n))
                    nc.scalar.activation(sq[:, n, :], core.ps[:, n, :], ACT.Square).then_inc(squared, 1)
                    act.wait_ge(summed, it * 2 + (2 - n))
                    nc.scalar.activation(rs[:, n, :], core.ps[:, 3 - n, :], ACT.Ln, bias=eps[:, 0:1], scale=1.0 / DH).then_inc(ln_done, 1)
                    act.wait_ge(ln_done, it * 2 + (2 - n))
                    nc.scalar.activation(rs[:, n, :], rs[:, n, :], ACT.Exp, scale=-0.5).then_inc(rs_done, 1)
                act.wait_ge(core.cleared, it * HG + 1)
                act.wait_ge(q_normed, it * 1 + 1)
                for h in (0, 1):
                    sl = slice(DH * h, DH * h + DH)
                    nc.scalar.activation(core.qp[sl, h, :], qn[sl, :], ACT.Copy).then_inc(q_act, 1)
                act.wait_ge(v_done, it * 1 + 1)
                nc.scalar.activation(v[:].rearrange("p t d -> p (t d)"), core.ps[:, 5, :], ACT.Copy).then_inc(v_ready, 1)
                act.wait_ge(v_ready, it * 1 + 1)
                act.sem_inc(w_free, 1)

            project(0)
            with act.Fori(0, NIT - 1) as it:
                core.scalar(act, it)
                project(it + 1)
            core.scalar(act, NIT - 1)

        @block.vector
        def _(dve):
            nc.vector.memset(eps[:], 1e-6).then_inc(eps_set, 1)
            dve.sem_inc(w_free, 1)
            dve.sem_inc(oT_written, 1)
            core.setup(dve)
            dve.wait_ge(const_in, N_C)

            def project(it):
                dve.wait_ge(rs_done, it * 2 + 1)
                for h in range(HG):
                    sl = slice(DH * h, DH * h + DH)
                    nc.vector.scalar_tensor_tensor(core.kp[sl, 0, h, :], core.ps[sl, 1, :], g[sl, 1:2], rs[sl, 1, :],
                                                   op0=ALU.mult, op1=ALU.mult).then_inc(qk_ready, 1)
                dve.wait_ge(rs_done, it * 2 + 2)
                nc.vector.scalar_tensor_tensor(qn[:], core.ps[:, 0, :], g[:, 0:1], rs[:, 0, :],
                                               op0=ALU.mult, op1=ALU.mult).then_inc(q_normed, 1)
                dve.wait_ge(q_normed, it * 1 + 1)
                for h in (2, 3):
                    sl = slice(DH * h, DH * h + DH)
                    nc.vector.tensor_copy(core.qp[sl, h, :], qn[sl, :]).then_inc(qk_ready, 1)

            def attend(it, b, k):
                core.vector(dve, it)
                nc.vector.scalar_tensor_tensor(t.oT[:, k, b, :].rearrange("p k o t -> p (k o t)"), core.ps[:, 4, :], -1.0,
                                               core.rec[:, 0, :], op0=ALU.mult, op1=ALU.mult).then_inc(oT_written, 1)

            project(0)
            with dve.Fori(0, B - 1) as b:
                with dve.Fori(0, KD) as k:
                    attend(b * KD + k, bass.ds(b, 1), bass.ds(k, 1))
                    project(b * KD + k + 1)
            with dve.Fori(0, KD - 1) as k:
                attend(k + (B - 1) * KD, slice(B - 1, B), bass.ds(k, 1))
                project(k + (B - 1) * KD + 1)
            attend(NIT - 1, slice(B - 1, B), slice(KD - 1, KD))


def route_stage(nc, t, W_out, gate_w, sg_w, su_w, sd_w):
    with ExitStack() as ctx:
        sem = ctx.enter_context(Sems(nc, "ro_"))

        def sb(name, shape, dt=F32):
            return ctx.enter_context(nc.sbuf_tensor("ro_" + name, shape, dt))

        NC = SI // P
        wout, stage = sb("wout", [P, KD, D]), sb("stage", [P, 4, D])
        gwT, sgT, suT, sdT = sb("gwT", [P, KD, E]), sb("sgT", [P, KD, SI]), sb("suT", [P, KD, SI]), sb("sdT", [P, NC, D])
        sdraw = sb("sdraw", [P, KD, SI])
        ob, yT, yb = sb("ob", [P, KD, T]), sb("yT", [P, KD, T]), sb("yb", [P, 2, TT, D])
        sil, hT = sb("sil", [P, 2, T]), sb("hT", [P, NC, T])
        lf, before, ones, carry = sb("lf", [P, P]), sb("before", [P, P], BF16), sb("ones", [P, P], BF16), sb("carry", [P, E], BF16)
        iota = sb("iota", [P, E])
        lg, v8, i8 = sb("lg", [P, TT, E]), sb("v8", [P, TT, 8]), sb("i8", [P, TT, 8], U32)
        nv, ex, se, ev, rs = sb("nv", [P, TT]), sb("ex", [P, TT, E]), sb("se", [P, TT]), sb("ev", [P, TT, 8]), sb("rs", [P, TT])
        ef, oh, mask = sb("ef", [P, TT * K]), sb("oh", [P, TT * K, E], BF16), sb("mask", [P, TT, E], BF16)
        posb, pr, pk, valid, sf = sb("posb", [P, TT, E], BF16), sb("pr", [P, TT * K, E]), sb("pk", [P, TT * K]), sb("valid", [P, TT * K]), sb("sf", [P, TT * K])
        slot = sb("slot", [P, TT * K], U32)
        pa = ctx.enter_context(nc.psum_tensor("ro_pa", [P, 4, 512], F32))
        pb = ctx.enter_context(nc.psum_tensor("ro_pb", [P, 4, 512], F32))
        names = """const_in raw_in zeroed setup_psum setup_copied ready ob_in y_psum y_ready
            yT_psum yT_act yT_dve logits gates ups silued hidden down_done added lg_copied top8 found nv_done
            exps e_done rs_done w1_done cast1 onehot masked mask_ready placed prod_done pk_done valid_done base_done
            base2_done sf_done tick slots_ready scattered w_done carried ld""".split()
        S = {n: sem(n) for n in names}
        block = ctx.enter_context(nc.Block())
        N_C = 16 * 3

        @block.sync
        def _(sp):
            sp.dma_start(wout[:], W_out.rearrange("(k p) n -> p k n", p=P)).then_inc(S["const_in"], 16)
            sp.dma_start(lf[:], t.const["before"]).then_inc(S["const_in"], 16)
            sp.dma_start(iota[:], t.const["iota"].unsqueeze(0).broadcast_to([P, E])).then_inc(S["const_in"], 16)
            sp.dma_start(stage[0:E, 0, :], gate_w).then_inc(S["raw_in"], 16)
            sp.dma_start(stage[:, 1:4, :], sg_w.rearrange("(c p) n -> p c n", p=P)).then_inc(S["raw_in"], 16)
            sp.dma_start(sdraw[:], sd_w.rearrange("(k p) n -> p k n", p=P)).then_inc(S["raw_in"], 16)
            sp.wait_ge(S["setup_copied"], 2 * KD)
            sp.dma_start(stage[:, 1:4, :], su_w.rearrange("(c p) n -> p c n", p=P)).then_inc(S["raw_in"], 16)
            with sp.Fori(0, B) as b:
                sp.wait_ge(S["ld"], b * 1 + 1)
                sp.dma_start(ob[:], t.oT[:, :, bass.ds(b, 1), :].rearrange("p k o t -> p (k o) t")).then_inc(S["ob_in"], 16)

        @block.tensor
        def _(pe):
            pe.wait_ge(S["raw_in"], 48)
            for k in range(KD):
                nc.tensor.transpose(pa[:, k, 0:E], stage[0:E, 0, k * P:(k + 1) * P], t.ident[0:E, 0:E]).then_inc(S["setup_psum"], 1)
            for k in range(KD):
                for c in range(NC):
                    last = nc.tensor.transpose(pb[:, k, c * P:(c + 1) * P], stage[:, 1 + c, k * P:(k + 1) * P], t.ident[:])
                last.then_inc(S["setup_psum"], 1)
            pe.wait_ge(S["setup_copied"], 2 * KD)
            for c in range(NC):
                for k in range(KD):
                    last = nc.tensor.transpose(pa[:, c, k * P:(k + 1) * P], sdraw[:, k, c * P:(c + 1) * P], t.ident[:])
                last.then_inc(S["setup_psum"], 1)
            pe.wait_ge(S["raw_in"], 64)
            for k in range(KD):
                for c in range(NC):
                    last = nc.tensor.transpose(pb[:, k, c * P:(c + 1) * P], stage[:, 1 + c, k * P:(k + 1) * P], t.ident[:])
                last.then_inc(S["setup_psum"], 1)
            pe.wait_ge(S["setup_copied"], 3 * KD + NC)
            pe.wait_ge(S["ready"], 3 + KD)
            def batch(b, y):
                pe.wait_ge(S["ob_in"], b * 16 + 16)
                for tt in range(TT):
                    for k in range(KD):
                        last = nc.tensor.matmul(pb[:, tt, :], ob[:, k, tt * P:(tt + 1) * P], wout[:, k, :], start=(k == 0), stop=(k == KD - 1))
                    last.then_inc(S["y_psum"], 1)
                pe.wait_ge(S["y_ready"], b * TT + TT)
                pe.wait_ge(S["prod_done"], b * 1 + 1)
                for k in range(KD):
                    for tt in range(TT):
                        last = nc.tensor.transpose(pa[:, k, tt * P:(tt + 1) * P], yb[:, y, tt, k * P:(k + 1) * P], t.ident[:])
                    last.then_inc(S["yT_psum"], 1)
                pe.wait_ge(S["yT_act"], b * 2 + 2)
                pe.wait_ge(S["yT_dve"], b * 2 + 2)
                for tt in range(TT):
                    for k in range(KD):
                        last = nc.tensor.matmul(pb[:, 0, tt * E:(tt + 1) * E], yT[:, k, tt * P:(tt + 1) * P], gwT[:, k, :], start=(k == 0), stop=(k == KD - 1))
                last.then_inc(S["logits"], 1)
                for c in range(NC):
                    if c >= 2:
                        pe.wait_ge(S["hidden"], b * NC + c - 1)
                    for wT, n, done in ((sgT, 0, "gates"), (suT, 1, "ups")):
                        for k in range(KD):
                            last = nc.tensor.matmul(pa[:, 2 * (c % 2) + n, :], wT[:, k, c * P:(c + 1) * P], yT[:, k, :], start=(k == 0), stop=(k == KD - 1))
                        last.then_inc(S[done], 1)
                pe.wait_ge(S["hidden"], b * NC + NC)
                pe.wait_ge(S["lg_copied"], b * 1 + 1)
                for tt in range(TT):
                    for c in range(NC):
                        last = nc.tensor.matmul(pb[:, tt, :], hT[:, c, tt * P:(tt + 1) * P], sdT[:, c, :], start=(c == 0), stop=(c == NC - 1))
                    last.then_inc(S["down_done"], 1)
                pe.wait_ge(S["mask_ready"], b * 1 + 1)
                for tt in range(TT):
                    acc = pa[:, 0, tt * E:(tt + 1) * E]
                    nc.tensor.matmul(acc, ones[:], carry[:], start=True, stop=False)
                    for u in range(tt):
                        nc.tensor.matmul(acc, ones[:], mask[:, u, :], start=False, stop=False)
                    last = nc.tensor.matmul(acc, before[:], mask[:, tt, :], start=False, stop=True)
                last.then_inc(S["placed"], 1)
                pe.wait_ge(S["added"], b * TT + TT)

            with pe.Fori(0, B // 2) as pair:
                for y in range(2):
                    batch(pair * 2 + y, y)

        @block.scalar
        def _(act):
            with act.Fori(0, B) as b:
                for k in (0, 2):
                    act.wait_ge(S["yT_psum"], b * KD + k + 1)
                    nc.scalar.activation(yT[:, k, :], pa[:, k, :], ACT.Copy).then_inc(S["yT_act"], 1)
                act.wait_ge(S["nv_done"], b * 1 + 1)
                for tt in range(TT):
                    nc.scalar.activation(ex[:, tt, :], lg[:, tt, :], ACT.Exp, bias=nv[:, tt:tt + 1], accum_out=se[:, tt:tt + 1])
                    last = nc.scalar.activation(ev[:, tt, :], v8[:, tt, :], ACT.Exp, bias=nv[:, tt:tt + 1])
                last.then_inc(S["exps"], 1)
                for c in range(NC):
                    act.wait_ge(S["gates"], b * NC + c + 1)
                    if c >= 2:
                        act.wait_ge(S["hidden"], b * NC + c - 1)
                    nc.scalar.activation(sil[:, c % 2, :], pa[:, 2 * (c % 2), :], ACT.Silu).then_inc(S["silued"], 1)

        @block.gpsimd
        def _(pool):
            pool.sem_inc(S["w_done"], 2)
            def batch(b, y):
                pool.wait_ge(S["slots_ready"], b * 1 + 1)
                pool.sem_inc(S["tick"], 1)
                for tt in range(TT):
                    for k in range(K):
                        nc.gpsimd.indirect_dma_start(
                            out=t.xg_dram, out_offset=bass.IndirectOffsetOnAxis(ap=slot[:, tt * K + k:tt * K + k + 1], axis=0),
                            in_=yb[:, y, tt, :], in_offset=None, bounds_check=SLOTS - 1, oob_is_err=False).then_inc(S["scattered"], 16)
                pool.wait_ge(S["scattered"], b * (TT * K * 16) + TT * K * 16)
                pool.sem_inc(S["w_done"], 1)

            with pool.Fori(0, B // 2) as pair:
                for y in range(2):
                    batch(pair * 2 + y, y)

        @block.vector
        def _(dve):
            dve.sem_inc(S["ld"], 1)
            dve.sem_inc(S["prod_done"], 1)
            dve.sem_inc(S["carried"], 1)
            nc.vector.memset(ones[:], 1.0).then_inc(S["ready"], 1)
            nc.vector.memset(carry[:], 0.0).then_inc(S["ready"], 1)
            n = 0

            def setup(dst, src, at):
                dve.wait_ge(S["setup_psum"], at)
                nc.vector.tensor_copy(dst, src).then_inc(S["setup_copied"], 1)

            for k in range(KD):
                setup(gwT[:, k, :], pa[:, k, 0:E], k + 1)
            for k in range(KD):
                setup(sgT[:, k, :], pb[:, k, 0:SI], KD + k + 1)
            for c in range(NC):
                setup(sdT[:, c, :], pa[:, c, :], 2 * KD + c + 1)
            for k in range(KD):
                setup(suT[:, k, :], pb[:, k, 0:SI], 2 * KD + NC + k + 1)
            dve.wait_ge(S["const_in"], N_C)
            nc.vector.tensor_copy(before[:], lf[:]).then_inc(S["ready"], 1)
            for k in range(KD):
                diag = wout[:, k, k * P:(k + 1) * P]
                nc.vector.tensor_tensor(diag, diag, t.ident[:], ALU.add).then_inc(S["ready"], 1)
            def batch(b, y):
                one = b * 1 + 1
                for tt in range(TT):
                    dve.wait_ge(S["y_psum"], b * TT + tt + 1)
                    if tt == 0:
                        dve.wait_ge(S["w_done"], one)
                    nc.vector.tensor_copy(yb[:, y, tt, :], pb[:, tt, :]).then_inc(S["y_ready"], 1)
                dve.wait_ge(S["y_ready"], b * TT + TT)
                dve.sem_inc(S["ld"], 1)
                for k in (1, 3):
                    dve.wait_ge(S["yT_psum"], b * KD + k + 1)
                    nc.vector.tensor_copy(yT[:, k, :], pa[:, k, :]).then_inc(S["yT_dve"], 1)
                dve.wait_ge(S["logits"], one)
                nc.vector.tensor_copy(lg[:].rearrange("p t e -> p (t e)"), pb[:, 0, 0:TT * E]).then_inc(S["lg_copied"], 1)
                dve.wait_ge(S["lg_copied"], one)
                dve.sem_inc(S["tick"], 1)
                for tt in range(TT):
                    nc.vector.max(v8[:, tt, :], lg[:, tt, :]).then_inc(S["top8"], 1)
                dve.wait_ge(S["top8"], b * TT + TT)
                nc.vector.tensor_scalar(nv[:], v8[:, :, 0], -1.0, None, ALU.mult).then_inc(S["nv_done"], 1)
                for tt in range(TT):
                    nc.vector.max_index(i8[:, tt, :], v8[:, tt, :], lg[:, tt, :]).then_inc(S["found"], 1)
                dve.wait_ge(S["found"], b * TT + TT)
                k24 = "p (t k) -> p t k"
                nc.vector.tensor_copy(ef[:].rearrange(k24, k=K), i8[:, :, 0:K]).then_inc(S["cast1"], 1)
                dve.wait_ge(S["cast1"], one)
                nc.vector.tensor_tensor(oh[:], iota[:].unsqueeze(1).broadcast_to([P, TT * K, E]),
                                        ef[:].unsqueeze(2).broadcast_to([P, TT * K, E]), ALU.is_equal).then_inc(S["onehot"], 1)
                dve.wait_ge(S["onehot"], one)
                with nc.allow_low_precision("a sum of at most one 1 is exact"):
                    for tt in range(TT):
                        nc.vector.tensor_reduce(mask[:, tt, :], oh[:, tt * K:(tt + 1) * K, :].rearrange("p k e -> p e k"), AX,
                                                ALU.add).then_inc(S["masked"], 1)
                dve.wait_ge(S["masked"], b * TT + TT)
                dve.wait_ge(S["carried"], b * TT + 1)
                dve.sem_inc(S["mask_ready"], 1)
                for c in range(NC):
                    dve.wait_ge(S["silued"], b * NC + c + 1)
                    dve.wait_ge(S["ups"], b * NC + c + 1)
                    nc.vector.tensor_tensor(hT[:, c, :], sil[:, c % 2, :], pa[:, 2 * (c % 2) + 1, :], ALU.mult).then_inc(S["hidden"], 1)
                dve.wait_ge(S["exps"], one)
                nc.vector.reciprocal(rs[:], se[:]).then_inc(S["rs_done"], 1)
                dve.wait_ge(S["rs_done"], one)
                wk = t.wk[:, bass.ds(b, 1), :].rearrange("p o k -> p (o k)")
                nc.vector.tensor_tensor(wk.rearrange(k24, k=K), ev[:, :, 0:K], rs[:].unsqueeze(2).broadcast_to([P, TT, K]),
                                        ALU.mult).then_inc(S["w1_done"], 1)
                for tt in range(TT):
                    dve.wait_ge(S["down_done"], b * TT + tt + 1)
                    x1 = t.x1[:, bass.ds(b * TT + tt, 1), :].rearrange("p o d -> p (o d)")
                    nc.vector.tensor_tensor(x1, x1, pb[:, tt, :], ALU.add).then_inc(S["added"], 1)
                dve.wait_ge(S["placed"], one)
                for tt in range(TT):
                    last = nc.vector.tensor_tensor(pr[:, tt * K:(tt + 1) * K, :], oh[:, tt * K:(tt + 1) * K, :],
                                                   pa[:, 0, tt * E:(tt + 1) * E].unsqueeze(1).broadcast_to([P, K, E]), ALU.mult)
                last.then_inc(S["prod_done"], 1)
                dve.wait_ge(S["prod_done"], b * 1 + 2)
                nc.vector.tensor_reduce(pk[:], pr[:], AX, ALU.add).then_inc(S["pk_done"], 1)
                dve.wait_ge(S["pk_done"], one)
                nc.vector.tensor_scalar(valid[:], pk[:], float(CAP), None, ALU.is_lt).then_inc(S["valid_done"], 1)
                nc.vector.scalar_tensor_tensor(sf[:], ef[:], float(CAP), pk[:], op0=ALU.mult, op1=ALU.add).then_inc(S["base_done"], 1)
                dve.wait_ge(S["valid_done"], one)
                dve.wait_ge(S["base_done"], one)
                nc.vector.scalar_tensor_tensor(sf[:], sf[:], -float(SLOTS), valid[:], op0=ALU.add, op1=ALU.mult).then_inc(S["base2_done"], 1)
                dve.wait_ge(S["base2_done"], one)
                nc.vector.tensor_scalar(sf[:], sf[:], float(SLOTS), None, ALU.add).then_inc(S["sf_done"], 1)
                dve.wait_ge(S["sf_done"], one)
                dve.wait_ge(S["w_done"], b * 1 + 2)
                nc.vector.tensor_copy(slot[:], sf[:]).then_inc(S["slots_ready"], 1)
                nc.vector.tensor_copy(t.slot[:, bass.ds(b, 1), :].rearrange("p o k -> p (o k)"), sf[:])
                dve.wait_ge(S["w1_done"], one)
                nc.vector.tensor_tensor(wk, wk, valid[:], ALU.mult)
                for tt in range(TT):
                    dve.wait_ge(S["carried"], b * TT + tt + 1)
                    nc.vector.tensor_tensor(carry[:], carry[:], mask[:, tt, :], ALU.add).then_inc(S["carried"], 1)

            with dve.Fori(0, B // 2) as pair:
                for y in range(2):
                    batch(pair * 2 + y, y)

def expert_stage(nc, t, gate_up, down):
    with ExitStack() as ctx:
        sem = ctx.enter_context(Sems(nc, "ex_"))
        U = 4

        def sb(name, shape, dt=F32):
            return ctx.enter_context(nc.sbuf_tensor("ex_" + name, shape, dt))

        HC = I // 2
        wg, wd, xg = sb("wg", [P, U, KD, 2 * I]), sb("wd", [HC, U, 2, D]), sb("xg", [P, U, D])
        xT, sil, hid, hT, eo = sb("xT", [P, 2, KD, P]), sb("sil", [P, 2, I]), sb("hid", [P, 2, I]), sb("hT", [HC, 2, 2, P]), sb("eo", [P, 2, D])
        px = ctx.enter_context(nc.psum_tensor("ex_px", [P, 2, 512], F32))
        pg = ctx.enter_context(nc.psum_tensor("ex_pg", [P, 2, 512], F32))
        ph = ctx.enter_context(nc.psum_tensor("ex_ph", [P, 2, 512], F32))
        pd = ctx.enter_context(nc.psum_tensor("ex_pd", [P, 2, 512], F32))
        w_in = [sem(f"w_in{u}") for u in range(U)]
        xT_psum, xT_ready, gu_done, silued, hid_ready, hT_psum, hT_ready, down_done, eo_ready = (sem(n) for n in (
            "xT_psum", "xT_ready", "gu_done", "silued", "hid_ready", "hT_psum", "hT_ready", "down_done", "eo_ready"))
        stored = [sem("stored0"), sem("stored1")]
        block = ctx.enter_context(nc.Block())
        NL = E // U

        def load(sp, e, u):
            sp.dma_start(xg[:, u, :], t.xg_dram[bass.ds(e * CAP, CAP), :]).then_inc(w_in[u], 16)
            sp.dma_start(wg[:, u, :, :], gate_up[bass.ds(e, 1), :, :].rearrange("o (k p) i -> p (o k) i", p=P)).then_inc(w_in[u], 16)
            sp.dma_start(wd[:, u, :, :], down[bass.ds(e, 1), :, :].rearrange("o (c q) h -> q (o c) h", q=HC)).then_inc(w_in[u], 16)

        def wait(eng, s, q, n):
            eng.wait_ge(s, q * U + n)

        @block.sync
        def _(sp):
            for u in range(U):
                load(sp, u, u)
            with sp.Fori(0, NL - 1) as q:
                for u in range(U):
                    wait(sp, down_done, q, u + 1)
                    load(sp, q * U + (U + u), u)

        @block.tensor
        def _(pe):
            def transpose_x(q, u, first):
                v = u % U
                pe.wait_ge(w_in[v], q * 48 + 48 * (u // U + 1))
                if not first or u >= 2:
                    wait(pe, xT_ready, q, u - 1)
                for k in range(KD):
                    last = nc.tensor.transpose(px[:, u % 2, k * P:(k + 1) * P], xg[:, v, k * P:(k + 1) * P], t.ident[:])
                last.then_inc(xT_psum, 1)

            def hidden(q, u, first):
                wait(pe, xT_ready, q, u + 1)
                if not first or u >= 2:
                    wait(pe, hid_ready, q, u - 1)
                for k in range(KD):
                    last = nc.tensor.matmul(pg[:, u % 2, 0:2 * I], xT[:, u % 2, k, :], wg[:, u, k, :], start=(k == 0), stop=(k == KD - 1))
                last.then_inc(gu_done, 1)

            def transpose_hidden(q, u, first):
                s = u % U
                wait(pe, hid_ready, q, u + 1)
                if not first or u >= 2:
                    wait(pe, hT_ready, q, u - 1)
                for c in range(2):
                    last = nc.tensor.transpose(ph[0:HC, s % 2, c * P:(c + 1) * P], hid[:, s % 2, c * HC:(c + 1) * HC], t.ident[:])
                last.then_inc(hT_psum, 1)

            def output(q, u, first):
                s = u % U
                wait(pe, hT_ready, q, u + 1)
                if not first or u >= 2:
                    wait(pe, eo_ready, q, u - 1)
                for c in range(2):
                    last = nc.tensor.matmul(pd[:, s % 2, :], hT[:, s % 2, c, :], wd[:, s, c, :], start=(c == 0), stop=(c == 1))
                last.then_inc(down_done, 1)

            def round_of(q, first=False, final=False):
                for u in range(U):
                    if not (final and u == U - 1):
                        transpose_x(q, u + 1, first)
                    if not first or u:
                        transpose_hidden(q, u - 1, first)
                    hidden(q, u, first)
                    if not first or u:
                        output(q, u - 1, first)

            transpose_x(0, 0, True)
            round_of(0, first=True)
            with pe.Fori(1, NL - 1) as q:
                round_of(q)
            round_of(NL - 1, final=True)
            transpose_hidden(NL - 1, U - 1, False)
            output(NL - 1, U - 1, False)

        @block.scalar
        def _(act):
            nc.scalar.preload_act_table_set("silu_and_others")

            def step(q, u, first, body=True):
                if body:
                    wait(act, gu_done, q, u + 1)
                    if not first or u >= 2:
                        wait(act, hid_ready, q, u - 1)
                    nc.scalar.activation(sil[:, u % 2, :], pg[:, u % 2, 0:I], ACT.Silu).then_inc(silued, 1)
                if not first or u >= 1:
                    v = u - 1
                    s = v % 2
                    wait(act, down_done, q, v + 1)
                    if not first or v >= 2:
                        act.wait_ge(stored[s], q * (16 * U // 2) + 16 * (v // 2))
                    nc.scalar.activation(eo[:, s, :], pd[:, s, :], ACT.Copy).then_inc(eo_ready, 1)

            for u in range(U):
                step(0, u, True)
            with act.Fori(1, NL) as q:
                for u in range(U):
                    step(q, u, False)
            step(NL, 0, False, body=False)

        @block.gpsimd
        def _(pool):
            with pool.Fori(0, NL) as q:
                for u in range(U):
                    wait(pool, eo_ready, q, u + 1)
                    nc.gpsimd.dma_start(t.eo_dram[bass.ds((q * U + u) * CAP, CAP), :], eo[:, u % 2, :]).then_inc(stored[u % 2], 16)
            for s in range(2):
                pool.wait_ge(stored[s], 16 * E // 2)

        @block.vector
        def _(dve):
            def copy_x(q, u, first):
                wait(dve, xT_psum, q, u + 1)
                if not first or u >= 2:
                    wait(dve, gu_done, q, u - 1)
                nc.vector.tensor_copy(xT[:, u % 2, :, :].rearrange("p k t -> p (k t)"), px[:, u % 2, :]).then_inc(xT_ready, 1)

            def copy_hidden(q, v, first):
                wait(dve, hT_psum, q, v + 1)
                if not first or v >= 2:
                    wait(dve, down_done, q, v - 1)
                nc.vector.tensor_copy(hT[:, v % 2, :, :].rearrange("p c t -> p (c t)"), ph[0:HC, v % 2, 0:2 * P]).then_inc(hT_ready, 1)

            def gate_up_product(q, u, first):
                wait(dve, silued, q, u + 1)
                if not first or u >= 2:
                    wait(dve, hT_psum, q, u - 1)
                nc.vector.tensor_tensor(hid[:, u % 2, :], sil[:, u % 2, :], pg[:, u % 2, I:2 * I], ALU.mult).then_inc(hid_ready, 1)

            def round_of(q, first=False, final=False):
                for u in range(U):
                    if not (final and u == U - 1):
                        copy_x(q, u + 1, first)
                    if not first or u:
                        copy_hidden(q, u - 1, first)
                    gate_up_product(q, u, first)

            copy_x(0, 0, True)
            round_of(0, first=True)
            with dve.Fori(1, NL - 1) as q:
                round_of(q)
            round_of(NL - 1, final=True)
            copy_hidden(NL - 1, U - 1, False)


def combine_stage(nc, t, out):
    with ExitStack() as ctx:
        sem = ctx.enter_context(Sems(nc, "co_"))
        got = ctx.enter_context(nc.sbuf_tensor("co_got", [P, 4, K, D], F32))
        idx = ctx.enter_context(nc.sbuf_tensor("co_idx", [P, B * TT * K], U32))
        acc = ctx.enter_context(nc.sbuf_tensor("co_acc", [P, 4, D], F32))
        gathered = [sem(f"gathered{i}") for i in range(4)]
        tick, idx_ready, summed, chain = sem("tick"), sem("idx_ready"), sem("summed"), sem("chain")
        stored = [sem(f"stored{i}") for i in range(4)]
        block = ctx.enter_context(nc.Block())
        out_t = out.rearrange("b t d -> (b t) d")

        @block.gpsimd
        def _(pool):
            with pool.Fori(0, B) as b:
                pool.wait_ge(idx_ready, b * 1 + 1)
                pool.sem_inc(tick, 1)
                for tt in range(TT):
                    pool.wait_ge(summed, b * TT + tt + 1)
                    pool.sem_inc(tick, 1)
                    for k in range(K):
                        nc.gpsimd.indirect_dma_start(
                            out=got[:, tt, k, :], out_offset=None, in_=t.eo_dram,
                            in_offset=bass.IndirectOffsetOnAxis(ap=idx[:, tt * K + k:tt * K + k + 1], axis=0)).then_inc(gathered[tt], 16)

        @block.sync
        def _(sp):
            with sp.Fori(0, B) as b:
                for tt in range(TT):
                    sp.wait_ge(summed, b * TT + tt + TT + 1)
                    sp.dma_start(out_t[bass.ds((b * TT + tt) * P, P), :], acc[:, tt, :]).then_inc(stored[tt], 16)
            for tt in range(TT):
                sp.wait_ge(stored[tt], 16 * B)

        @block.vector
        def _(dve):
            dve.sem_inc(summed, TT)
            nc.vector.tensor_copy(idx[:, 0:TT * K], t.slot[:, 0, :]).then_inc(idx_ready, 1)

            def tile(b, tt, first):
                dve.wait_ge(gathered[tt], b * (16 * K) + 16 * K)
                if not first:
                    dve.wait_ge(stored[tt], b * 16)
                src = t.x1[:, bass.ds(b * TT + tt, 1), :].rearrange("p o d -> p (o d)")
                wk = t.wk[:, bass.ds(b, 1), :].rearrange("p o k -> p (o k)")
                for k in range(K):
                    last = nc.vector.scalar_tensor_tensor(acc[:, tt, :], got[:, tt, k, :], wk[:, tt * K + k:tt * K + k + 1], src,
                                                          op0=ALU.mult, op1=ALU.add)
                    src = acc[:, tt, :]
                    if k < K - 1:
                        last.then_inc(chain, 1)
                        dve.wait_ge(chain, (b * TT + tt) * (K - 1) + k + 1)
                last.then_inc(summed, 1)

            for tt in range(TT):
                tile(0, tt, True)
            with dve.Fori(1, B) as b:
                nc.vector.tensor_copy(idx[:, 0:TT * K], t.slot[:, bass.ds(b, 1), :].rearrange("p o k -> p (o k)")).then_inc(idx_ready, 1)
                for tt in range(TT):
                    tile(b, tt, False)


def constants():
    f = np.float32
    p = np.arange(P)
    freq = 1.0 / 10000.0 ** (np.arange(0, DQ, 2, dtype=f) / f(DQ))
    angle = np.outer(np.arange(T, dtype=f), freq).astype(f)
    of = (p % DQ) // 2
    swap = np.zeros((P, P), f)
    swap[p[1::2], p[0::2]] = -1.0
    swap[p[0::2], p[1::2]] = 1.0
    nf = T // 2 + 1
    filt = np.exp(-0.5 * (np.linspace(0.0, 1.0, nf) / 0.15) ** 2)
    weight = np.full(nf, 2.0)
    weight[0] = weight[-1] = 1.0
    col = (weight * filt) @ np.cos(2 * np.pi * np.arange(nf)[:, None] * np.arange(T) / T) / T
    return {
        "ident": np.eye(P, dtype=f),
        "cs": np.stack([np.cos(angle)[:, of].T, np.sin(angle)[:, of].T]).astype(f),
        "swap": swap,
        "half": np.stack([p % DH < DQ, p % DH >= DQ], 1).astype(f),
        "mask": np.stack([np.where(p[None, :] > p[:, None], -1e30, 0.0), np.where(p[None, :] < p[:, None], -1e30, 0.0)]).astype(f),
        "filt": col[(np.arange(T)[:, None] - np.arange(T)) % T].astype(f),
        "headones": (p[:, None] // DH == p // DH).astype(f),
        "before": (p[:, None] < p).astype(f),
        "iota": np.arange(E, dtype=f),
    }


class Held:
    pass


def program(nc, a, out):
    t = Held()
    with ExitStack() as ctx:
        def sb(stack, name, shape, dt=F32):
            return stack.enter_context(nc.sbuf_tensor(name, shape, dt))

        t.xg_dram = nc.dram_tensor("xg", (SLOTS, D), F32, kind="Internal").ap()
        t.eo_dram = nc.dram_tensor("eo", (SLOTS + 1, D), F32, kind="Internal").ap()
        t.const = a
        t.ident = sb(ctx, "ident", [P, P])
        wide = sb(ctx, "wide", [P, KD * B * T])
        t.ahead = sb(ctx, "ahead", [P, 3 * KD * D])
        t.hsT = wide[:, :].rearrange("p (k b t) -> p k b t", k=KD, b=B)
        t.x1 = wide[:, :].rearrange("p (n d) -> p n d", d=D)
        with ExitStack() as gru:
            t.h, t.giT = sb(gru, "h", [P, ST, 4]), sb(gru, "giT", [P, T, 3 * ST])
            gate_inputs_stage(nc, t, a["x"], a["L0_cond_W_ih"], a["L0_cond_b_ih"], a["L0_cond_b_hh"])
            gru_stage(nc, t, a["cond_2048"], a["L0_cond_W_hh"], a["L0_cond_b_hh"],
                      [a["L0_attn_W" + n] for n in "qkv"])
        t.A = sb(ctx, "A", [P, TT, B, D])
        t.slot, t.wk = sb(ctx, "slot", [P, B, TT * K], U32), sb(ctx, "wk", [P, B, TT * K])
        diff_attention_stage(nc, t, [a["L0_attn_lambda_" + n] for n in ("q1", "k1", "q2", "k2")])
        t.oT = t.A[:].rearrange("p i b f -> p (i b f)").rearrange("p (k b t) -> p k b t", k=KD, b=B)
        with ExitStack() as mid:
            t.xnT = sb(mid, "xnT", [P, B, KD, T])
            filter_stage(nc, t, a["x"], a["L0_attn_Wout"], a["L0_attn_rms_weight"], a["cond_2048"],
                         a["L0_cond2_W_emb"], a["L0_cond2_b_emb"], a["L0_cond2_g_norm"], a["L0_cond2_W_qkv"])
            full_attention_stage(nc, t, a["L0_cond2_g_q"], a["L0_cond2_g_k"])
        route_stage(nc, t, a["L0_cond2_W_out"], a["L0_ffn_gate_w"], a["L0_ffn_shared_gate_w"], a["L0_ffn_shared_up_w"],
                    a["L0_ffn_shared_down_w"])
        expert_stage(nc, t, a["L0_ffn_gate_up_proj"], a["L0_ffn_down_proj"])
        combine_stage(nc, t, out)


INPUTS = ["x", "cond_2048", "L0_cond_W_ih", "L0_cond_W_hh", "L0_cond_b_ih", "L0_cond_b_hh", "L0_attn_Wq", "L0_attn_Wk",
          "L0_attn_Wv", "L0_attn_Wout", "L0_attn_lambda_q1", "L0_attn_lambda_k1", "L0_attn_lambda_q2",
          "L0_attn_lambda_k2", "L0_attn_rms_weight", "L0_cond2_W_emb", "L0_cond2_b_emb", "L0_cond2_g_norm",
          "L0_cond2_W_qkv", "L0_cond2_g_q", "L0_cond2_g_k", "L0_cond2_W_out", "L0_ffn_gate_w", "L0_ffn_gate_up_proj",
          "L0_ffn_down_proj", "L0_ffn_shared_gate_w", "L0_ffn_shared_up_w", "L0_ffn_shared_down_w"]
CONSTANTS = ["ident", "cs", "swap", "half", "mask", "filt", "headones", "before", "iota"]


def kernel(**inputs):
    import concourse.bacc as bacc
    from concourse.bass_utils import run_bass_kernel_spmd

    nc = bacc.Bacc("TRN2", target_bir_lowering=False, num_devices=1)
    arrays, aps = {}, {}
    consts = constants()
    for name in INPUTS + CONSTANTS:
        a = np.ascontiguousarray(inputs[name] if name in inputs else consts[name])
        arrays["in_" + name] = a
        aps[name] = nc.dram_tensor("in_" + name, a.shape, mybir.dt.from_np(a.dtype), kind="ExternalInput").ap()
    out = nc.dram_tensor("out_0", (B, T, D), F32, kind="ExternalOutput").ap()
    program(nc, aps, out)
    r = run_bass_kernel_spmd(nc, [arrays], core_ids=[0])
    return r.results[0]["out_0"]
```
